# Optimizing a Trainium2 kernel written in Bass

```python
import numpy as np
import jax
import jax.numpy as jnp

def _softmax(x, axis=-1):
    return jax.nn.softmax(x, axis=axis)

def _gelu(x):
    return jax.nn.gelu(x, approximate=True)

def _silu(x):
    return jax.nn.silu(x)

def _sigmoid(x):
    return jax.nn.sigmoid(x)

def _layernorm(x, axis=-1, eps=1e-05):
    m = jnp.mean(x, axis=axis, keepdims=True)
    v = jnp.var(x, axis=axis, keepdims=True)
    return (x - m) / jnp.sqrt(v + eps)

def _scatter_add(tgt, idx, src, axis=0):
    return tgt.at[idx].add(src)

def _segment_sum(src, seg, n):
    return jax.ops.segment_sum(src, seg, n)
kernel_name = 'mk_gnn_ffn_d4_gnn_r64_6d9267'

def setup_inputs(seed: int=0):
    np.random.seed(seed)
    _w = jnp.asarray

    def _rec_inputs():
        import jax
        import jax.numpy as jnp
        _gk = jax.random.key(seed)
        x = -0.0001538 + 1 * jax.random.normal(jax.random.fold_in(_gk, 1), (128, 768), jnp.float32)
        src = jax.random.randint(jax.random.fold_in(_gk, 2), (2048,), 0, 128, jnp.int32)
        dst = jax.random.randint(jax.random.fold_in(_gk, 3), (2048,), 0, 128, jnp.int32)
        _o = jnp.argsort(dst, stable=True)
        src = src[_o]
        dst = dst[_o]
        return (x, src, dst)
    x, src, dst = _rec_inputs()

    def _L0_gnn_setup():
        import jax, jax.numpy as jnp
        import numpy as np
        NEG_SLOPE = 0.2
        EPS = 1e-16
        N_NODES = 128
        N_EDGES = 1024
        D_IN = 768
        D_HID = 768
        H1 = 8
        H2 = 1

        def gat_layer(x, W, a_s, a_d, b, edge_index, concat):
            n = x.shape[0]
            H, C = a_s.shape
            h = (x @ W).reshape(n, H, C)
            src, dst = (edge_index[0], edge_index[1])
            alpha_s = jnp.einsum('nhc,hc->nh', h, a_s)
            alpha_d = jnp.einsum('nhc,hc->nh', h, a_d)
            e = jax.nn.leaky_relu(alpha_s[src] + alpha_d[dst], NEG_SLOPE)
            m = jax.ops.segment_max(e, dst, num_segments=n)
            e = jnp.exp(e - m[dst])
            denom = jax.ops.segment_sum(e, dst, num_segments=n)
            alpha = e / (denom[dst] + EPS)
            msg = h[src] * alpha[:, :, None]
            out = jax.ops.segment_sum(msg, dst, num_segments=n)
            out = out.reshape(n, H * C) if concat else out.mean(axis=1)
            return out + b
        key = jax.random.key(seed)
        ks = jax.random.split(key, 10)
        x = jax.random.normal(ks[0], (N_NODES, D_IN), dtype=jnp.float32)
        edge_list = jax.random.randint(ks[1], (2, N_EDGES), 0, N_NODES, dtype=jnp.int32)
        s = 0.05
        W1 = jax.random.normal(ks[2], (D_IN, H1 * D_HID), dtype=jnp.float32) * s
        a_src1 = jax.random.normal(ks[3], (H1, D_HID), dtype=jnp.float32) * s
        a_dst1 = jax.random.normal(ks[4], (H1, D_HID), dtype=jnp.float32) * s
        b1 = jnp.zeros((H1 * D_HID,), dtype=jnp.float32)
        W2 = jax.random.normal(ks[5], (H1 * D_HID, H2 * D_HID), dtype=jnp.float32) * s
        a_src2 = jax.random.normal(ks[6], (H2, D_HID), dtype=jnp.float32) * s
        a_dst2 = jax.random.normal(ks[7], (H2, D_HID), dtype=jnp.float32) * s
        b2 = jnp.zeros((H2 * D_HID,), dtype=jnp.float32)
        return {'x': x, 'W1': W1, 'a_src1': a_src1, 'a_dst1': a_dst1, 'b1': b1, 'W2': W2, 'a_src2': a_src2, 'a_dst2': a_dst2, 'b2': b2, 'edge_list': edge_list}
    _L0_gnn_all = _L0_gnn_setup()
    _L0_gnn_in = {k: v for k, v in _L0_gnn_all.items() if k in ('W1', 'a_src1', 'a_dst1', 'b1', 'W2', 'a_src2', 'a_dst2', 'b2')}
    del _L0_gnn_all

    def _L0_ffn_setup():
        import jax, jax.numpy as jnp
        import numpy as np
        B, L, D, H, F = (4, 32, 768, 12, 48)
        ROUTE_FRAC = 0.15
        LN_EPS = 1e-05

        def _ln(x, g, b):
            m = jnp.mean(x, axis=-1, keepdims=True)
            v = jnp.mean((x - m) ** 2, axis=-1, keepdims=True)
            return (x - m) * jax.lax.rsqrt(v + LN_EPS) * g + b
        key = jax.random.key(seed)
        ks = jax.random.split(key, 20)
        s = 0.02
        return {'hidden_states': jax.random.normal(ks[0], (B, L, D), dtype=jnp.float32), 'g1': jnp.ones((D,), jnp.float32), 'b1': jnp.zeros((D,), jnp.float32), 'g2': jnp.ones((D,), jnp.float32), 'b2': jnp.zeros((D,), jnp.float32), 'Wr': jax.random.normal(ks[1], (D,), jnp.float32) * s, 'br': jnp.zeros((), jnp.float32), 'Wq': jax.random.normal(ks[2], (D, D), jnp.float32) * s, 'bq': jnp.zeros((D,), jnp.float32), 'Wk': jax.random.normal(ks[3], (D, D), jnp.float32) * s, 'bk': jnp.zeros((D,), jnp.float32), 'Wv': jax.random.normal(ks[4], (D, D), jnp.float32) * s, 'bv': jnp.zeros((D,), jnp.float32), 'Wo': jax.random.normal(ks[5], (D, D), jnp.float32) * s, 'bo': jnp.zeros((D,), jnp.float32), 'Wm': jax.random.normal(ks[6], (D, D), jnp.float32) * s, 'bm': jnp.zeros((D,), jnp.float32), 'W1': jax.random.normal(ks[7], (D, F), jnp.float32) * s, 'bf1': jnp.zeros((F,), jnp.float32), 'W2': jax.random.normal(ks[8], (F, D), jnp.float32) * s, 'bf2': jnp.zeros((D,), jnp.float32)}
    _L0_ffn_all = _L0_ffn_setup()
    _L0_ffn_in = {k: v for k, v in _L0_ffn_all.items() if k in ('g1', 'b1', 'g2', 'b2', 'Wr', 'br', 'Wq', 'bq', 'Wk', 'bk', 'Wv', 'bv', 'Wo', 'bo', 'Wm', 'bm', 'W1', 'bf1', 'W2', 'bf2')}
    del _L0_ffn_all

    def _L1_gnn_setup():
        import jax, jax.numpy as jnp
        import numpy as np
        N_NODES = 10000
        NEG_SLOPE = 0.2
        EPS = 1e-16

        def gat_layer(x, W, att_src, att_dst, bias, src, dst, heads, out_ch, concat):
            n = x.shape[0]
            h = (x @ W.T).reshape(n, heads, out_ch)
            a_src = jnp.einsum('nhc,hc->nh', h, att_src)
            a_dst = jnp.einsum('nhc,hc->nh', h, att_dst)
            e = a_src[src] + a_dst[dst]
            e = jax.nn.leaky_relu(e, NEG_SLOPE)
            m = jax.ops.segment_max(e, dst, num_segments=n)
            ex = jnp.exp(e - m[dst])
            denom = jax.ops.segment_sum(ex, dst, num_segments=n)
            alpha = ex / (denom[dst] + EPS)
            msg = alpha[:, :, None] * h[src]
            out = jax.ops.segment_sum(msg, dst, num_segments=n)
            if concat:
                out = out.reshape(n, heads * out_ch)
            else:
                out = out.mean(axis=1)
            return out + bias
        key = jax.random.key(seed)
        ks = jax.random.split(key, 12)
        x = jax.random.normal(ks[0], (N_NODES, 768), dtype=jnp.float32)
        edge_index = jax.random.randint(ks[1], (2, 2500), 0, N_NODES, dtype=jnp.int64)
        s1 = 1.0 / np.sqrt(768.0)
        W1 = jax.random.normal(ks[2], (8 * 128, 768), dtype=jnp.float32) * s1
        att_src1 = jax.random.normal(ks[3], (8, 128), dtype=jnp.float32) * (1.0 / np.sqrt(128.0))
        att_dst1 = jax.random.normal(ks[4], (8, 128), dtype=jnp.float32) * (1.0 / np.sqrt(128.0))
        b1 = jnp.zeros((8 * 128,), dtype=jnp.float32)
        s2 = 1.0 / np.sqrt(1024.0)
        W2 = jax.random.normal(ks[5], (1 * 768, 1024), dtype=jnp.float32) * s2
        att_src2 = jax.random.normal(ks[6], (1, 768), dtype=jnp.float32) * (1.0 / np.sqrt(768.0))
        att_dst2 = jax.random.normal(ks[7], (1, 768), dtype=jnp.float32) * (1.0 / np.sqrt(768.0))
        b2 = jnp.zeros((768,), dtype=jnp.float32)
        return {'x': x, 'edge_index': edge_index, 'W1': W1, 'att_src1': att_src1, 'att_dst1': att_dst1, 'b1': b1, 'W2': W2, 'att_src2': att_src2, 'att_dst2': att_dst2, 'b2': b2}
    _L1_gnn_all = _L1_gnn_setup()
    _L1_gnn_in = {k: v for k, v in _L1_gnn_all.items() if k in ('W1', 'att_src1', 'att_dst1', 'b1', 'W2', 'att_src2', 'att_dst2', 'b2')}
    del _L1_gnn_all

    def _L1_ffn_setup():
        import jax, jax.numpy as jnp
        import numpy as np
        B, S, D = (2, 32, 768)
        E, K, F = (8, 2, 1536)

        def _swiglu(xf, wg, wu, wd):
            return jax.nn.silu(xf @ wg.T) * (xf @ wu.T) @ wd.T
        key = jax.random.key(seed)
        ks = jax.random.split(key, 9)
        scale = 0.02
        x = jax.random.normal(ks[0], (B, S, D), dtype=jnp.float32)
        w_router = jax.random.normal(ks[1], (E, D), dtype=jnp.float32) * scale
        expert_bias = jnp.zeros((E,), dtype=jnp.float32)
        Wg = jax.random.normal(ks[2], (E, F, D), dtype=jnp.float32) * scale
        Wu = jax.random.normal(ks[3], (E, F, D), dtype=jnp.float32) * scale
        Wd = jax.random.normal(ks[4], (E, D, F), dtype=jnp.float32) * scale
        sg = jax.random.normal(ks[5], (F, D), dtype=jnp.float32) * scale
        su = jax.random.normal(ks[6], (F, D), dtype=jnp.float32) * scale
        sd = jax.random.normal(ks[7], (D, F), dtype=jnp.float32) * scale
        return {'x': x, 'w_router': w_router, 'expert_bias': expert_bias, 'Wg': Wg, 'Wu': Wu, 'Wd': Wd, 'sg': sg, 'su': su, 'sd': sd}
    _L1_ffn_all = _L1_ffn_setup()
    _L1_ffn_in = {k: v for k, v in _L1_ffn_all.items() if k in ('w_router', 'expert_bias', 'Wg', 'Wu', 'Wd', 'sg', 'su', 'sd')}
    del _L1_ffn_all

    def _L2_gnn_setup():
        import jax, jax.numpy as jnp
        import numpy as np
        N = 20000
        DEG = 16
        E = N * DEG
        H = 12
        DIN = 64
        DOUT = 64
        NEG_SLOPE = 0.2
        key = jax.random.key(seed)
        k_h, k_src, k_w, k_al, k_ar, k_wr = jax.random.split(key, 6)
        std = 1.414 * np.sqrt(2.0 / (DIN + DOUT))
        h = jax.random.normal(k_h, (N, H * DIN), dtype=jnp.float32)
        src = jax.random.randint(k_src, (E,), 0, N, dtype=jnp.int64)
        dst = jnp.repeat(jnp.arange(N, dtype=jnp.int64), DEG)
        W = jax.random.normal(k_w, (DOUT, DIN), dtype=jnp.float32) * std
        attn_l = jax.random.normal(k_al, (1, H, DOUT), dtype=jnp.float32) * std
        attn_r = jax.random.normal(k_ar, (1, H, DOUT), dtype=jnp.float32) * std
        W_res = jax.random.normal(k_wr, (DOUT, DIN), dtype=jnp.float32) * std
        return {'h': h, 'src': src, 'dst': dst, 'W': W, 'attn_l': attn_l, 'attn_r': attn_r, 'W_res': W_res}
    _L2_gnn_all = _L2_gnn_setup()
    _L2_gnn_in = {k: v for k, v in _L2_gnn_all.items() if k in ('W', 'attn_l', 'attn_r', 'W_res')}
    del _L2_gnn_all

    def _L2_ffn_setup():
        import jax, jax.numpy as jnp
        import numpy as np
        DIM = 768
        NUM_EXPERTS = 8
        HIDDEN = 48
        TOP_K = 2
        B, N = (1, 1024)
        key = jax.random.key(seed)
        ks = jax.random.split(key, 8)
        s_in = 1.0 / np.sqrt(DIM)
        s_hid = 1.0 / np.sqrt(HIDDEN)
        return {'x': jax.random.normal(ks[0], (B, N, DIM), dtype=jnp.float32), 'Wg': jax.random.uniform(ks[1], (DIM, NUM_EXPERTS), jnp.float32, -s_in, s_in), 'bg': jax.random.uniform(ks[2], (NUM_EXPERTS,), jnp.float32, -s_in, s_in), 'W1': jax.random.uniform(ks[3], (NUM_EXPERTS, DIM, HIDDEN), jnp.float32, -s_in, s_in), 'b1': jax.random.uniform(ks[4], (NUM_EXPERTS, HIDDEN), jnp.float32, -s_in, s_in), 'W2': jax.random.uniform(ks[5], (NUM_EXPERTS, HIDDEN, DIM), jnp.float32, -s_hid, s_hid), 'b2': jax.random.uniform(ks[6], (NUM_EXPERTS, DIM), jnp.float32, -s_hid, s_hid)}
    _L2_ffn_all = _L2_ffn_setup()
    _L2_ffn_in = {k: v for k, v in _L2_ffn_all.items() if k in ('Wg', 'bg', 'W1', 'b1', 'W2', 'b2')}
    del _L2_ffn_all

    def _L3_gnn_setup():
        import jax, jax.numpy as jnp
        import numpy as np
        N_NODES = 10000
        N_EDGES = 2500
        NEG_SLOPE = 0.2

        def _gat_layer(x, src, dst, W, a_src, a_dst, bias, concat):
            N = x.shape[0]
            H, C = a_src.shape
            h = (x @ W).reshape(N, H, C)
            al_s = jnp.einsum('nhc,hc->nh', h, a_src)
            al_d = jnp.einsum('nhc,hc->nh', h, a_dst)
            e = jax.nn.leaky_relu(al_s[src] + al_d[dst], NEG_SLOPE)
            m = jax.ops.segment_max(e, dst, num_segments=N)
            ex = jnp.exp(e - m[dst])
            denom = jax.ops.segment_sum(ex, dst, num_segments=N)
            alpha = ex / (denom[dst] + 1e-16)
            msg = h[src] * alpha[:, :, None]
            out = jax.ops.segment_sum(msg, dst, num_segments=N)
            out = out.reshape(N, H * C) if concat else out.mean(axis=1)
            return out + bias
        key = jax.random.key(seed)
        ks = jax.random.split(key, 10)
        in_dim, hid, out_dim, heads = (768, 512, 768, 4)
        x = jax.random.normal(ks[0], (N_NODES, in_dim), dtype=jnp.float32)
        edge_index = jax.random.randint(ks[1], (2, N_EDGES), 0, N_NODES, dtype=jnp.int64)
        g = lambda k, shape, fan: jax.random.normal(k, shape, jnp.float32) / np.sqrt(fan)
        return {'x': x, 'edge_index': edge_index, 'W1': g(ks[2], (in_dim, heads * hid), in_dim), 'att_src1': g(ks[3], (heads, hid), hid), 'att_dst1': g(ks[4], (heads, hid), hid), 'b1': jnp.zeros((heads * hid,), jnp.float32), 'W2': g(ks[5], (heads * hid, out_dim), heads * hid), 'att_src2': g(ks[6], (1, out_dim), out_dim), 'att_dst2': g(ks[7], (1, out_dim), out_dim), 'b2': jnp.zeros((out_dim,), jnp.float32)}
    _L3_gnn_all = _L3_gnn_setup()
    _L3_gnn_in = {k: v for k, v in _L3_gnn_all.items() if k in ('W1', 'att_src1', 'att_dst1', 'b1', 'W2', 'att_src2', 'att_dst2', 'b2')}
    del _L3_gnn_all

    def _L3_ffn_setup():
        import jax, jax.numpy as jnp
        import numpy as np
        B, T, D, E, K = (4, 32, 768, 8, 2)
        H = 4 * D
        key = jax.random.key(seed)
        k0, k1, k2, k3, k4 = jax.random.split(key, 5)
        s = 0.02
        return {'x': jax.random.normal(k0, (B, T, D), jnp.float32), 'router_w': jax.random.uniform(k1, (E, D), jnp.float32, -s * 0.1, s * 0.1), 'Wg': jax.random.uniform(k2, (E, H, D), jnp.float32, -s * 0.4, s * 0.4), 'Wu': jax.random.uniform(k3, (E, H, D), jnp.float32, -s * 0.4, s * 0.4), 'Wd': jax.random.normal(k4, (E, D, H), jnp.float32) * 0.01}
    _L3_ffn_all = _L3_ffn_setup()
    _L3_ffn_in = {k: v for k, v in _L3_ffn_all.items() if k in ('router_w', 'Wg', 'Wu', 'Wd')}
    del _L3_ffn_all
    return {'x': x, 'src': src, 'dst': dst, 'L0_gnn_W1': _L0_gnn_in['W1'], 'L0_gnn_a_src1': _L0_gnn_in['a_src1'], 'L0_gnn_a_dst1': _L0_gnn_in['a_dst1'], 'L0_gnn_b1': _L0_gnn_in['b1'], 'L0_gnn_W2': _L0_gnn_in['W2'], 'L0_gnn_a_src2': _L0_gnn_in['a_src2'], 'L0_gnn_a_dst2': _L0_gnn_in['a_dst2'], 'L0_gnn_b2': _L0_gnn_in['b2'], 'L0_ffn_g1': _L0_ffn_in['g1'], 'L0_ffn_b1': _L0_ffn_in['b1'], 'L0_ffn_g2': _L0_ffn_in['g2'], 'L0_ffn_b2': _L0_ffn_in['b2'], 'L0_ffn_Wr': _L0_ffn_in['Wr'], 'L0_ffn_br': _L0_ffn_in['br'], 'L0_ffn_Wq': _L0_ffn_in['Wq'], 'L0_ffn_bq': _L0_ffn_in['bq'], 'L0_ffn_Wk': _L0_ffn_in['Wk'], 'L0_ffn_bk': _L0_ffn_in['bk'], 'L0_ffn_Wv': _L0_ffn_in['Wv'], 'L0_ffn_bv': _L0_ffn_in['bv'], 'L0_ffn_Wo': _L0_ffn_in['Wo'], 'L0_ffn_bo': _L0_ffn_in['bo'], 'L0_ffn_Wm': _L0_ffn_in['Wm'], 'L0_ffn_bm': _L0_ffn_in['bm'], 'L0_ffn_W1': _L0_ffn_in['W1'], 'L0_ffn_bf1': _L0_ffn_in['bf1'], 'L0_ffn_W2': _L0_ffn_in['W2'], 'L0_ffn_bf2': _L0_ffn_in['bf2'], 'L1_gnn_W1': _L1_gnn_in['W1'], 'L1_gnn_att_src1': _L1_gnn_in['att_src1'], 'L1_gnn_att_dst1': _L1_gnn_in['att_dst1'], 'L1_gnn_b1': _L1_gnn_in['b1'], 'L1_gnn_W2': _L1_gnn_in['W2'], 'L1_gnn_att_src2': _L1_gnn_in['att_src2'], 'L1_gnn_att_dst2': _L1_gnn_in['att_dst2'], 'L1_gnn_b2': _L1_gnn_in['b2'], 'L1_ffn_w_router': _L1_ffn_in['w_router'], 'L1_ffn_expert_bias': _L1_ffn_in['expert_bias'], 'L1_ffn_Wg': _L1_ffn_in['Wg'], 'L1_ffn_Wu': _L1_ffn_in['Wu'], 'L1_ffn_Wd': _L1_ffn_in['Wd'], 'L1_ffn_sg': _L1_ffn_in['sg'], 'L1_ffn_su': _L1_ffn_in['su'], 'L1_ffn_sd': _L1_ffn_in['sd'], 'L2_gnn_W': _L2_gnn_in['W'], 'L2_gnn_attn_l': _L2_gnn_in['attn_l'], 'L2_gnn_attn_r': _L2_gnn_in['attn_r'], 'L2_gnn_W_res': _L2_gnn_in['W_res'], 'L2_ffn_Wg': _L2_ffn_in['Wg'], 'L2_ffn_bg': _L2_ffn_in['bg'], 'L2_ffn_W1': _L2_ffn_in['W1'], 'L2_ffn_b1': _L2_ffn_in['b1'], 'L2_ffn_W2': _L2_ffn_in['W2'], 'L2_ffn_b2': _L2_ffn_in['b2'], 'L3_gnn_W1': _L3_gnn_in['W1'], 'L3_gnn_att_src1': _L3_gnn_in['att_src1'], 'L3_gnn_att_dst1': _L3_gnn_in['att_dst1'], 'L3_gnn_b1': _L3_gnn_in['b1'], 'L3_gnn_W2': _L3_gnn_in['W2'], 'L3_gnn_att_src2': _L3_gnn_in['att_src2'], 'L3_gnn_att_dst2': _L3_gnn_in['att_dst2'], 'L3_gnn_b2': _L3_gnn_in['b2'], 'L3_ffn_router_w': _L3_ffn_in['router_w'], 'L3_ffn_Wg': _L3_ffn_in['Wg'], 'L3_ffn_Wu': _L3_ffn_in['Wu'], 'L3_ffn_Wd': _L3_ffn_in['Wd']}

def reference(x, src, dst, L0_gnn_W1, L0_gnn_a_src1, L0_gnn_a_dst1, L0_gnn_b1, L0_gnn_W2, L0_gnn_a_src2, L0_gnn_a_dst2, L0_gnn_b2, L0_ffn_g1, L0_ffn_b1, L0_ffn_g2, L0_ffn_b2, L0_ffn_Wr, L0_ffn_br, L0_ffn_Wq, L0_ffn_bq, L0_ffn_Wk, L0_ffn_bk, L0_ffn_Wv, L0_ffn_bv, L0_ffn_Wo, L0_ffn_bo, L0_ffn_Wm, L0_ffn_bm, L0_ffn_W1, L0_ffn_bf1, L0_ffn_W2, L0_ffn_bf2, L1_gnn_W1, L1_gnn_att_src1, L1_gnn_att_dst1, L1_gnn_b1, L1_gnn_W2, L1_gnn_att_src2, L1_gnn_att_dst2, L1_gnn_b2, L1_ffn_w_router, L1_ffn_expert_bias, L1_ffn_Wg, L1_ffn_Wu, L1_ffn_Wd, L1_ffn_sg, L1_ffn_su, L1_ffn_sd, L2_gnn_W, L2_gnn_attn_l, L2_gnn_attn_r, L2_gnn_W_res, L2_ffn_Wg, L2_ffn_bg, L2_ffn_W1, L2_ffn_b1, L2_ffn_W2, L2_ffn_b2, L3_gnn_W1, L3_gnn_att_src1, L3_gnn_att_dst1, L3_gnn_b1, L3_gnn_W2, L3_gnn_att_src2, L3_gnn_att_dst2, L3_gnn_b2, L3_ffn_router_w, L3_ffn_Wg, L3_ffn_Wu, L3_ffn_Wd):
    import jax
    import jax.numpy as jnp

    def _L0_gnn_ref(x, W1, a_src1, a_dst1, b1, W2, a_src2, a_dst2, b2, edge_list):
        import jax, jax.numpy as jnp
        import numpy as np
        NEG_SLOPE = 0.2
        EPS = 1e-16
        N_NODES = 128
        N_EDGES = 1024
        D_IN = 768
        D_HID = 768
        H1 = 8
        H2 = 1

        def gat_layer(x, W, a_s, a_d, b, edge_index, concat):
            n = x.shape[0]
            H, C = a_s.shape
            h = (x @ W).reshape(n, H, C)
            src, dst = (edge_index[0], edge_index[1])
            alpha_s = jnp.einsum('nhc,hc->nh', h, a_s)
            alpha_d = jnp.einsum('nhc,hc->nh', h, a_d)
            e = jax.nn.leaky_relu(alpha_s[src] + alpha_d[dst], NEG_SLOPE)
            m = jax.ops.segment_max(e, dst, num_segments=n)
            e = jnp.exp(e - m[dst])
            denom = jax.ops.segment_sum(e, dst, num_segments=n)
            alpha = e / (denom[dst] + EPS)
            msg = h[src] * alpha[:, :, None]
            out = jax.ops.segment_sum(msg, dst, num_segments=n)
            out = out.reshape(n, H * C) if concat else out.mean(axis=1)
            return out + b
        h = gat_layer(x, W1, a_src1, a_dst1, b1, edge_list, concat=True)
        h = jax.nn.elu(h)
        out = gat_layer(h, W2, a_src2, a_dst2, b2, edge_list, concat=True)
        return out

    def _L0_ffn_ref(hidden_states, g1, b1, g2, b2, Wr, br, Wq, bq, Wk, bk, Wv, bv, Wo, bo, Wm, bm, W1, bf1, W2, bf2):
        import jax, jax.numpy as jnp
        import numpy as np
        B, L, D, H, F = (4, 32, 768, 12, 48)
        ROUTE_FRAC = 0.15
        LN_EPS = 1e-05

        def _ln(x, g, b):
            m = jnp.mean(x, axis=-1, keepdims=True)
            v = jnp.mean((x - m) ** 2, axis=-1, keepdims=True)
            return (x - m) * jax.lax.rsqrt(v + LN_EPS) * g + b
        b, l, d = hidden_states.shape
        dh = d // H
        normed = _ln(hidden_states, g1, b1)
        scores = jax.nn.sigmoid(jnp.einsum('bld,d->bl', normed, Wr) + br)
        k = max(1, int(round(ROUTE_FRAC * l)))
        _, idx = jax.lax.top_k(-scores, k)
        attn_mask = jnp.zeros((b, l), bool).at[jnp.arange(b)[:, None], idx].set(True)
        q = (normed @ Wq + bq).reshape(b, l, H, dh)
        kk = (normed @ Wk + bk).reshape(b, l, H, dh)
        v = (normed @ Wv + bv).reshape(b, l, H, dh)
        logits = jnp.einsum('blhd,bmhd->bhlm', q, kk) / jnp.sqrt(jnp.float32(dh))
        probs = jax.nn.softmax(logits, axis=-1)
        ctx = jnp.einsum('bhlm,bmhd->blhd', probs, v).reshape(b, l, d)
        attn_out = ctx @ Wo + bo
        w = scores / (jnp.sum(scores, axis=1, keepdims=True) + 1e-06)
        pooled = jnp.einsum('bl,bld->bd', w, normed)
        mix_out = (normed + scores[..., None] * pooled[:, None, :]) @ Wm + bm
        merged = jnp.where(attn_mask[..., None], attn_out, mix_out)
        h = hidden_states + merged
        n2 = _ln(h, g2, b2)
        ffn = jax.nn.gelu(n2 @ W1 + bf1, approximate=False) @ W2 + bf2
        return h + ffn

    def _L1_gnn_ref(x, edge_index, W1, att_src1, att_dst1, b1, W2, att_src2, att_dst2, b2):
        import jax, jax.numpy as jnp
        import numpy as np
        N_NODES = 10000
        NEG_SLOPE = 0.2
        EPS = 1e-16

        def gat_layer(x, W, att_src, att_dst, bias, src, dst, heads, out_ch, concat):
            n = x.shape[0]
            h = (x @ W.T).reshape(n, heads, out_ch)
            a_src = jnp.einsum('nhc,hc->nh', h, att_src)
            a_dst = jnp.einsum('nhc,hc->nh', h, att_dst)
            e = a_src[src] + a_dst[dst]
            e = jax.nn.leaky_relu(e, NEG_SLOPE)
            m = jax.ops.segment_max(e, dst, num_segments=n)
            ex = jnp.exp(e - m[dst])
            denom = jax.ops.segment_sum(ex, dst, num_segments=n)
            alpha = ex / (denom[dst] + EPS)
            msg = alpha[:, :, None] * h[src]
            out = jax.ops.segment_sum(msg, dst, num_segments=n)
            if concat:
                out = out.reshape(n, heads * out_ch)
            else:
                out = out.mean(axis=1)
            return out + bias
        src, dst = (edge_index[0], edge_index[1])
        h = gat_layer(x, W1, att_src1, att_dst1, b1, src, dst, heads=8, out_ch=128, concat=True)
        h = jax.nn.relu(h)
        out = gat_layer(h, W2, att_src2, att_dst2, b2, src, dst, heads=1, out_ch=768, concat=True)
        return out

    def _L1_ffn_ref(x, w_router, expert_bias, Wg, Wu, Wd, sg, su, sd):
        import jax, jax.numpy as jnp
        import numpy as np
        B, S, D = (2, 32, 768)
        E, K, F = (8, 2, 1536)

        def _swiglu(xf, wg, wu, wd):
            return jax.nn.silu(xf @ wg.T) * (xf @ wu.T) @ wd.T
        b, s, d = x.shape
        xf = x.reshape(-1, d)
        T = xf.shape[0]
        e = w_router.shape[0]
        logits = xf @ w_router.T
        scores = jax.nn.softmax(logits, axis=-1)
        selection = scores + expert_bias[None, :]
        _, top_idx = jax.lax.top_k(selection, K)
        top_s = jnp.take_along_axis(scores, top_idx, axis=-1)
        top_s = top_s / (jnp.sum(top_s, axis=-1, keepdims=True) + 1e-09)
        comb = jnp.zeros((T, e), dtype=x.dtype).at[jnp.arange(T)[:, None], top_idx].add(top_s)

        def body(acc, p):
            wg, wu, wd, c = p
            return (acc + c[:, None] * _swiglu(xf, wg, wu, wd), None)
        routed, _ = jax.lax.scan(body, jnp.zeros_like(xf), (Wg, Wu, Wd, comb.T))
        out = routed + _swiglu(xf, sg, su, sd)
        return out.reshape(b, s, d)

    def _L2_gnn_ref(h, src, dst, W, attn_l, attn_r, W_res):
        import jax, jax.numpy as jnp
        import numpy as np
        N = 20000
        DEG = 16
        E = N * DEG
        H = 12
        DIN = 64
        DOUT = 64
        NEG_SLOPE = 0.2
        n = h.shape[0]
        hv = h.reshape(n, H, DIN)
        ft = jnp.einsum('nhd,od->nho', hv, W)
        a1 = jnp.sum(ft * attn_l, axis=-1)
        a2 = jnp.sum(ft * attn_r, axis=-1)
        e = jax.nn.leaky_relu(a1[src] + a2[dst], negative_slope=NEG_SLOPE)
        m = jax.ops.segment_max(e, dst, num_segments=n)
        m = jnp.where(jnp.isfinite(m), m, 0.0)
        w = jnp.exp(e - m[dst])
        denom = jax.ops.segment_sum(w, dst, num_segments=n)
        alpha = w / jnp.maximum(denom[dst], 1e-16)
        msg = alpha[:, :, None] * ft[src]
        agg = jax.ops.segment_sum(msg, dst, num_segments=n)
        res = jnp.einsum('nhd,od->nho', hv, W_res)
        out = jax.nn.relu((agg + res).reshape(n, H * DOUT))
        return out

    def _L2_ffn_ref(x, Wg, bg, W1, b1, W2, b2):
        import jax, jax.numpy as jnp
        import numpy as np
        DIM = 768
        NUM_EXPERTS = 8
        HIDDEN = 48
        TOP_K = 2
        B, N = (1, 1024)
        Bc, Nc, D = x.shape
        xt = x.reshape(-1, D)
        gate = xt @ Wg + bg
        scores, idx = jax.lax.top_k(gate, TOP_K)
        h = jax.nn.gelu(jnp.einsum('td,edh->eth', xt, W1) + b1[:, None, :], approximate=False)
        y = jnp.einsum('eth,ehd->etd', h, W2) + b2[:, None, :]
        comb = jnp.sum(jax.nn.one_hot(idx, NUM_EXPERTS, dtype=x.dtype) * scores[..., None], axis=1)
        out = jnp.einsum('te,etd->td', comb, y)
        return out.reshape(Bc, Nc, D)

    def _L3_gnn_ref(x, edge_index, W1, att_src1, att_dst1, b1, W2, att_src2, att_dst2, b2):
        import jax, jax.numpy as jnp
        import numpy as np
        N_NODES = 10000
        N_EDGES = 2500
        NEG_SLOPE = 0.2

        def _gat_layer(x, src, dst, W, a_src, a_dst, bias, concat):
            N = x.shape[0]
            H, C = a_src.shape
            h = (x @ W).reshape(N, H, C)
            al_s = jnp.einsum('nhc,hc->nh', h, a_src)
            al_d = jnp.einsum('nhc,hc->nh', h, a_dst)
            e = jax.nn.leaky_relu(al_s[src] + al_d[dst], NEG_SLOPE)
            m = jax.ops.segment_max(e, dst, num_segments=N)
            ex = jnp.exp(e - m[dst])
            denom = jax.ops.segment_sum(ex, dst, num_segments=N)
            alpha = ex / (denom[dst] + 1e-16)
            msg = h[src] * alpha[:, :, None]
            out = jax.ops.segment_sum(msg, dst, num_segments=N)
            out = out.reshape(N, H * C) if concat else out.mean(axis=1)
            return out + bias
        N = x.shape[0]
        loops = jnp.arange(N, dtype=edge_index.dtype)
        src = jnp.concatenate([edge_index[0], loops])
        dst = jnp.concatenate([edge_index[1], loops])
        h = jax.nn.elu(_gat_layer(x, src, dst, W1, att_src1, att_dst1, b1, concat=True))
        out = _gat_layer(h, src, dst, W2, att_src2, att_dst2, b2, concat=False)
        return out

    def _L3_ffn_ref(x, router_w, Wg, Wu, Wd):
        import jax, jax.numpy as jnp
        import numpy as np
        B, T, D, E, K = (4, 32, 768, 8, 2)
        H = 4 * D
        Bv, Tv, Dv = x.shape
        N = Bv * Tv
        xf = x.reshape(N, Dv)
        logits = (xf @ router_w.T).astype(jnp.float32)
        top_logits, top_idx = jax.lax.top_k(logits, K)
        top_w = jax.nn.softmax(top_logits, axis=-1).astype(x.dtype)
        out = jnp.zeros_like(xf)
        for e in range(E):
            w_e = jnp.sum(top_w * (top_idx == e), axis=-1)
            h = jax.nn.silu(xf @ Wg[e].T) * (xf @ Wu[e].T)
            out = out + h @ Wd[e].T * w_e[:, None]
        return out.reshape(Bv, Tv, Dv)
    edge_index = jnp.stack([src, dst])
    x = x + _L0_gnn_ref(_layernorm(x, axis=-1), L0_gnn_W1, L0_gnn_a_src1, L0_gnn_a_dst1, L0_gnn_b1, L0_gnn_W2, L0_gnn_a_src2, L0_gnn_a_dst2, L0_gnn_b2, edge_index)
    x = x + _L0_ffn_ref(_layernorm(x, axis=-1)[None], L0_ffn_g1, L0_ffn_b1, L0_ffn_g2, L0_ffn_b2, L0_ffn_Wr, L0_ffn_br, L0_ffn_Wq, L0_ffn_bq, L0_ffn_Wk, L0_ffn_bk, L0_ffn_Wv, L0_ffn_bv, L0_ffn_Wo, L0_ffn_bo, L0_ffn_Wm, L0_ffn_bm, L0_ffn_W1, L0_ffn_bf1, L0_ffn_W2, L0_ffn_bf2)[0]
    x = x + _L1_gnn_ref(_layernorm(x, axis=-1), edge_index, L1_gnn_W1, L1_gnn_att_src1, L1_gnn_att_dst1, L1_gnn_b1, L1_gnn_W2, L1_gnn_att_src2, L1_gnn_att_dst2, L1_gnn_b2)
    x = x + _L1_ffn_ref(_layernorm(x, axis=-1)[None], L1_ffn_w_router, L1_ffn_expert_bias, L1_ffn_Wg, L1_ffn_Wu, L1_ffn_Wd, L1_ffn_sg, L1_ffn_su, L1_ffn_sd)[0]
    x = x + _L2_gnn_ref(_layernorm(x, axis=-1), src, dst, L2_gnn_W, L2_gnn_attn_l, L2_gnn_attn_r, L2_gnn_W_res)
    x = x + _L2_ffn_ref(_layernorm(x, axis=-1)[None], L2_ffn_Wg, L2_ffn_bg, L2_ffn_W1, L2_ffn_b1, L2_ffn_W2, L2_ffn_b2)[0]
    x = x + _L3_gnn_ref(_layernorm(x, axis=-1), edge_index, L3_gnn_W1, L3_gnn_att_src1, L3_gnn_att_dst1, L3_gnn_b1, L3_gnn_W2, L3_gnn_att_src2, L3_gnn_att_dst2, L3_gnn_b2)
    x = x + _L3_ffn_ref(_layernorm(x, axis=-1)[None], L3_ffn_router_w, L3_ffn_Wg, L3_ffn_Wu, L3_ffn_Wd)[0]
    return x

_drawn_inputs = setup_inputs


def setup_inputs(seed=0):
    import zlib

    import numpy as np

    out = dict(_drawn_inputs(seed))
    spreads = {'L0_gnn_b1': (0.0, 0.1),
     'L0_gnn_b2': (0.0, 0.1),
     'L0_ffn_g1': (1.0, 0.2),
     'L0_ffn_b1': (0.0, 0.271),
     'L0_ffn_g2': (1.0, 0.6),
     'L0_ffn_b2': (0.0, 0.8),
     'L0_ffn_bq': (0.0, 2.0),
     'L0_ffn_bk': (0.0, 2.0),
     'L0_ffn_bv': (0.0, 0.8),
     'L0_ffn_bo': (0.0, 0.628),
     'L0_ffn_bm': (0.0, 0.1),
     'L0_ffn_bf1': (0.0, 0.8),
     'L0_ffn_bf2': (0.0, 0.1),
     'L1_gnn_b1': (0.0, 0.354),
     'L1_gnn_b2': (0.0, 0.1),
     'L1_ffn_expert_bias': (0.0, 0.329),
     'L3_gnn_b1': (0.0, 0.309),
     'L3_gnn_b2': (0.0, 0.283)}
    factors = {'L0_ffn_Wq': 8.0,
     'L0_ffn_Wk': 8.0,
     'L0_ffn_W1': 3.632,
     'L0_ffn_W2': 3.821,
     'L1_gnn_att_src1': 3.223,
     'L1_gnn_att_dst1': 8.0,
     'L1_gnn_att_src2': 8.0,
     'L1_gnn_att_dst2': 8.0,
     'L2_ffn_bg': 8.0,
     'L2_ffn_b1': 8.0,
     'L3_gnn_att_src1': 2.898,
     'L3_gnn_att_dst1': 8.0,
     'L3_gnn_att_src2': 8.0,
     'L3_gnn_att_dst2': 8.0,
     'L3_ffn_router_w': 8.0,
     'L3_ffn_Wg': 8.0,
     'L3_ffn_Wu': 8.0,
     'L3_ffn_Wd': 8.0}
    for name, (base, spread) in spreads.items():
        noise = np.random.default_rng([zlib.crc32(name.encode()), seed]).standard_normal(out[name].shape)
        drawn = base * np.exp(spread * noise) if base else spread * noise
        out[name] = jnp.asarray(drawn.astype(out[name].dtype))
    for name, factor in factors.items():
        out[name] = (out[name] * factor).astype(out[name].dtype)
    return out
```

```python
from contextlib import ExitStack

import concourse.bass as bass
from concourse import mybir

ALU = mybir.AluOpType
ACT = mybir.ActivationFunctionType
AX_X = mybir.AxisListType.X
F32 = mybir.dt.float32
F32R = mybir.dt.float32r
BF16 = mybir.dt.bfloat16
I32 = mybir.dt.int32

P = 128
D = 768
KT = D // P
E_TILES = 16
SLAB = 3072
SEG = 512
RING = 6
LN_EPS = 1e-5
SLOPE = 0.2
NOT_AN_EDGE = 1e30
ROUTED = 19
HEADS = 12
DH = D // HEADS
F0 = 48
E8 = 8
F2 = 48

GAT = [
    dict(H=8, C=768, loops=False),
    dict(H=1, C=768, loops=False),
    dict(H=8, C=128, loops=False),
    dict(H=1, C=768, loops=False),
    dict(H=12, C=64, loops=False),
    dict(H=4, C=512, loops=True),
    dict(H=1, C=768, loops=True),
]
FIRST = {
    0: dict(w1=0, w2=12, segs=12, bias=0, elu=True),
    2: dict(w1=32, w2=34, segs=2, bias=12, elu=False),
    5: dict(w1=119, w2=123, segs=4, bias=14, elu=True),
}
LAYER2_BIAS = {1: 18, 3: 19, 6: 20}
ROW_BV, ROW_BF2, ROW_L2B1, ROW_L2BG = 21, 22, 23, 24
ROWS = 32
FFN0_SLAB = 24
L2_SLAB = 117
N_SLABS = 271
MOE = {
    1: dict(slab=36, chunks=27, per=3, first=0),
    3: dict(slab=127, chunks=48, per=6, first=27),
}


def is_moe_slab(n):
    return any(m["slab"] <= n < m["slab"] + 3 * m["chunks"] for m in MOE.values())


def gnn_ffn_kernel(nc, x_in, edges_in, weights, rows_in, cols_in, small_in, attn_in, ffn0_vectors, l2_b2, out):
    with ExitStack() as ctx:
        def sb(name, shape, dt=F32):
            return ctx.enter_context(nc.sbuf_tensor(name, shape, dt))

        def psum(name, shape, dt=F32):
            return ctx.enter_context(nc.psum_tensor(name, shape, dt))

        sems = {}

        def S(name):
            if name not in sems:
                sems[name] = ctx.enter_context(nc.semaphore(name))
            return sems[name]

        ring = sb("ring", [P, RING, SLAB])
        X = sb("X", [P, D])
        XN = sb("XN", [P, D])
        HID = sb("HID", [P, D])
        H1 = sb("H1", [P, D])
        XT = sb("XT", [P, 2, KT, P])
        ident = sb("ident", [P, P])
        ones = sb("ones", [P, P])
        below = sb("below", [P, P])
        tie8 = sb("tie8", [P, E8, E8])
        counts = sb("counts", [P, 2, P])
        maskb = sb("maskb", [P, 2, P])
        rows = sb("rows", [ROWS, D])
        cols = sb("cols", [P, 16])
        small = sb("small", [P, 2 * KT * E8 + 2 * P])
        b2m = sb("b2m", [E8, D])
        stats = sb("stats", [P, 2, 6])
        mv = sb("mv", [P, 2])
        std = sb("std", [P, 1])
        rstd = sb("rstd", [P, 1])
        eps = sb("eps", [P, 1])
        al = sb("al", [P, 2, HEADS])
        hmax = sb("hmax", [P, HEADS])
        hsum = sb("hsum", [P, HEADS])
        hrec = sb("hrec", [P, HEADS])
        tk = sb("tk", [P, 8])
        r8 = sb("r8", [P, 8, E8])
        g64 = sb("g64", [P, 2, E8, E8])
        CB = sb("CB", [P, 48])
        low = sb("low", [P, 2, SEG])
        act1 = sb("act1", [P, 2, SEG])
        act1T = sb("act1T", [P, 2, SEG])
        silu = sb("silu", [P, SEG])
        hexp = sb("hexp", [P, SEG])
        XTh = sb("XTh", [P, KT, P], F32R)
        XTl = sb("XTl", [P, KT, P], F32R)
        hTh = sb("hTh", [P, 4, P], F32R)
        hTl = sb("hTl", [P, 4, P], F32R)

        with nc.sbuf_tensor("scratch", [P, 6 * SLAB], F32) as scratch:
            pass
        wh = {k: sb(f"w_hi_{k}", [P, SLAB], F32R) for k in "gud"}
        wl = {k: sb(f"w_lo_{k}", [P, SLAB], F32R) for k in "gud"}
        hs1 = scratch[:, 0:6144]
        AB = [scratch[:, 6144:9216], scratch[:, 9216:13312]]
        EE = scratch[:, 13312:14848]
        ALT = scratch[:, 14848:16384]
        hs2 = scratch[:, 16384:17152]
        junk = scratch[:, 17152:17920]
        ids_i = scratch[:, 13312:13344].bitcast(I32)
        ids_f = scratch[:, 13344:13376]
        iota_i = scratch[:, 13440:13568].bitcast(I32)
        iota_f = scratch[:, 13568:13696]
        onehot = scratch[:, 0:2048].bitcast(BF16).rearrange("p (a t n) -> p a t n", a=2, t=E_TILES)
        NV = 7
        vec0 = scratch[:, 0:NV * D + 1]
        qT = scratch[:, 6144:6912]
        kz = scratch[:, 6912:8448].rearrange("p (t a n) -> p t a n", t=KT, a=2)
        V = scratch[:, 8448:9216]
        MIX = scratch[:, 9216:9984]
        CTX = scratch[:, 9984:10752]
        FT = scratch[:, 10752:10880]
        G2 = scratch[:, 0:384]
        G2T = scratch[:, 384:768]
        CBT = scratch[:, 768:896]

        def vec(i):
            return vec0[:, i * D:(i + 1) * D]

        PJ = psum("PJ", [P, 2 * SEG])
        TP = psum("TP", [P, 3 * SEG])
        MS = psum("MS", [P, SEG])
        AC = psum("AC", [P, 2 * SEG])

        land = [S(f"slab_landed_{i}") for i in range(RING)]

        def landed(eng, n):
            eng.wait_ge(land[n % RING], 16 * (n // RING + 1))

        def halves():
            return ((0, SEG), (SEG, D))

        SEG_BASE = {0: 0, 2: 12, 5: 14}
        N_BASE = [0, 12, 13, 15, 16, 17, 21]

        def w_tile(t, c0, c1):
            n = FFN0_SLAB + t // 4
            return ring[:, n % RING, (t % 4) * D + c0:(t % 4) * D + c1]

        block = ctx.enter_context(nc.Block())

        @block.sync
        def _(sp):
            sp.dma_start(X[:], x_in).then_inc(S("x_loaded"), 16)

            def slab(n, index):
                sp.dma_start(ring[:, n % RING, :], weights[index]).then_inc(land[n % RING], 16)

            def single(n):
                old = n - RING
                if old >= 0:
                    if is_moe_slab(old):
                        m = MOE[1] if old < 127 else MOE[3]
                        k = old - m["slab"]
                        sp.wait_ge(S("lo_" + "gud"[k % 3]), m["first"] + k // 3 + 1)
                    else:
                        sp.wait_ge(S("slabs_used"), sum(not is_moe_slab(i) for i in range(old + 1)))
                slab(n, n)

            for n in range(42):
                single(n)
            with sp.Fori(0, 12) as it:
                for j in range(6):
                    sp.wait_ge(S("lo_" + "gud"[j % 3]), it * 2 + (1 + j // 3))
                    slab(42 + j, it * 6 + (42 + j))
            for n in range(114, 133):
                single(n)
            with sp.Fori(0, 23) as it:
                for j in range(6):
                    sp.wait_ge(S("lo_" + "gud"[j % 3]), it * 2 + (MOE[3]["first"] + 1 + j // 3))
                    slab(133 + j, it * 6 + (133 + j))
            sp.wait_ge(S("x_ready"), 8)
            sp.dma_start(out, X[:]).then_inc(S("out_stored"), 16)
            sp.wait_ge(S("out_stored"), 16)

        @block.gpsimd
        def _(pool):
            pool.dma_start(ids_i, edges_in).then_inc(S("edges_loaded"), 16)
            nc.gpsimd.iota(iota_i, pattern=[[1, P]], base=0, channel_multiplier=0).then_inc(S("iota_made"), 1)
            nc.gpsimd.memset(ident[:], 0.0).then_inc(S("const_filled"), 1)
            nc.gpsimd.memset(ones[:], 1.0).then_inc(S("const_filled"), 1)
            nc.gpsimd.memset(below[:], 1.0).then_inc(S("const_filled"), 1)
            nc.gpsimd.memset(tie8[:], 1.0).then_inc(S("const_filled"), 1)
            nc.gpsimd.memset(eps[:], LN_EPS).then_inc(S("const_filled"), 1)
            pool.wait_ge(S("const_filled"), 5)
            nc.gpsimd.affine_select(out=ident[:], in_=ident[:], compare_op=ALU.not_equal, fill=1.0, base=0,
                                    pattern=[[-1, P]], channel_multiplier=1).then_inc(S("const_ready"), 1)
            nc.gpsimd.affine_select(out=below[:], in_=below[:], compare_op=ALU.is_gt, fill=0.0, base=0,
                                    pattern=[[-1, P]], channel_multiplier=1).then_inc(S("const_ready"), 1)
            nc.gpsimd.affine_select(out=tie8[:], in_=tie8[:], compare_op=ALU.is_gt, fill=0.0, base=0,
                                    pattern=[[1, E8], [-1, E8]], channel_multiplier=0).then_inc(S("const_ready"), 1)

            def attn_vectors(c, buf, at, n, off):
                pool.dma_start(AB[buf][:, at:at + n], attn_in[:, off:off + n].to_broadcast([P, n])) \
                    .then_inc(S(f"attn_loaded_{c}"), 16)

            for h in range(2):
                pool.dma_start(AB[0][:, 1536 * h:1536 * h + 1536],
                               attn_in[:, 1536 * h:1536 * h + 1536].to_broadcast([P, 1536])) \
                    .then_inc(S(f"attn_head_loaded_{h}"), 16)
            pool.dma_start(rows[:], rows_in).then_inc(S("small_loaded"), 16)
            pool.dma_start(cols[:], cols_in).then_inc(S("small_loaded"), 16)
            pool.dma_start(small[:], small_in).then_inc(S("small_loaded"), 16)
            pool.dma_start(b2m[:], l2_b2).then_inc(S("small_loaded"), 16)
            attn_vectors(1, 1, 0, 1536, 12288)
            for h in range(2, 8):
                pool.wait_ge(S("head_terms"), h - 1)
                pool.dma_start(AB[0][:, 1536 * (h % 2):1536 * (h % 2) + 1536],
                               attn_in[:, 1536 * h:1536 * h + 1536].to_broadcast([P, 1536])) \
                    .then_inc(S(f"attn_head_loaded_{h % 2}"), 16)
            pool.wait_ge(S("segment_product"), 12)
            pool.dma_start(vec0, ffn0_vectors.to_broadcast([P, NV * D + 1])).then_inc(S("ffn0_vectors_loaded"), 16)
            pool.wait_ge(S("x_ready"), 2)
            attn_vectors(2, 0, 0, 2048, 13824)
            attn_vectors(3, 1, 0, 1536, 15872)
            pool.wait_ge(S("x_ready"), 4)
            attn_vectors(4, 0, 0, 1536, 17408)
            attn_vectors(5, 1, 0, 4096, 18944)
            pool.wait_ge(S("terms_ready"), 5)
            attn_vectors(6, 0, 0, 1536, 23040)

        @block.scalar
        def _(act):
            A = nc.scalar.activation

            def ln_std(i):
                act.wait_ge(S("ln_variance"), i + 1)
                A(std[:], mv[:, 1:2], ACT.Sqrt, bias=eps[:]).then_inc(S("ln_std"), 1)

            def transposed(k):
                act.wait_ge(S("tr_product"), k + 1)
                A(XT[:, k % 2].rearrange("p k n -> p (k n)"), TP[:, 0:D], ACT.Copy).then_inc(S("tr_ready"), 1)

            def copy_h(c):
                if c in FIRST:
                    for j in range(FIRST[c]["segs"]):
                        act.wait_ge(S("projected"), N_BASE[c] + j + 1)
                        A(hs1[:, j * SEG:(j + 1) * SEG], PJ[:, (j % 2) * SEG:(j % 2 + 1) * SEG], ACT.Copy) \
                            .then_inc(S("h_copied"), 1)
                else:
                    act.wait_ge(S("projected"), N_BASE[c] + 1)
                    A(hs2, AC[:, 0:D], ACT.Copy).then_inc(S("h_copied"), 1)

            def attention(c):
                n = GAT[c]["H"] * P
                act.wait_ge(S("logits_shifted"), c + 1)
                A(EE[:, 0:n], EE[:, 0:n], ACT.Exp).then_inc(S("exps_ready"), 1)
                act.wait_ge(S("attn_turned"), c + 1)
                A(ALT[:, 0:n], TP[:, 0:n], ACT.Copy).then_inc(S("attn_ready"), 1)

            def segments(c):
                f = FIRST[c]
                for i in range(f["segs"] + 1):
                    if i < f["segs"] and f["elu"]:
                        act.wait_ge(S("low_ready"), {0: 0, 5: 12}[c] + i + 1)
                        A(low[:, i % 2, :], low[:, i % 2, :], ACT.Exp).then_inc(S("low_exp"), 1)
                    if i >= 1:
                        s = SEG_BASE[c] + i - 1
                        act.wait_ge(S("segment_turned"), s + 1)
                        if i >= 3:
                            act.wait_ge(S("segment_used"), s - 1)
                        bank = MS[:] if (i - 1) % 2 == 0 else TP[:, 0:SEG]
                        A(act1T[:, (i - 1) % 2, :], bank, ACT.Copy).then_inc(S("segmentT_ready"), 1)

            def mixture(l):
                m = MOE[l]

                def hi(kind, c0, it):
                    n = m["slab"] + 3 * c0 + "gud".index(kind)
                    act.wait_ge(land[n % RING], it * 16 + 16 * (n // RING + 1))
                    if m["first"] + c0:
                        act.wait_ge(S("pe_" + kind), it * 2 + (m["first"] + c0))
                    A(wh[kind][:], ring[:, n % RING, :], ACT.Copy).then_inc(S("hi_" + kind), 1)

                def chunk(c0, it=0, first=False, last=False):
                    q = m["first"] + c0
                    act.wait_ge(S("pe_g"), it * 2 + (q + 1))
                    if q:
                        act.wait_ge(S("hidden_ready"), it * 2 + q)
                    A(silu[:], PJ[:, 0:SEG], ACT.Silu).then_inc(S("silu_ready"), 1)
                    if not first:
                        act.wait_ge(S("pe_t"), it * 2 + q)
                        A(hTh[:].rearrange("p k n -> p (k n)"), TP[:, 0:SEG], ACT.Copy).then_inc(S("hTh_ready"), 1)
                    if not last:
                        hi("g", c0 + 1, it)
                        hi("u", c0 + 1, it)
                    hi("d", c0, it)

                k = {1: 6, 3: 10}[l]
                transposed(k)
                act.wait_ge(S("tr_ready"), k + 1)
                A(XTh[:], XT[:, k % 2], ACT.Copy).then_inc(S("XTh_ready"), 1)
                hi("g", 0, 0)
                hi("u", 0, 0)
                act.wait_ge(S("router_shifted"), {1: 1, 3: 2}[l])
                A(r8[:, 1, :], r8[:, 0, :], ACT.Exp).then_inc(S("router_exp"), 1)
                chunk(0, first=True)
                pairs = (m["chunks"] - 2) // 2
                with act.Fori(0, pairs) as it:
                    chunk(1, it)
                    chunk(2, it)
                for c in range(1 + 2 * pairs, m["chunks"]):
                    chunk(c, last=(c == m["chunks"] - 1))
                act.wait_ge(S("pe_t"), m["first"] + m["chunks"])
                A(hTh[:].rearrange("p k n -> p (k n)"), TP[:, 0:SEG], ACT.Copy).then_inc(S("hTh_ready"), 1)

            act.wait_ge(S("const_filled"), 5)
            ln_std(0)
            transposed(0)
            copy_h(0)
            attention(0)
            segments(0)
            copy_h(1)
            attention(1)
            ln_std(1)
            ln_std(2)
            transposed(1)
            act.wait_ge(S("router0_logit"), 1)
            A(tk[:, 1:2], tk[:, 0:1], ACT.Sigmoid, bias=vec0[:, NV * D:NV * D + 1]).then_inc(S("sigmoid_ready"), 1)
            act.wait_ge(S("small_loaded"), 64)
            act.wait_ge(S("q_product"), 1)
            for t in range(KT):
                A(qT[:, t * P:(t + 1) * P], TP[:, t * P:(t + 1) * P], ACT.Identity,
                  bias=cols[:, t:t + 1]).then_inc(S("q_ready"), 1)
            act.wait_ge(S("v_product"), 1)
            A(V, AC[:, 0:D], ACT.Copy).then_inc(S("v_ready"), 1)
            act.wait_ge(S("self_logits_shifted"), 1)
            A(EE[:, 0:HEADS * P], EE[:, 0:HEADS * P], ACT.Exp, scale=DH ** -0.5).then_inc(S("self_exps"), 1)
            act.wait_ge(S("self_turned"), 1)
            A(ALT[:, 0:HEADS * P], TP[:, 0:HEADS * P], ACT.Copy).then_inc(S("self_attn_ready"), 1)
            transposed(2)
            transposed(3)
            ln_std(3)
            transposed(4)
            act.wait_ge(S("f_product"), 1)
            A(FT[0:F0, :], MS[0:F0, 0:P], ACT.Gelu, bias=cols[0:F0, 12:13]).then_inc(S("f_ready"), 1)
            ln_std(4)
            transposed(5)
            copy_h(2)
            attention(2)
            segments(2)
            copy_h(3)
            attention(3)
            ln_std(5)
            mixture(1)
            ln_std(6)
            transposed(7)
            act.wait_ge(S("projected"), N_BASE[4] + 1)
            A(hs2, AC[:, 0:D], ACT.Copy).then_inc(S("h_copied"), 1)
            attention(4)
            ln_std(7)
            transposed(8)
            act.wait_ge(S("l2_hidden_product"), 1)
            A(G2, PJ[:, 0:E8 * F2], ACT.Gelu).then_inc(S("l2_gelu"), 1)
            act.wait_ge(S("l2_turned"), 1)
            A(G2T, TP[:, 0:384], ACT.Copy).then_inc(S("l2_T_ready"), 1)
            A(CBT[0:E8, :], TP[0:E8, SEG:SEG + P], ACT.Copy).then_inc(S("l2_T_ready"), 1)
            ln_std(8)
            transposed(9)
            copy_h(5)
            attention(5)
            segments(5)
            copy_h(6)
            attention(6)
            ln_std(9)
            mixture(3)

        @block.vector
        def _(dve):
            v = nc.vector
            step = [0]

            def then(ins):
                step[0] += 1
                ins.then_inc(S("vector_step"), 1)
                dve.wait_ge(S("vector_step"), step[0])

            def layernorm(i, src, dst, sem=None, count=0):
                then(v.bn_stats(stats[:, 0, :], src[:, 0:384]))
                then(v.bn_stats(stats[:, 1, :], src[:, 384:768]))
                v.bn_aggr(mv[:], stats[:]).then_inc(S("ln_variance"), 1)
                dve.wait_ge(S("ln_variance"), i + 1)
                dve.wait_ge(S("ln_std"), i + 1)
                then(v.reciprocal(rstd[:], std[:]))
                last = v.tensor_scalar(dst, src, mv[:, 0:1], rstd[:], ALU.subtract, ALU.mult)
                if sem is None:
                    then(last)
                else:
                    last.then_inc(S(sem), 1)
                    dve.wait_ge(S(sem), count)

            def softmax_tail(n, heads, exps_sem, exps_count, weight, guard, done_sem):
                e3 = EE[:, 0:n].rearrange("p (h s) -> p h s", h=heads)
                dve.wait_ge(S(exps_sem), exps_count)
                if weight is not None:
                    then(v.tensor_tensor(e3, e3, weight.unsqueeze(1).to_broadcast([P, heads, P]), ALU.mult))
                then(v.tensor_reduce(hsum[:, 0:heads], e3, AX_X, ALU.add))
                if guard is not None:
                    then(v.tensor_scalar(hsum[:, 0:heads], hsum[:, 0:heads], 1e-16, None, guard))
                then(v.reciprocal(hrec[:, 0:heads], hsum[:, 0:heads]))
                v.tensor_tensor(e3, e3, hrec[:, 0:heads].unsqueeze(2).to_broadcast([P, heads, P]), ALU.mult) \
                    .then_inc(S(done_sem), 1)

            def gat(c):
                g = GAT[c]
                H, C, loop = g["H"], g["C"], int(g["loops"])
                hs = hs1 if c in FIRST else hs2
                n = H * P
                if c:
                    dve.wait_ge(S(f"attn_loaded_{c}"), 16)
                buf = 0 if c in (0, 2, 4, 6) else 1
                for h in range(H):
                    if c in FIRST:
                        dve.wait_ge(S("h_copied"), N_BASE[c] + ((h + 1) * C + SEG - 1) // SEG)
                    else:
                        dve.wait_ge(S("h_copied"), N_BASE[c] + 1)
                    if c == 0:
                        dve.wait_ge(S(f"attn_head_loaded_{h % 2}"), 16 * (h // 2 + 1))
                    for side in range(2):
                        a = AB[0][:, 1536 * (h % 2) + side * C:1536 * (h % 2) + (side + 1) * C] if c == 0 else \
                            AB[buf][:, side * H * C + h * C:side * H * C + (h + 1) * C]
                        ins = v.tensor_tensor_reduce(out=junk[:, 0:C], in0=hs[:, h * C:(h + 1) * C], in1=a, scale=1.0,
                                                     scalar=0.0, op0=ALU.mult, op1=ALU.add,
                                                     accum_out=al[:, side, h:h + 1])
                        if side == 0:
                            then(ins)
                    if c == 0 and h < H - 1:
                        ins.then_inc(S("head_terms"), 1)
                        dve.wait_ge(S("head_terms"), h + 1)
                    elif h < H - 1:
                        then(ins)
                ins.then_inc(S("terms_ready"), 1)
                dve.wait_ge(S("terms_ready"), c + 1)
                dve.wait_ge(S("term_rows"), c + 1)
                e3 = EE[:, 0:n].rearrange("p (h s) -> p h s", h=H)
                r3 = TP[:, 0:n].rearrange("p (h s) -> p h s", h=H)
                then(v.tensor_tensor(e3, r3, al[:, 1, 0:H].unsqueeze(2).to_broadcast([P, H, P]), ALU.add))
                then(v.scalar_tensor_tensor(EE[:, 0:n], EE[:, 0:n], SLOPE, EE[:, 0:n], ALU.mult, ALU.max))
                then(v.tensor_tensor(e3, e3, maskb[:, loop, :].unsqueeze(1).to_broadcast([P, H, P]), ALU.add))
                then(v.tensor_reduce(hmax[:, 0:H], e3, AX_X, ALU.max))
                v.tensor_tensor(e3, e3, hmax[:, 0:H].unsqueeze(2).to_broadcast([P, H, P]), ALU.subtract) \
                    .then_inc(S("logits_shifted"), 1)
                softmax_tail(n, H, "exps_ready", c + 1, counts[:, loop, :],
                             ALU.max if c == 4 else ALU.add, "attn_weights")

            def segments(c):
                f = FIRST[c]
                for i in range(f["segs"]):
                    s = SEG_BASE[c] + i
                    z = PJ[:, (i % 2) * SEG:(i % 2 + 1) * SEG]
                    dve.wait_ge(S("segment_product"), s + 1)
                    if i >= 2:
                        dve.wait_ge(S("segment_turned"), s - 1)
                    if f["elu"]:
                        v.tensor_scalar(low[:, i % 2, :], z, 0.0, None, ALU.min).then_inc(S("low_ready"), 1)
                        dve.wait_ge(S("low_exp"), {0: 0, 5: 12}[c] + i + 1)
                        v.scalar_tensor_tensor(act1[:, i % 2, :], low[:, i % 2, :], -1.0, z, ALU.add, ALU.max) \
                            .then_inc(S("segment_ready"), 1)
                    else:
                        v.tensor_scalar(act1[:, i % 2, :], z, 0.0, None, ALU.max).then_inc(S("segment_ready"), 1)
                dve.wait_ge(S("segment_ready"), SEG_BASE[c] + f["segs"])

            def take_x(n, relu=False):
                dve.wait_ge(S("x_product"), n)
                if relu:
                    ins = v.scalar_tensor_tensor(X[:], AC[:, 0:D], 0.0, X[:], ALU.max, ALU.add)
                else:
                    ins = v.tensor_copy(X[:], AC[:, 0:D])
                ins.then_inc(S("x_ready"), 1)
                dve.wait_ge(S("x_ready"), n)

            def top2(values, chosen):
                vi = values.unsqueeze(2).to_broadcast([P, E8, E8])
                vj = values.unsqueeze(1).to_broadcast([P, E8, E8])
                then(v.tensor_tensor(g64[:, 0], vj, vi, ALU.is_gt))
                then(v.tensor_tensor(g64[:, 1], vj, vi, ALU.is_equal))
                then(v.tensor_tensor(g64[:, 1], g64[:, 1], tie8[:], ALU.mult))
                then(v.tensor_tensor(g64[:, 0], g64[:, 0], g64[:, 1], ALU.add))
                then(v.tensor_reduce(r8[:, 7, :], g64[:, 0], AX_X, ALU.add))
                then(v.tensor_scalar(chosen, r8[:, 7, :], 2.0, None, ALU.is_lt))

            def mixture(l):
                m = MOE[l]
                k = {1: 6, 3: 10}[l]
                dve.wait_ge(S("tr_ready"), k + 1)
                dve.wait_ge(S("XTh_ready"), {1: 1, 3: 2}[l])
                v.tensor_tensor(XTl[:], XT[:, k % 2], XTh[:].bitcast(F32), ALU.subtract).then_inc(S("XTl_ready"), 1)

                def lo(kind, c0, it):
                    n = m["slab"] + 3 * c0 + "gud".index(kind)
                    dve.wait_ge(S("hi_" + kind), it * 2 + (m["first"] + c0 + 1))
                    v.tensor_tensor(wl[kind][:], ring[:, n % RING, :], wh[kind][:].bitcast(F32), ALU.subtract) \
                        .then_inc(S("lo_" + kind), 1)

                def turned(q, it):
                    dve.wait_ge(S("hTh_ready"), it * 2 + q)
                    v.tensor_tensor(hTl[:].rearrange("p k n -> p (k n)"), TP[:, 0:SEG],
                                    hTh[:].bitcast(F32).rearrange("p k n -> p (k n)"), ALU.subtract) \
                        .then_inc(S("hTl_ready"), 1)

                def chunk(c0, it=0, first=False, last=False):
                    q = m["first"] + c0
                    if not first:
                        lo("d", c0 - 1, it)
                        turned(q, it)
                    if not last:
                        lo("g", c0 + 1, it)
                    dve.wait_ge(S("silu_ready"), it * 2 + (q + 1))
                    dve.wait_ge(S("pe_u"), it * 2 + (q + 1))
                    v.scalar_tensor_tensor(hexp[:], silu[:], CB[:, bass.ds(it * 2 + c0, 1)], PJ[:, SEG:2 * SEG],
                                           ALU.mult, ALU.mult).then_inc(S("hidden_ready"), 1)
                    if not last:
                        lo("u", c0 + 1, it)

                lo("g", 0, 0)
                lo("u", 0, 0)
                dve.wait_ge(S("router_product"), {1: 1, 3: 2}[l])
                then(v.tensor_copy(r8[:, 2, :], MS[:, 0:E8]))
                then(v.tensor_reduce(hmax[:, 0:1], r8[:, 2, :], AX_X, ALU.max))
                v.tensor_scalar(r8[:, 0, :], r8[:, 2, :], hmax[:, 0:1], None, ALU.subtract) \
                    .then_inc(S("router_shifted"), 1)
                dve.wait_ge(S("router_exp"), {1: 1, 3: 2}[l])
                if l == 1:
                    then(v.tensor_reduce(hsum[:, 0:1], r8[:, 1, :], AX_X, ALU.add))
                    then(v.reciprocal(hrec[:, 0:1], hsum[:, 0:1]))
                    then(v.tensor_scalar(r8[:, 1, :], r8[:, 1, :], hrec[:, 0:1], None, ALU.mult))
                    then(v.tensor_tensor(r8[:, 3, :], r8[:, 1, :], MS[:, 8:16], ALU.add))
                    top2(r8[:, 3, :], r8[:, 4, :])
                    then(v.tensor_tensor(r8[:, 1, :], r8[:, 1, :], r8[:, 4, :], ALU.mult))
                    then(v.tensor_reduce(hsum[:, 0:1], r8[:, 1, :], AX_X, ALU.add))
                    then(v.tensor_scalar(hsum[:, 0:1], hsum[:, 0:1], 1e-9, None, ALU.add))
                else:
                    top2(r8[:, 2, :], r8[:, 4, :])
                    then(v.tensor_tensor(r8[:, 1, :], r8[:, 1, :], r8[:, 4, :], ALU.mult))
                    then(v.tensor_reduce(hsum[:, 0:1], r8[:, 1, :], AX_X, ALU.add))
                then(v.reciprocal(hrec[:, 0:1], hsum[:, 0:1]))
                then(v.tensor_scalar(r8[:, 5, :], r8[:, 1, :], hrec[:, 0:1], None, ALU.mult))
                per = m["per"]
                then(v.tensor_copy(CB[:, 0:E8 * per].rearrange("p (e j) -> p e j", j=per),
                                   r8[:, 5, :].unsqueeze(2).to_broadcast([P, E8, per])))
                if l == 1:
                    then(v.memset(CB[:, E8 * per:E8 * per + per], 1.0))
                chunk(0, first=True)
                pairs = (m["chunks"] - 2) // 2
                with dve.Fori(0, pairs) as it:
                    chunk(1, it)
                    chunk(2, it)
                for c in range(1 + 2 * pairs, m["chunks"]):
                    chunk(c, last=(c == m["chunks"] - 1))
                lo("d", m["chunks"] - 1, 0)
                turned(m["first"] + m["chunks"], 0)

            dve.wait_ge(S("iota_made"), 1)
            then(v.tensor_copy(iota_f, iota_i))
            dve.wait_ge(S("edges_loaded"), 16)
            then(v.tensor_copy(ids_f, ids_i))
            ids3 = ids_f.rearrange("p (a t) -> p a t", a=2)
            for a in range(2):
                v.tensor_tensor(onehot[:, a], iota_f.unsqueeze(1).to_broadcast([P, E_TILES, P]),
                                ids3[:, a].unsqueeze(2).to_broadcast([P, E_TILES, P]), ALU.is_equal) \
                    .then_inc(S("onehot_ready"), 1)
            dve.wait_ge(S("x_loaded"), 16)
            layernorm(0, X[:], XN[:], "tr_input", 1)
            dve.wait_ge(S("counts_product"), 1)
            dve.wait_ge(S("const_ready"), 3)
            then(v.tensor_copy(counts[:, 0, :], MS[:, 0:P]))
            then(v.tensor_tensor(counts[:, 1, :], counts[:, 0, :], ident[:], ALU.add))
            then(v.tensor_scalar(maskb[:], counts[:], 0.0, NOT_AN_EDGE, ALU.is_gt, ALU.mult))
            then(v.tensor_scalar(maskb[:], maskb[:], NOT_AN_EDGE, None, ALU.subtract))
            gat(0)
            segments(0)
            gat(1)
            take_x(1)
            then(v.memset(kz, 0.0))
            layernorm(1, X[:], HID[:])
            layernorm(2, HID[:], XN[:])
            dve.wait_ge(S("ffn0_vectors_loaded"), 16)
            then(v.tensor_tensor(XN[:], XN[:], vec(0), ALU.mult))
            v.tensor_tensor(XN[:], XN[:], vec(1), ALU.add).then_inc(S("tr_input"), 1)
            dve.wait_ge(S("tr_input"), 2)
            v.tensor_tensor_reduce(out=junk, in0=XN[:], in1=vec(2), scale=1.0, scalar=0.0, op0=ALU.mult,
                                   op1=ALU.add, accum_out=tk[:, 0:1]).then_inc(S("router0_logit"), 1)
            dve.wait_ge(S("sigmoid_ready"), 1)
            dve.wait_ge(S("score_row"), 1)
            row = MS[:, 0:P]
            then(v.tensor_scalar(low[:, 0, 0:P], row, tk[:, 1:2], None, ALU.is_lt))
            then(v.scalar_tensor_tensor(low[:, 0, P:2 * P], row, tk[:, 1:2], below[:], ALU.is_equal, ALU.mult))
            then(v.tensor_tensor(low[:, 0, 0:P], low[:, 0, 0:P], low[:, 0, P:2 * P], ALU.add))
            then(v.tensor_reduce(tk[:, 2:3], low[:, 0, 0:P], AX_X, ALU.add))
            then(v.tensor_scalar(tk[:, 3:4], tk[:, 2:3], float(ROUTED), None, ALU.is_lt))
            then(v.tensor_scalar(tk[:, 4:5], tk[:, 2:3], float(ROUTED), None, ALU.is_ge))
            then(v.tensor_scalar(tk[:, 5:6], MS[:, P:P + 1], 1e-6, None, ALU.add))
            then(v.reciprocal(tk[:, 6:7], tk[:, 5:6]))
            v.tensor_tensor(tk[:, 7:8], tk[:, 1:2], tk[:, 6:7], ALU.mult).then_inc(S("pool_weight"), 1)
            dve.wait_ge(S("small_loaded"), 64)
            dve.wait_ge(S("k_product"), 1)
            for t in range(KT):
                for a in range(2):
                    r = slice(a * DH, (a + 1) * DH)
                    v.tensor_scalar(kz[r, t, a, :], PJ[r, t * P:(t + 1) * P], cols[r, 6 + t:7 + t], None,
                                    ALU.add).then_inc(S("k_ready"), 1)
            dve.wait_ge(S("pooled"), 1)
            then(v.scalar_tensor_tensor(MIX, AC[:, 0:D], tk[:, 1:2], XN[:], ALU.mult, ALU.add))
            v.tensor_scalar(MIX, MIX, tk[:, 4:5], None, ALU.mult).then_inc(S("tr_input"), 1)
            n = HEADS * P
            e3 = EE[:, 0:n].rearrange("p (h s) -> p h s", h=HEADS)
            r3 = TP[:, 0:n].rearrange("p (h s) -> p h s", h=HEADS)
            dve.wait_ge(S("self_logits"), 1)
            then(v.tensor_reduce(hmax[:], r3, AX_X, ALU.max))
            v.tensor_tensor(e3, r3, hmax[:].unsqueeze(2).to_broadcast([P, HEADS, P]), ALU.subtract) \
                .then_inc(S("self_logits_shifted"), 1)
            softmax_tail(n, HEADS, "self_exps", 1, None, None, "self_weights")
            dve.wait_ge(S("context"), 1)
            v.tensor_scalar(CTX, AC[:, 0:D], tk[:, 3:4], None, ALU.mult).then_inc(S("tr_input"), 1)
            dve.wait_ge(S("merged"), 1)
            then(v.scalar_tensor_tensor(H1[:], vec(5), tk[:, 3:4], PJ[:, 0:D], ALU.mult, ALU.add))
            then(v.scalar_tensor_tensor(H1[:], vec(6), tk[:, 4:5], H1[:], ALU.mult, ALU.add))
            layernorm(3, H1[:], XN[:])
            then(v.tensor_tensor(XN[:], XN[:], vec(3), ALU.mult))
            v.tensor_tensor(XN[:], XN[:], vec(4), ALU.add).then_inc(S("tr_input"), 1)
            take_x(2)
            layernorm(4, X[:], XN[:], "tr_input", 6)
            gat(2)
            segments(2)
            gat(3)
            take_x(3)
            layernorm(5, X[:], XN[:], "tr_input", 7)
            mixture(1)
            take_x(4)
            layernorm(6, X[:], XN[:], "tr_input", 8)
            gat(4)
            take_x(5, relu=True)
            layernorm(7, X[:], XN[:], "tr_input", 9)
            dve.wait_ge(S("l2_gate_product"), 1)
            then(v.tensor_copy(r8[:, 2, :], MS[:, 0:E8]))
            top2(r8[:, 2, :], r8[:, 4, :])
            then(v.tensor_tensor(r8[:, 5, :], r8[:, 2, :], r8[:, 4, :], ALU.mult))
            dve.wait_ge(S("l2_gelu"), 1)
            g3 = G2.rearrange("p (e f) -> p e f", e=E8)
            v.tensor_tensor(g3, g3, r8[:, 5, :].unsqueeze(2).to_broadcast([P, E8, F2]), ALU.mult) \
                .then_inc(S("l2_weighted"), 1)
            take_x(6)
            layernorm(8, X[:], XN[:], "tr_input", 10)
            gat(5)
            segments(5)
            gat(6)
            take_x(7)
            layernorm(9, X[:], XN[:], "tr_input", 11)
            mixture(3)
            take_x(8)

        @block.tensor
        def _(pe):
            mm = nc.tensor.matmul
            used = [0]

            def slab_used(ins, n=1):
                used[0] += n
                return ins.then_inc(S("slabs_used"), n)

            def turn(k, src):
                pe.wait_ge(S("tr_input"), k + 1)
                for t in range(KT):
                    ins = nc.tensor.transpose(TP[:, t * P:(t + 1) * P], src[:, t * P:(t + 1) * P], ident[:])
                ins.then_inc(S("tr_product"), 1)

            def xt(k, t):
                return XT[:, k % 2, t, :]

            def bias_row(dst, r, c0, c1, start=False, stop=False):
                return mm(dst, ident[0:ROWS, r:r + 1].to_broadcast([ROWS, P]), rows[:, c0:c1], start=start,
                          stop=stop, skip_group_check=True)

            def add_whole(src):
                for a, b in halves():
                    mm(AC[:, a:b], ident[:], src[:, a:b], start=False, stop=False, skip_group_check=True)

            def project(c, k):
                f = FIRST[c]
                pe.wait_ge(S("tr_ready"), k + 1)
                for j in range(f["segs"]):
                    n = f["w1"] + j
                    if j >= 2:
                        pe.wait_ge(S("h_copied"), N_BASE[c] + j - 1)
                    landed(pe, n)
                    for t in range(KT):
                        ins = mm(PJ[:, (j % 2) * SEG:(j % 2 + 1) * SEG], xt(k, t),
                                 ring[:, n % RING, t * SEG:(t + 1) * SEG], start=(t == 0), stop=(t == KT - 1))
                    ins.then_inc(S("projected"), 1)
                    pe.wait_ge(S("projected"), N_BASE[c] + j + 1)
                    pe.sem_inc(S("slabs_used"), 1)

            def attention(c):
                H = GAT[c]["H"]
                pe.wait_ge(S("terms_ready"), c + 1)
                for h in range(H):
                    ins = mm(TP[:, h * P:(h + 1) * P], al[:, 0, h:h + 1].to_broadcast([P, P]), ident[:],
                             start=True, stop=True)
                ins.then_inc(S("term_rows"), 1)
                pe.wait_ge(S("attn_weights"), c + 1)
                for h in range(H):
                    ins = nc.tensor.transpose(TP[:, h * P:(h + 1) * P], EE[:, h * P:(h + 1) * P], ident[:])
                ins.then_inc(S("attn_turned"), 1)
                pe.wait_ge(S("attn_ready"), c + 1)

            def segments(c):
                f, C = FIRST[c], GAT[c]["C"]
                for i in range(f["segs"] + 2):
                    if i < f["segs"]:
                        s = SEG_BASE[c] + i
                        base = (i % 2) * SEG
                        if i >= 2:
                            pe.wait_ge(S("segment_ready"), s - 1)
                        bias_row(PJ[:, base:base + SEG], f["bias"] + i, 0, SEG, start=True)
                        at = i * SEG
                        while at < (i + 1) * SEG:
                            h = at // C
                            end = min((h + 1) * C, (i + 1) * SEG)
                            ins = mm(PJ[:, base + at - i * SEG:base + end - i * SEG], ALT[:, h * P:(h + 1) * P],
                                     hs1[:, at:end], start=False, stop=(end == (i + 1) * SEG), skip_group_check=True)
                            at = end
                        ins.then_inc(S("segment_product"), 1)
                    if 1 <= i <= f["segs"]:
                        s = SEG_BASE[c] + i - 1
                        pe.wait_ge(S("segment_ready"), s + 1)
                        if i >= 3:
                            pe.wait_ge(S("segmentT_ready"), s - 1)
                        bank = MS if (i - 1) % 2 == 0 else TP
                        for t in range(4):
                            ins = nc.tensor.transpose(bank[:, t * P:(t + 1) * P],
                                                      act1[:, (i - 1) % 2, t * P:(t + 1) * P], ident[:])
                        ins.then_inc(S("segment_turned"), 1)
                    if i >= 2:
                        j = i - 2
                        s, n = SEG_BASE[c] + j, f["w2"] + j
                        pe.wait_ge(S("segmentT_ready"), s + 1)
                        landed(pe, n)
                        for t in range(4):
                            for a, b in halves():
                                ins = mm(AC[:, a:b], act1T[:, j % 2, t * P:(t + 1) * P],
                                         ring[:, n % RING, t * D + a:t * D + b], start=(j == 0 and t == 0),
                                         stop=(j == f["segs"] - 1 and t == 3), skip_group_check=True)
                        ins.then_inc(S("segment_used"), 1)
                        pe.wait_ge(S("segment_used"), s + 1)
                        pe.sem_inc(S("slabs_used"), 1)
                pe.sem_inc(S("projected"), 1)

            def second(c):
                for a, b in halves():
                    bias_row(AC[:, a:b], LAYER2_BIAS[c], a, b, start=True)
                add_whole(X)
                for a, b in halves():
                    ins = mm(AC[:, a:b], ALT[:, 0:P], hs2[:, a:b], start=False, stop=True, skip_group_check=True)
                ins.then_inc(S("x_product"), 1)

            def mixture(l):
                m = MOE[l]
                k = {1: 6, 3: 10}[l]
                turn(k, XN)
                pe.wait_ge(S("tr_ready"), k + 1)
                at = {1: 0, 3: KT * E8}[l]
                for t in range(KT):
                    ins = mm(MS[:, 0:E8], xt(k, t), small[:, at + t * E8:at + (t + 1) * E8], start=(t == 0),
                             stop=(t == KT - 1))
                if l == 1:
                    ins = mm(MS[:, 8:16], ident[0:ROWS, 25:26].to_broadcast([ROWS, P]), rows[:, 0:E8], start=True,
                             stop=True)
                ins.then_inc(S("router_product"), 1)
                for a, b in halves():
                    mm(AC[:, a:b], ident[:], X[:, a:b], start=True, stop=False, skip_group_check=True)
                pe.wait_ge(S("XTl_ready"), {1: 1, 3: 2}[l])

                def up(kind, base, q, it):
                    pe.wait_ge(S("lo_" + kind), it * 2 + (q + 1))
                    for t in range(KT):
                        w = slice(t * SEG, (t + 1) * SEG)
                        dst = PJ[:, base:base + SEG]
                        mm(dst, XTl[:, t, :], wh[kind][:, w], start=(t == 0), stop=False)
                        mm(dst, XTh[:, t, :], wl[kind][:, w], start=False, stop=False)
                        ins = mm(dst, XTh[:, t, :], wh[kind][:, w], start=False, stop=(t == KT - 1))
                    ins.then_inc(S("pe_" + kind), 1)

                def turn_hidden(q, it):
                    pe.wait_ge(S("hidden_ready"), it * 2 + q)
                    for t in range(4):
                        ins = nc.tensor.transpose(TP[:, t * P:(t + 1) * P], hexp[:, t * P:(t + 1) * P], ident[:])
                    ins.then_inc(S("pe_t"), 1)

                def down(q, it, stop=False):
                    pe.wait_ge(S("lo_d"), it * 2 + q)
                    pe.wait_ge(S("hTl_ready"), it * 2 + q)
                    for t in range(4):
                        for x, w in ((hTl, wh["d"]), (hTh, wl["d"]), (hTh, wh["d"])):
                            for a, b in halves():
                                ins = mm(AC[:, a:b], x[:, t, :], w[:, t * D + a:t * D + b], start=False,
                                         stop=stop and t == 3 and x is hTh and w is wh["d"], skip_group_check=True)
                    ins.then_inc(S("pe_d"), 1)

                def chunk(c0, it=0, first=False):
                    q = m["first"] + c0
                    if q:
                        pe.wait_ge(S("silu_ready"), it * 2 + q)
                    up("g", 0, q, it)
                    if not first:
                        turn_hidden(q, it)
                    up("u", SEG, q, it)
                    if not first:
                        down(q, it)

                chunk(0, first=True)
                pairs = (m["chunks"] - 2) // 2
                with pe.Fori(0, pairs) as it:
                    chunk(1, it)
                    chunk(2, it)
                for c in range(1 + 2 * pairs, m["chunks"]):
                    chunk(c)
                q = m["first"] + m["chunks"]
                turn_hidden(q, 0)
                down(q, 0, stop=True)
                pe.wait_ge(S("pe_d"), q)
                pe.sem_inc(S("x_product"), 1)

            pe.wait_ge(S("onehot_ready"), 2)
            for t in range(E_TILES):
                ins = mm(MS[:, 0:P], onehot[:, 1, t, :], onehot[:, 0, t, :], start=(t == 0), stop=(t == E_TILES - 1))
            ins.then_inc(S("counts_product"), 1)
            pe.wait_ge(S("const_ready"), 3)
            turn(0, XN)
            pe.wait_ge(S("counts_product"), 1)
            project(0, 0)
            attention(0)
            pe.wait_ge(S("small_loaded"), 64)
            segments(0)
            attention(1)
            second(1)
            turn(1, XN)
            pe.wait_ge(S("sigmoid_ready"), 1)
            mm(MS[:, 0:P], tk[:, 1:2].to_broadcast([P, P]), ident[:], start=True, stop=True)
            mm(MS[:, P:P + 1], ones[:], tk[:, 1:2], start=True, stop=True).then_inc(S("score_row"), 1)
            pe.wait_ge(S("tr_ready"), 2)
            for w, dst, sem in ((0, TP, "q_product"), (1, PJ, "k_product")):
                for n in range(6 * w // 4, (6 * w + 5) // 4 + 1):
                    landed(pe, FFN0_SLAB + n)
                for t in range(KT):
                    for k in range(KT):
                        ins = mm(dst[:, t * P:(t + 1) * P], w_tile(6 * w + k, t * P, (t + 1) * P), xt(1, k),
                                 start=(k == 0), stop=(k == KT - 1))
                ins.then_inc(S(sem), 1)
                pe.wait_ge(S(sem), 1)
                pe.sem_inc(S("slabs_used"), 1 + w)
            for n in (3, 4):
                landed(pe, FFN0_SLAB + n)
            for a, b in halves():
                bias_row(AC[:, a:b], ROW_BV, a, b, start=True)
                for k in range(KT):
                    ins = mm(AC[:, a:b], xt(1, k), w_tile(12 + k, a, b), start=False, stop=(k == KT - 1),
                             skip_group_check=True)
            ins.then_inc(S("v_product"), 1)
            pe.wait_ge(S("v_product"), 1)
            pe.sem_inc(S("slabs_used"), 1)
            pe.wait_ge(S("q_ready"), KT)
            pe.wait_ge(S("k_ready"), 2 * KT)
            for t in range(KT):
                ins = mm(TP[:, t * 2 * P:(t + 1) * 2 * P], qT[:, t * P:(t + 1) * P],
                         kz[:, t].rearrange("p a n -> p (a n)"), start=True, stop=True)
            ins.then_inc(S("self_logits"), 1)
            pe.wait_ge(S("v_ready"), 1)
            pe.wait_ge(S("pool_weight"), 1)
            for a, b in halves():
                ins = mm(AC[:, a:b], tk[:, 7:8].to_broadcast([P, P]), XN[:, a:b], start=True, stop=True)
            ins.then_inc(S("pooled"), 1)
            pe.wait_ge(S("self_weights"), 1)
            for h in range(HEADS):
                ins = nc.tensor.transpose(TP[:, h * P:(h + 1) * P], EE[:, h * P:(h + 1) * P], ident[:])
            ins.then_inc(S("self_turned"), 1)
            pe.wait_ge(S("self_attn_ready"), 1)
            for h in range(HEADS):
                ins = mm(AC[:, h * DH:(h + 1) * DH], ALT[:, h * P:(h + 1) * P], V[:, h * DH:(h + 1) * DH],
                         start=True, stop=True)
            ins.then_inc(S("context"), 1)
            turn(2, MIX)
            pe.wait_ge(S("tr_ready"), 3)
            for a, b in halves():
                mm(PJ[:, a:b], ident[:], HID[:, a:b], start=True, stop=False, skip_group_check=True)
            landed(pe, FFN0_SLAB + 5)
            for k in range(KT):
                for a, b in halves():
                    mm(PJ[:, a:b], xt(2, k), w_tile(18 + k, a, b), start=False, stop=False, skip_group_check=True)
            turn(3, CTX)
            pe.wait_ge(S("tr_ready"), 4)
            for n in (6, 7):
                landed(pe, FFN0_SLAB + n)
            for k in range(KT):
                for a, b in halves():
                    ins = mm(PJ[:, a:b], xt(3, k), w_tile(24 + k, a, b), start=False, stop=(k == KT - 1),
                             skip_group_check=True)
            ins.then_inc(S("merged"), 1)
            pe.wait_ge(S("merged"), 1)
            pe.sem_inc(S("slabs_used"), 3)
            turn(4, XN)
            pe.wait_ge(S("tr_ready"), 5)
            for k in range(KT):
                ins = mm(MS[0:F0, 0:P], w_tile(30, k * F0, (k + 1) * F0), xt(4, k), start=(k == 0),
                         stop=(k == KT - 1))
            ins.then_inc(S("f_product"), 1)
            for a, b in halves():
                bias_row(AC[:, a:b], ROW_BF2, a, b, start=True)
            add_whole(X)
            add_whole(H1)
            pe.wait_ge(S("f_ready"), 1)
            for a, b in halves():
                ins = mm(AC[:, a:b], FT[0:F0, :], w_tile(31, a, b)[0:F0], start=False, stop=True,
                         skip_group_check=True)
            ins.then_inc(S("x_product"), 1)
            pe.wait_ge(S("x_product"), 2)
            pe.sem_inc(S("slabs_used"), 1)
            turn(5, XN)
            project(2, 5)
            attention(2)
            segments(2)
            attention(3)
            second(3)
            mixture(1)
            turn(7, XN)
            pe.wait_ge(S("tr_ready"), 8)
            at = 2 * KT * E8
            for t in range(KT):
                ins = mm(AC[:, t * P:(t + 1) * P], xt(7, t), small[:, at:at + P], start=True, stop=True)
            ins.then_inc(S("projected"), 1)
            attention(4)
            for t in range(KT):
                mm(AC[:, t * P:(t + 1) * P], xt(7, t), small[:, at + P:at + 2 * P], start=True, stop=False,
                   skip_group_check=True)
                for h in (2 * t, 2 * t + 1):
                    ins = mm(AC[:, h * 64:(h + 1) * 64], ALT[:, h * P:(h + 1) * P], hs2[:, h * 64:(h + 1) * 64],
                             start=False, stop=(h % 2 == 1), skip_group_check=True)
            ins.then_inc(S("x_product"), 1)
            turn(8, XN)
            pe.wait_ge(S("tr_ready"), 9)
            n = L2_SLAB
            landed(pe, n)
            bias_row(MS[:, 0:E8], ROW_L2BG, 0, E8, start=True)
            for k in range(KT):
                ins = mm(MS[:, 0:E8], xt(8, k), ring[:, n % RING, 2304 + k * E8:2304 + (k + 1) * E8], start=False,
                         stop=(k == KT - 1), skip_group_check=True)
            ins.then_inc(S("l2_gate_product"), 1)
            bias_row(PJ[:, 0:384], ROW_L2B1, 0, 384, start=True)
            for k in range(KT):
                ins = mm(PJ[:, 0:384], xt(8, k), ring[:, n % RING, k * 384:(k + 1) * 384], start=False,
                         stop=(k == KT - 1), skip_group_check=True)
            ins.then_inc(S("l2_hidden_product"), 1)
            pe.wait_ge(S("l2_hidden_product"), 1)
            pe.sem_inc(S("slabs_used"), 1)
            pe.wait_ge(S("l2_weighted"), 1)
            for t in range(3):
                nc.tensor.transpose(TP[:, t * P:(t + 1) * P], G2[:, t * P:(t + 1) * P], ident[:])
            nc.tensor.transpose(TP[0:E8, SEG:SEG + P], r8[:, 5, :], ident[:]).then_inc(S("l2_turned"), 1)
            n = L2_SLAB + 1
            landed(pe, n)
            for a, b in halves():
                mm(AC[:, a:b], ident[:], X[:, a:b], start=True, stop=False, skip_group_check=True)
            pe.wait_ge(S("l2_T_ready"), 2)
            for a, b in halves():
                mm(AC[:, a:b], CBT[0:E8, :], b2m[:, a:b], start=False, stop=False, skip_group_check=True)
                for t in range(3):
                    ins = mm(AC[:, a:b], G2T[:, t * P:(t + 1) * P], ring[:, n % RING, t * D + a:t * D + b],
                             start=False, stop=(t == 2), skip_group_check=True)
            ins.then_inc(S("x_product"), 1)
            pe.wait_ge(S("x_product"), 6)
            pe.sem_inc(S("slabs_used"), 1)
            turn(9, XN)
            project(5, 9)
            attention(5)
            segments(5)
            attention(6)
            second(6)
            mixture(3)


def _k_tiles(w):
    k, n = w.shape
    return w.reshape(k // 128, 128, n).transpose(1, 0, 2)


def kernel(**inputs):
    import numpy as np
    import concourse.bacc as bacc
    from concourse.bass_utils import run_bass_kernel_spmd

    i = {k: np.asarray(v) for k, v in inputs.items()}
    f32 = np.float32
    stream = np.zeros((N_SLABS, P, SLAB), f32)

    def by_columns(n, w):
        for j in range(w.shape[1] // SEG):
            stream[n + j] = _k_tiles(w[:, j * SEG:(j + 1) * SEG]).reshape(P, SLAB)

    def by_rows(n, w):
        for j in range(w.shape[0] // SEG):
            stream[n + j] = _k_tiles(w[j * SEG:(j + 1) * SEG]).reshape(P, SLAB)

    by_columns(0, i["L0_gnn_W1"])
    by_rows(12, i["L0_gnn_W2"])
    tiles = np.zeros((P, 32, D), f32)
    for j, name in enumerate(("Wq", "Wk", "Wv", "Wm", "Wo")):
        tiles[:, 6 * j:6 * j + 6] = _k_tiles(i["L0_ffn_" + name])
    tiles[:, 30, 0:KT * F0] = _k_tiles(i["L0_ffn_W1"]).reshape(P, KT * F0)
    tiles[0:F0, 31] = i["L0_ffn_W2"]
    stream[FFN0_SLAB:FFN0_SLAB + 8] = tiles.reshape(P, 8, SLAB).transpose(1, 0, 2)
    by_columns(32, i["L1_gnn_W1"].T)
    by_rows(34, i["L1_gnn_W2"].T)

    def experts(l, e, gate, up, down):
        m = MOE[l]
        for j in range(m["per"]):
            n = m["slab"] + 3 * (e * m["per"] + j)
            f = slice(j * SEG, (j + 1) * SEG)
            by_columns(n, gate[f].T)
            by_columns(n + 1, up[f].T)
            by_rows(n + 2, down[:, f].T)

    for e in range(E8):
        experts(1, e, i["L1_ffn_Wg"][e], i["L1_ffn_Wu"][e], i["L1_ffn_Wd"][e])
        experts(3, e, i["L3_ffn_Wg"][e], i["L3_ffn_Wu"][e], i["L3_ffn_Wd"][e])
    experts(1, E8, i["L1_ffn_sg"], i["L1_ffn_su"], i["L1_ffn_sd"])
    stream[L2_SLAB, :, 0:2304] = _k_tiles(i["L2_ffn_W1"].transpose(1, 0, 2).reshape(D, E8 * F2)).reshape(P, 2304)
    stream[L2_SLAB, :, 2304:2304 + KT * E8] = _k_tiles(i["L2_ffn_Wg"]).reshape(P, KT * E8)
    stream[L2_SLAB + 1, :, 0:2304] = _k_tiles(i["L2_ffn_W2"].reshape(E8 * F2, D)).reshape(P, 2304)
    by_columns(119, i["L3_gnn_W1"])
    by_rows(123, i["L3_gnn_W2"])

    rows = np.zeros((ROWS, D), f32)
    rows[0:12, 0:SEG] = i["L0_gnn_b1"].reshape(12, SEG)
    rows[12:14, 0:SEG] = i["L1_gnn_b1"].reshape(2, SEG)
    rows[14:18, 0:SEG] = i["L3_gnn_b1"].reshape(4, SEG)
    for r, name in ((18, "L0_gnn_b2"), (19, "L1_gnn_b2"), (20, "L3_gnn_b2"), (ROW_BV, "L0_ffn_bv"),
                    (ROW_BF2, "L0_ffn_bf2")):
        rows[r] = i[name]
    rows[ROW_L2B1, 0:384] = i["L2_ffn_b1"].reshape(384)
    rows[ROW_L2BG, 0:E8] = i["L2_ffn_bg"]
    rows[25, 0:E8] = i["L1_ffn_expert_bias"]

    cols = np.zeros((P, 16), f32)
    cols[:, 0:6] = i["L0_ffn_bq"].reshape(KT, P).T
    cols[:, 6:12] = i["L0_ffn_bk"].reshape(KT, P).T
    cols[0:F0, 12] = i["L0_ffn_bf1"]

    small = np.zeros((P, 2 * KT * E8 + 2 * P), f32)
    small[:, 0:48] = _k_tiles(i["L1_ffn_w_router"].T).reshape(P, 48)
    small[:, 48:96] = _k_tiles(i["L3_ffn_router_w"].T).reshape(P, 48)
    for j, name in enumerate(("L2_gnn_W", "L2_gnn_W_res")):
        for a in range(2):
            small[64 * a:64 * a + 64, 96 + P * j + 64 * a:96 + P * j + 64 * a + 64] = i[name].T

    attn = [i["L0_gnn_" + n][h] for h in range(8) for n in ("a_src1", "a_dst1")]
    for a, b in (("L0_gnn_a_src2", "L0_gnn_a_dst2"), ("L1_gnn_att_src1", "L1_gnn_att_dst1"),
                 ("L1_gnn_att_src2", "L1_gnn_att_dst2"), ("L2_gnn_attn_l", "L2_gnn_attn_r"),
                 ("L3_gnn_att_src1", "L3_gnn_att_dst1"), ("L3_gnn_att_src2", "L3_gnn_att_dst2")):
        attn += [i[a].reshape(-1), i[b].reshape(-1)]
    attn = np.concatenate(attn)[None, :]
    vectors = np.concatenate([i["L0_ffn_" + n].reshape(-1)
                              for n in ("g1", "b1", "Wr", "g2", "b2", "bo", "bm", "br")])[None, :]
    edges = np.concatenate([i["src"].reshape(P, E_TILES), i["dst"].reshape(P, E_TILES)], axis=1)

    nc = bacc.Bacc("TRN2", target_bir_lowering=False, num_devices=1)
    arrays = {}

    def given(name, a):
        arrays["in_" + name] = np.ascontiguousarray(a)
        return nc.dram_tensor("in_" + name, a.shape, mybir.dt.from_np(a.dtype), kind="ExternalInput").ap()

    out = nc.dram_tensor("out", (P, D), F32, kind="ExternalOutput").ap()
    gnn_ffn_kernel(nc, given("x", i["x"]), given("edges", edges), given("weights", stream), given("rows", rows),
                   given("cols", cols), given("small", small), given("attn", attn),
                   given("ffn0_vectors", vectors), given("l2_b2", i["L2_ffn_b2"]), out)
    result = run_bass_kernel_spmd(nc, [arrays], core_ids=[0])
    return result.results[0]["out"]
```

```python
from contextlib import ExitStack

import concourse.bass as bass
from concourse import mybir

ALU = mybir.AluOpType
ACT = mybir.ActivationFunctionType
AX_X = mybir.AxisListType.X
F32 = mybir.dt.float32
F32R = mybir.dt.float32r
BF16 = mybir.dt.bfloat16
I32 = mybir.dt.int32

P = 128
D = 768
KT = D // P
E_TILES = 16
SLAB = 3072
SEG = 512
RING = 6
LN_EPS = 1e-5
SLOPE = 0.2
NOT_AN_EDGE = 1e30
ROUTED = 19
HEADS = 12
DH = D // HEADS
F0 = 48
E8 = 8
F2 = 48

GAT = [
    dict(H=8, C=768, group=2, loops=False, unit=0),
    dict(H=1, C=768, group=1, loops=False, unit=8),
    dict(H=8, C=128, group=4, loops=False, unit=9),
    dict(H=1, C=768, group=1, loops=False, unit=11),
    dict(H=12, C=64, group=4, loops=False, unit=12),
    dict(H=4, C=512, group=1, loops=True, unit=13),
    dict(H=1, C=768, group=1, loops=True, unit=17),
]
UNIT = [1536] * 9 + [1024] * 2 + [1536] * 2 + [1024] * 4 + [1536]
FIRST = {
    0: dict(slab=0, segs=12, per=3, bias=0, elu=True),
    2: dict(slab=32, segs=2, per=1, bias=12, elu=False),
    5: dict(slab=119, segs=4, per=1, bias=14, elu=True),
}
LAYER2_BIAS = {1: 18, 3: 19, 6: 20}
ROW_BV, ROW_BF2, ROW_MIXED, ROW_B2 = 21, 22, 23, 24
MIXED_BG, MIXED_EB = 384, 392
ROWS = 32
FFN0_SLAB = 24
L2_SLAB = 117
N_SLABS = 271
MOE = {
    1: dict(slab=36, chunks=27, per=3, first=0),
    3: dict(slab=127, chunks=48, per=6, first=27),
}
SEG_BASE = {0: 0, 2: 12, 5: 14}
GROUP_BASE = [0, 4, 5, 7, 8, 11, 15]


def w1_slab(c, j):
    f = FIRST[c]
    if f["per"] == 1:
        return f["slab"] + j
    return f["slab"] + j + max(j // f["per"] - 1, 0) * f["per"]


def w2_slab(c, j):
    f = FIRST[c]
    if f["per"] == 1:
        return f["slab"] + f["segs"] + j
    return f["slab"] + j + min((j // f["per"] + 2) * f["per"], f["segs"])


def when_used(n):
    for m in MOE.values():
        if m["slab"] <= n < m["slab"] + 3 * m["chunks"]:
            k = n - m["slab"]
            return "lo_" + "gud"[k % 3], m["first"] + k // 3 + 1
    for c, f in FIRST.items():
        for j in range(f["segs"]):
            if n == w1_slab(c, j):
                return "projected", SEG_BASE[c] + j + 1
            if n == w2_slab(c, j):
                return "segment_used", SEG_BASE[c] + j + 1
    return {24: ("q_product", 1), 25: ("k_product", 1), 26: ("k_product", 1), 27: ("v_product", 1),
            28: ("merged", 1), 29: ("merged", 1), 30: ("merged", 1), 31: ("x_product", 2),
            117: ("l2_hidden_product", 1), 118: ("x_product", 5)}[n]


def gnn_ffn_kernel(nc, x_in, edges_in, weights, rows_in, cols_in, small_in, attn_in, ffn0_vectors, out):
    with ExitStack() as ctx:
        def sb(name, shape, dt=F32):
            return ctx.enter_context(nc.sbuf_tensor(name, shape, dt))

        def psum(name, shape, dt=F32):
            return ctx.enter_context(nc.psum_tensor(name, shape, dt))

        sems = {}

        def S(name):
            if name not in sems:
                sems[name] = ctx.enter_context(nc.semaphore(name))
            return sems[name]

        ring = sb("ring", [P, RING, SLAB])
        X = sb("X", [P, D])
        XN = sb("XN", [P, D])
        HID = sb("HID", [P, D])
        H1 = sb("H1", [P, D])
        XT = sb("XT", [P, KT, P])
        ident = sb("ident", [P, P])
        ones = sb("ones", [P, P])
        below = sb("below", [P, P])
        tie8 = sb("tie8", [P, E8, E8])
        counts = sb("counts", [P, 2, P])
        maskb = sb("maskb", [P, 2, P])
        rows = sb("rows", [ROWS, D])
        cols = sb("cols", [P, 16])
        small = sb("small", [P, 2 * KT * E8 + 2 * P])
        stats = sb("stats", [P, 2, 6])
        mv = sb("mv", [P, 2])
        veps = sb("veps", [P, 1])
        rstd = sb("rstd", [P, 1])
        power = sb("power", [P, 1])
        al = sb("al", [P, 2, HEADS])
        hmax = sb("hmax", [P, HEADS])
        hneg = sb("hneg", [P, HEADS])
        hsum = sb("hsum", [P, HEADS])
        hrec = sb("hrec", [P, HEADS])
        tk = sb("tk", [P, 8])
        r8 = sb("r8", [P, 8, E8])
        comb32 = sb("comb32", [P, ROWS])
        g64 = sb("g64", [P, 2, E8, E8])
        CB = sb("CB", [P, 48])
        low = sb("low", [P, 2, SEG])
        act1 = sb("act1", [P, 2, SEG])
        act1T = sb("act1T", [P, 2, SEG])
        silu = low[:, 0, :]
        hexp = act1[:, 0, :]
        XTh = sb("XTh", [P, KT, P], F32R)
        XTl = sb("XTl", [P, KT, P], F32R)
        hTh = sb("hTh", [P, 4, P], F32R)
        hTl = sb("hTl", [P, 4, P], F32R)
        AB = sb("AB", [P, 2, 1536])
        hs2 = sb("hs2", [P, D])

        junk = H1[:]

        with nc.sbuf_tensor("scratch", [P, 6 * SLAB], F32) as scratch:
            pass
        wh, wl = {}, {}
        for kind in "dgu":
            wh[kind] = sb(f"w_hi_{kind}", [P, SLAB], F32R)
            wl[kind] = sb(f"w_lo_{kind}", [P, SLAB], F32R)
        hs1 = scratch[:, 0:3072]
        EE = scratch[:, 3072:4608]
        ALT = scratch[:, 4608:6144]
        ids_i = scratch[:, 6144:6176].bitcast(I32)
        ids_f = scratch[:, 6176:6208]
        iota_i = scratch[:, 6208:6336].bitcast(I32)
        iota_f = scratch[:, 6336:6464]
        onehot = scratch[:, 6464:8512].bitcast(BF16).rearrange("p (a t n) -> p a t n", a=2, t=E_TILES)
        NV = 7
        vec0 = scratch[:, 6144:6144 + NV * D + 1]
        kz = scratch[:, 11524:13060].rearrange("p (t a n) -> p t a n", t=KT, a=2)
        qT = scratch[:, 13060:13828]
        V = scratch[:, 13828:14596]
        MIX = scratch[:, 14596:15364]
        CTX = scratch[:, 15364:16132]
        BH = scratch[:, 16132:16900]
        FT = scratch[:, 16900:17028]
        XH = scratch[:, 17028:17796]
        G2 = scratch[:, 0:384]
        G2T = scratch[:, 384:768]
        CBT = scratch[:, 768:896]

        def vec(i):
            return vec0[:, i * D:(i + 1) * D]

        PJ = psum("PJ", [P, 2 * SEG])
        TP = psum("TP", [P, 3 * SEG])
        MS = psum("MS", [P, SEG])
        AC = psum("AC", [P, 2 * SEG])

        land = [S(f"slab_landed_{i}") for i in range(RING)]

        def landed(eng, n):
            eng.wait_ge(land[n % RING], 16 * (n // RING + 1))

        def halves():
            return ((0, SEG), (SEG, D))

        def group(c, g):
            k = GAT[c]["group"]
            n = min(k, GAT[c]["H"] - g * k)
            at = (g % 3) * SEG
            return GROUP_BASE[c] + g, n, slice(at, at + n * P)

        def unit_of(c, g):
            if c == 0:
                return 2 * g + 1
            return GAT[c]["unit"] + (0 if c == 4 else g)

        def ring_seg(j):
            return slice((j % RING) * SEG, (j % RING + 1) * SEG)

        def bank(j):
            return PJ[:, (j % 2) * SEG:(j % 2 + 1) * SEG]

        def w_tile(t, c0, c1):
            n = FFN0_SLAB + t // 4
            return ring[:, n % RING, (t % 4) * D + c0:(t % 4) * D + c1]

        block = ctx.enter_context(nc.Block())

        @block.sync
        def _(sp):
            sp.dma_start(X[:], x_in).then_inc(S("x_loaded"), 16)

            def slab(n, index):
                sp.dma_start(ring[:, n % RING, :], weights[index]).then_inc(land[n % RING], 16)

            def single(n):
                if n >= RING:
                    name, value = when_used(n - RING)
                    sp.wait_ge(S(name), value)
                slab(n, n)

            for n in range(42):
                single(n)
            with sp.Fori(0, 12) as it:
                for j in range(6):
                    sp.wait_ge(S("lo_" + "gud"[j % 3]), it * 2 + (1 + j // 3))
                    slab(42 + j, it * 6 + (42 + j))
            for n in range(114, 133):
                single(n)
            with sp.Fori(0, 23) as it:
                for j in range(6):
                    sp.wait_ge(S("lo_" + "gud"[j % 3]), it * 2 + (MOE[3]["first"] + 1 + j // 3))
                    slab(133 + j, it * 6 + (133 + j))
            sp.wait_ge(S("x_ready"), 8)
            sp.dma_start(out, X[:]).then_inc(S("out_stored"), 16)
            sp.wait_ge(S("out_stored"), 16)

        @block.gpsimd
        def _(pool):
            pool.dma_start(ids_i, edges_in).then_inc(S("edges_loaded"), 16)
            nc.gpsimd.memset(power[:], -0.5).then_inc(S("const_filled"), 1)
            nc.gpsimd.memset(ident[:], 0.0).then_inc(S("const_filled"), 1)
            nc.gpsimd.memset(ones[:], 1.0).then_inc(S("const_filled"), 1)
            nc.gpsimd.memset(below[:], 1.0).then_inc(S("const_filled"), 1)
            nc.gpsimd.memset(tie8[:], 1.0).then_inc(S("const_filled"), 1)
            pool.wait_ge(S("const_filled"), 5)
            nc.gpsimd.affine_select(out=ident[:], in_=ident[:], compare_op=ALU.not_equal, fill=1.0, base=0,
                                    pattern=[[-1, P]], channel_multiplier=1).then_inc(S("const_ready"), 1)
            nc.gpsimd.iota(iota_i, pattern=[[1, P]], base=0, channel_multiplier=0).then_inc(S("iota_made"), 1)
            nc.gpsimd.affine_select(out=below[:], in_=below[:], compare_op=ALU.is_gt, fill=0.0, base=0,
                                    pattern=[[-1, P]], channel_multiplier=1).then_inc(S("const_ready"), 1)
            nc.gpsimd.affine_select(out=tie8[:], in_=tie8[:], compare_op=ALU.is_gt, fill=0.0, base=0,
                                    pattern=[[1, E8], [-1, E8]], channel_multiplier=0).then_inc(S("const_ready"), 1)

            def ln_power(i):
                pool.wait_ge(S("ln_variance"), i + 1)
                nc.gpsimd.tensor_tensor(rstd[:], veps[:], power[:], ALU.pow).then_inc(S("ln_rstd"), 1)

            def vectors(u):
                if u >= 2:
                    pool.wait_ge(S("vectors_used"), u - 1)
                at = sum(UNIT[:u])
                pool.dma_start(AB[:, u % 2, 0:UNIT[u]], attn_in[:, at:at + UNIT[u]].to_broadcast([P, UNIT[u]])) \
                    .then_inc(S(f"vectors_loaded_{u % 2}"), 16)

            ln_power(0)
            vectors(0)
            vectors(1)
            pool.dma_start(rows[:], rows_in).then_inc(S("small_loaded"), 16)
            pool.dma_start(cols[:], cols_in).then_inc(S("small_loaded"), 16)
            pool.dma_start(small[:], small_in).then_inc(S("small_loaded"), 16)
            nc.gpsimd.memset(kz, 0.0).then_inc(S("k_zeroed"), 1)
            for u in range(2, 5):
                vectors(u)
            pool.wait_ge(S("counts_product"), 1)
            pool.dma_start(vec0, ffn0_vectors.to_broadcast([P, NV * D + 1])).then_inc(S("ffn0_vectors_loaded"), 16)
            for u in range(5, 11):
                vectors(u)
            for i in range(1, 5):
                ln_power(i)
            for u in range(11, 14):
                vectors(u)
            ln_power(5)
            ln_power(6)
            vectors(14)
            ln_power(7)
            ln_power(8)
            for u in range(15, 18):
                vectors(u)
            ln_power(9)

        @block.scalar
        def _(act):
            A = nc.scalar.activation

            def transposed(k):
                act.wait_ge(S("tr_product"), k + 1)
                A(XT[:].rearrange("p k n -> p (k n)"), TP[:, 0:D], ACT.Copy).then_inc(S("tr_ready"), 1)

            def copy_h(c, j):
                act.wait_ge(S("projected"), SEG_BASE[c] + j + 1)
                A(hs1[:, ring_seg(j)], bank(j), ACT.Copy).then_inc(S("h_copied"), 1)

            def copy_h2():
                A(hs2[:], AC[:, 0:D], ACT.Copy).then_inc(S("h2_copied"), 1)

            def exps(c, g):
                gb, k, at = group(c, g)
                act.wait_ge(S("logits_ready"), gb + 1)
                for i in range(k):
                    e = EE[:, at.start + i * P:at.start + (i + 1) * P]
                    h = g * GAT[c]["group"] + i
                    ins = A(e, e, ACT.Exp, bias=hneg[:, h:h + 1])
                ins.then_inc(S("exps_ready"), 1)

            def turned(c, g):
                gb, k, at = group(c, g)
                act.wait_ge(S("attn_turned"), gb + 1)
                A(ALT[:, at], TP[:, 2 * SEG:2 * SEG + k * P], ACT.Copy).then_inc(S("attn_ready"), 1)

            def low_exp(c, i):
                if FIRST[c]["elu"]:
                    act.wait_ge(S("low_ready"), {0: 0, 5: 12}[c] + i + 1)
                    A(low[:, i % 2, :], low[:, i % 2, :], ACT.Exp).then_inc(S("low_exp"), 1)

            def segment_turned(c, i):
                s = SEG_BASE[c] + i
                act.wait_ge(S("segment_turned"), s + 1)
                if i >= 2:
                    act.wait_ge(S("segment_used"), s - 1)
                src = MS[:] if i % 2 == 0 else TP[:, 0:SEG]
                A(act1T[:, i % 2, :], src, ACT.Copy).then_inc(S("segmentT_ready"), 1)

            def first_wide(c):
                per = FIRST[c]["per"]
                groups = FIRST[c]["segs"] // per
                for g in range(groups + 1):
                    if g < groups:
                        copy_h(c, g * per)
                    if g:
                        exps(c, g - 1)
                    if g < groups:
                        for j in range(1, per):
                            copy_h(c, g * per + j)
                    if g:
                        turned(c, g - 1)
                        for i in range(per + 1):
                            if i < per:
                                low_exp(c, (g - 1) * per + i)
                            if i:
                                segment_turned(c, (g - 1) * per + i - 1)

            def first_narrow(c):
                n = FIRST[c]["segs"]
                for t in range(n + 3):
                    if t < n:
                        copy_h(c, t)
                    if 0 <= t - 3:
                        segment_turned(c, t - 3)
                    if 0 <= t - 2 < n:
                        turned(c, t - 2)
                    if 0 <= t - 1 < n:
                        exps(c, t - 1)
                    if 0 <= t - 2 < n:
                        low_exp(c, t - 2)

            def second(c):
                first = c - 1
                act.wait_ge(S("segment_used"), SEG_BASE[first] + FIRST[first]["segs"])
                copy_h2()
                exps(c, 0)
                turned(c, 0)

            def hi(l, kind, c0, it, dst=None):
                m = MOE[l]
                n = m["slab"] + 3 * c0 + "gud".index(kind)
                act.wait_ge(land[n % RING], it * 16 + 16 * (n // RING + 1))
                if dst:
                    act.wait_ge(S("pe_" + dst), it * 2 + (m["first"] + c0 + 1))
                elif m["first"] + c0:
                    act.wait_ge(S("pe_" + kind), it * 2 + (m["first"] + c0))
                    if c0 == 0:
                        act.wait_ge(S("pe_d"), m["first"])
                A(wh[dst or kind][:], ring[:, n % RING, :], ACT.Copy).then_inc(S("hi_" + kind), 1)

            def mixture(l):
                m = MOE[l]
                k = {1: 6, 3: 10}[l]

                def chunk(c0, it=0, first=False, last=False):
                    q = m["first"] + c0
                    act.wait_ge(S("pe_g"), it * 2 + (q + 1))
                    if q:
                        act.wait_ge(S("hidden_ready"), it * 2 + q)
                    A(silu, PJ[:, 0:SEG], ACT.Silu).then_inc(S("silu_ready"), 1)
                    if not first:
                        act.wait_ge(S("pe_t"), it * 2 + q)
                        A(hTh[:].rearrange("p k n -> p (k n)"), TP[:, 0:SEG], ACT.Copy).then_inc(S("hTh_ready"), 1)
                    if last:
                        hi(l, "d", c0, it, dst="g")
                    else:
                        hi(l, "g", c0 + 1, it)
                        hi(l, "u", c0 + 1, it)
                        hi(l, "d", c0, it)

                hi(l, "g", 0, 0)
                transposed(k)
                act.wait_ge(S("tr_ready"), k + 1)
                A(XTh[:], XT[:], ACT.Copy).then_inc(S("XTh_ready"), 1)
                hi(l, "u", 0, 0)
                act.wait_ge(S("router_shifted"), {1: 1, 3: 2}[l])
                A(r8[:, 1, :], r8[:, 0, :], ACT.Exp).then_inc(S("router_exp"), 1)
                chunk(0, first=True)
                pairs = (m["chunks"] - 2) // 2
                with act.Fori(0, pairs) as it:
                    chunk(1, it)
                    chunk(2, it)
                for c in range(1 + 2 * pairs, m["chunks"]):
                    chunk(c, last=(c == m["chunks"] - 1))
                act.wait_ge(S("pe_t"), m["first"] + m["chunks"])
                A(hTh[:].rearrange("p k n -> p (k n)"), TP[:, 0:SEG], ACT.Copy).then_inc(S("hTh_ready"), 1)

            transposed(0)
            first_wide(0)
            second(1)
            transposed(1)
            act.wait_ge(S("router0_logit"), 1)
            A(tk[:, 1:2], tk[:, 0:1], ACT.Sigmoid, bias=vec0[:, NV * D:NV * D + 1]).then_inc(S("sigmoid_ready"), 1)
            act.wait_ge(S("small_loaded"), 48)
            act.wait_ge(S("q_product"), 1)
            for t in range(KT):
                ins = A(qT[:, t * P:(t + 1) * P], TP[:, t * P:(t + 1) * P], ACT.Identity, bias=cols[:, t:t + 1])
            ins.then_inc(S("q_ready"), 1)
            act.wait_ge(S("self_max"), 1)
            for h in range(HEADS):
                ins = A(EE[:, h * P:(h + 1) * P], TP[:, h * P:(h + 1) * P], ACT.Exp, bias=hneg[:, h:h + 1],
                        scale=DH ** -0.5, accum_out=hsum[:, h:h + 1])
            ins.then_inc(S("self_exps"), 1)
            act.wait_ge(S("v_product"), 1)
            A(V, AC[:, 0:D], ACT.Copy).then_inc(S("v_ready"), 1)
            transposed(2)
            act.wait_ge(S("self_turned"), 1)
            A(ALT[:, 0:HEADS * P], TP[:, 0:HEADS * P], ACT.Copy).then_inc(S("self_attn_ready"), 1)
            transposed(3)
            transposed(4)
            act.wait_ge(S("f_product"), 1)
            A(FT[0:F0, :], MS[0:F0, 0:P], ACT.Gelu, bias=cols[0:F0, 12:13]).then_inc(S("f_ready"), 1)
            transposed(5)
            first_narrow(2)
            second(3)
            mixture(1)
            transposed(7)
            act.wait_ge(S("l2_h_product"), 1)
            copy_h2()
            exps(4, 0)
            for g in range(3):
                if g < 2:
                    exps(4, g + 1)
                turned(4, g)
            transposed(8)
            act.wait_ge(S("l2_hidden_product"), 1)
            A(G2, PJ[:, 0:E8 * F2], ACT.Gelu).then_inc(S("l2_gelu"), 1)
            act.wait_ge(S("l2_turned"), 1)
            A(G2T, TP[:, 0:384], ACT.Copy).then_inc(S("l2_T_ready"), 1)
            A(CBT[0:ROWS, :], TP[0:ROWS, SEG:SEG + P], ACT.Copy).then_inc(S("l2_T_ready"), 1)
            transposed(9)
            first_narrow(5)
            second(6)
            mixture(3)

        @block.vector
        def _(dve):
            v = nc.vector
            step = [0]

            def then(ins):
                step[0] += 1
                ins.then_inc(S("vector_step"), 1)
                dve.wait_ge(S("vector_step"), step[0])

            def layernorm(i, src, dst, sem=None, count=0):
                v.bn_stats(stats[:, 0, :], src[:, 0:384])
                then(v.bn_stats(stats[:, 1, :], src[:, 384:768]))
                then(v.bn_aggr(mv[:], stats[:]))
                v.tensor_scalar(veps[:], mv[:, 1:2], LN_EPS, None, ALU.add).then_inc(S("ln_variance"), 1)
                dve.wait_ge(S("ln_rstd"), i + 1)
                last = v.tensor_scalar(dst, src, mv[:, 0:1], rstd[:], ALU.subtract, ALU.mult)
                if sem is None:
                    then(last)
                else:
                    last.then_inc(S(sem), 1)
                    dve.wait_ge(S(sem), count)

            def terms(u, heads, C, src):
                dve.wait_ge(S(f"vectors_loaded_{u % 2}"), 16 * (u // 2 + 1))
                k = len(heads)
                for side in range(2):
                    for i, h in enumerate(heads):
                        ins = v.tensor_tensor_reduce(out=junk[:, i * C:(i + 1) * C], in0=src[:, i * C:(i + 1) * C],
                                                     in1=AB[:, u % 2, (side * k + i) * C:(side * k + i + 1) * C],
                                                     scale=1.0, scalar=0.0, op0=ALU.mult, op1=ALU.add,
                                                     accum_out=al[:, side, h:h + 1])
                    if side == 0:
                        then(ins)
                ins.then_inc(S("vectors_used"), 1)
                dve.wait_ge(S("vectors_used"), u + 1)

            def logits(c, g):
                gb, k, at = group(c, g)
                h0 = g * GAT[c]["group"]
                mask = maskb[:, int(GAT[c]["loops"]), :]
                e3 = EE[:, at].rearrange("p (h s) -> p h s", h=k)
                r3 = TP[:, SEG:SEG + k * P].rearrange("p (h s) -> p h s", h=k)
                dve.wait_ge(S("term_rows"), gb + 1)
                then(v.tensor_tensor(e3, r3, al[:, 1, h0:h0 + k].unsqueeze(2).to_broadcast([P, k, P]), ALU.add))
                then(v.scalar_tensor_tensor(EE[:, at], EE[:, at], SLOPE, EE[:, at], ALU.mult, ALU.max))
                for i in range(k):
                    ins = v.tensor_tensor_reduce(out=e3[:, i, :], in0=e3[:, i, :], in1=mask, scale=1.0,
                                                 scalar=-3.0e38, op0=ALU.add, op1=ALU.max,
                                                 accum_out=hmax[:, h0 + i:h0 + i + 1])
                then(ins)
                v.tensor_scalar(hneg[:, h0:h0 + k], hmax[:, h0:h0 + k], -1.0, None, ALU.mult) \
                    .then_inc(S("logits_ready"), 1)

            def weights_of(c, g):
                gb, k, at = group(c, g)
                h0 = g * GAT[c]["group"]
                e3 = EE[:, at].rearrange("p (h s) -> p h s", h=k)
                dve.wait_ge(S("exps_ready"), gb + 1)
                for i in range(k):
                    ins = v.tensor_tensor_reduce(out=e3[:, i, :], in0=e3[:, i, :],
                                                 in1=counts[:, int(GAT[c]["loops"]), :], scale=1.0, scalar=0.0,
                                                 op0=ALU.mult, op1=ALU.add, accum_out=hsum[:, h0 + i:h0 + i + 1])
                then(ins)
                then(v.tensor_scalar(hsum[:, h0:h0 + k], hsum[:, h0:h0 + k], 1e-16, None,
                                     ALU.max if c == 4 else ALU.add))
                then(v.reciprocal(hrec[:, h0:h0 + k], hsum[:, h0:h0 + k]))
                v.tensor_tensor(e3, e3, hrec[:, h0:h0 + k].unsqueeze(2).to_broadcast([P, k, P]), ALU.mult) \
                    .then_inc(S("attn_weights"), 1)

            def activate(c, i):
                s = SEG_BASE[c] + i
                z = bank(i)
                dve.wait_ge(S("segment_product"), s + 1)
                if i >= 2:
                    dve.wait_ge(S("segment_turned"), s - 1)
                if FIRST[c]["elu"]:
                    v.tensor_scalar(low[:, i % 2, :], z, 0.0, None, ALU.min).then_inc(S("low_ready"), 1)
                    dve.wait_ge(S("low_exp"), {0: 0, 5: 12}[c] + i + 1)
                    v.scalar_tensor_tensor(act1[:, i % 2, :], low[:, i % 2, :], -1.0, z, ALU.add, ALU.max) \
                        .then_inc(S("segment_ready"), 1)
                else:
                    v.tensor_scalar(act1[:, i % 2, :], z, 0.0, None, ALU.max).then_inc(S("segment_ready"), 1)

            def first_wide(c):
                per, C = FIRST[c]["per"], GAT[c]["C"]
                groups = FIRST[c]["segs"] // per
                for g in range(groups + 1):
                    if g:
                        logits(c, g - 1)
                        weights_of(c, g - 1)
                    if g < groups:
                        for h in (2 * g, 2 * g + 1):
                            dve.wait_ge(S("h_copied"), SEG_BASE[c] + ((h + 1) * C + SEG - 1) // SEG)
                            at = h * C % (RING * SEG)
                            terms(h, [h], C, hs1[:, at:at + C])
                    if g:
                        for i in range(per):
                            activate(c, (g - 1) * per + i)

            def first_narrow(c):
                n, k, C = FIRST[c]["segs"], GAT[c]["group"], GAT[c]["C"]
                for t in range(n + 2):
                    if 0 <= t - 1 < n:
                        logits(c, t - 1)
                    if t < n:
                        dve.wait_ge(S("h_copied"), SEG_BASE[c] + t + 1)
                        terms(GAT[c]["unit"] + t, range(t * k, t * k + k), C, hs1[:, ring_seg(t)])
                    if 0 <= t - 1 < n:
                        weights_of(c, t - 1)
                    if 0 <= t - 2:
                        activate(c, t - 2)

            def second(c, n):
                dve.wait_ge(S("h2_copied"), n)
                terms(GAT[c]["unit"], [0], D, hs2)
                logits(c, 0)
                weights_of(c, 0)

            def take_x(n, add, relu=False):
                if n in (4, 8):
                    dve.wait_ge(S("pe_d"), {4: 27, 8: 75}[n])
                else:
                    dve.wait_ge(S("x_product"), n - (n > 4))
                if relu:
                    ins = v.scalar_tensor_tensor(X[:], AC[:, 0:D], 0.0, X[:], ALU.max, ALU.add)
                elif add is not None:
                    ins = v.tensor_tensor(X[:], AC[:, 0:D], add, ALU.add)
                else:
                    ins = v.tensor_copy(X[:], AC[:, 0:D])
                ins.then_inc(S("x_ready"), 1)
                dve.wait_ge(S("x_ready"), n)

            def top2(values, chosen):
                vi = values.unsqueeze(2).to_broadcast([P, E8, E8])
                vj = values.unsqueeze(1).to_broadcast([P, E8, E8])
                v.tensor_tensor(g64[:, 0], vj, vi, ALU.is_gt)
                then(v.tensor_tensor(g64[:, 1], vj, vi, ALU.is_equal))
                then(v.tensor_tensor(g64[:, 1], g64[:, 1], tie8[:], ALU.mult))
                then(v.tensor_tensor(g64[:, 0], g64[:, 0], g64[:, 1], ALU.add))
                then(v.tensor_reduce(r8[:, 7, :], g64[:, 0], AX_X, ALU.add))
                then(v.tensor_scalar(chosen, r8[:, 7, :], 2.0, None, ALU.is_lt))

            def mixture(l):
                m = MOE[l]
                k = {1: 6, 3: 10}[l]

                def lo(kind, c0, it, dst=None):
                    n = m["slab"] + 3 * c0 + "gud".index(kind)
                    dve.wait_ge(S("hi_" + kind), it * 2 + (m["first"] + c0 + 1))
                    v.tensor_tensor(wl[dst or kind][:], ring[:, n % RING, :], wh[dst or kind][:].bitcast(F32),
                                    ALU.subtract).then_inc(S("lo_" + kind), 1)

                def turned(q, it):
                    dve.wait_ge(S("hTh_ready"), it * 2 + q)
                    v.tensor_tensor(hTl[:].rearrange("p k n -> p (k n)"), TP[:, 0:SEG],
                                    hTh[:].bitcast(F32).rearrange("p k n -> p (k n)"), ALU.subtract) \
                        .then_inc(S("hTl_ready"), 1)

                def chunk(c0, it=0, first=False, last=False):
                    q = m["first"] + c0
                    if not first:
                        lo("d", c0 - 1, it)
                        turned(q, it)
                    if last:
                        lo("d", c0, it, dst="g")
                    else:
                        lo("g", c0 + 1, it)
                    dve.wait_ge(S("silu_ready"), it * 2 + (q + 1))
                    dve.wait_ge(S("pe_u"), it * 2 + (q + 1))
                    v.scalar_tensor_tensor(hexp, silu, CB[:, bass.ds(it * 2 + c0, 1)], PJ[:, SEG:2 * SEG],
                                           ALU.mult, ALU.mult).then_inc(S("hidden_ready"), 1)
                    if not last:
                        lo("u", c0 + 1, it)

                lo("g", 0, 0)
                dve.wait_ge(S("tr_ready"), k + 1)
                dve.wait_ge(S("XTh_ready"), {1: 1, 3: 2}[l])
                v.tensor_tensor(XTl[:], XT[:], XTh[:].bitcast(F32), ALU.subtract).then_inc(S("XTl_ready"), 1)
                lo("u", 0, 0)
                dve.wait_ge(S("router_product"), {1: 1, 3: 2}[l])
                then(v.tensor_copy(r8[:, 2, :], MS[:, 0:E8]))
                then(v.tensor_reduce(hmax[:, 0:1], r8[:, 2, :], AX_X, ALU.max))
                v.tensor_scalar(r8[:, 0, :], r8[:, 2, :], hmax[:, 0:1], None, ALU.subtract) \
                    .then_inc(S("router_shifted"), 1)
                dve.wait_ge(S("router_exp"), {1: 1, 3: 2}[l])
                if l == 1:
                    then(v.tensor_reduce(hsum[:, 0:1], r8[:, 1, :], AX_X, ALU.add))
                    then(v.reciprocal(hrec[:, 0:1], hsum[:, 0:1]))
                    then(v.tensor_scalar(r8[:, 1, :], r8[:, 1, :], hrec[:, 0:1], None, ALU.mult))
                    then(v.tensor_tensor(r8[:, 3, :], r8[:, 1, :], MS[:, 8:16], ALU.add))
                    top2(r8[:, 3, :], r8[:, 4, :])
                    then(v.tensor_tensor(r8[:, 1, :], r8[:, 1, :], r8[:, 4, :], ALU.mult))
                    then(v.tensor_reduce(hsum[:, 0:1], r8[:, 1, :], AX_X, ALU.add))
                    then(v.tensor_scalar(hsum[:, 0:1], hsum[:, 0:1], 1e-9, None, ALU.add))
                else:
                    top2(r8[:, 2, :], r8[:, 4, :])
                    then(v.tensor_tensor(r8[:, 1, :], r8[:, 1, :], r8[:, 4, :], ALU.mult))
                    then(v.tensor_reduce(hsum[:, 0:1], r8[:, 1, :], AX_X, ALU.add))
                then(v.reciprocal(hrec[:, 0:1], hsum[:, 0:1]))
                then(v.tensor_scalar(r8[:, 5, :], r8[:, 1, :], hrec[:, 0:1], None, ALU.mult))
                per = m["per"]
                then(v.tensor_copy(CB[:, 0:E8 * per].rearrange("p (e j) -> p e j", j=per),
                                   r8[:, 5, :].unsqueeze(2).to_broadcast([P, E8, per])))
                if l == 1:
                    then(v.memset(CB[:, E8 * per:E8 * per + per], 1.0))
                chunk(0, first=True)
                pairs = (m["chunks"] - 2) // 2
                with dve.Fori(0, pairs) as it:
                    chunk(1, it)
                    chunk(2, it)
                for c in range(1 + 2 * pairs, m["chunks"]):
                    chunk(c, last=(c == m["chunks"] - 1))
                turned(m["first"] + m["chunks"], 0)

            dve.wait_ge(S("x_loaded"), 16)
            layernorm(0, X[:], XN[:], "tr_input", 1)
            dve.wait_ge(S("iota_made"), 1)
            v.tensor_copy(iota_f, iota_i)
            dve.wait_ge(S("edges_loaded"), 16)
            then(v.tensor_copy(ids_f, ids_i))
            ids3 = ids_f.rearrange("p (a t) -> p a t", a=2)
            for a in range(2):
                ins = v.tensor_tensor(onehot[:, a], iota_f.unsqueeze(1).to_broadcast([P, E_TILES, P]),
                                      ids3[:, a].unsqueeze(2).to_broadcast([P, E_TILES, P]), ALU.is_equal)
            ins.then_inc(S("onehot_ready"), 1)
            dve.wait_ge(S("counts_product"), 1)
            dve.wait_ge(S("const_ready"), 3)
            then(v.tensor_copy(counts[:, 0, :], MS[:, 0:P]))
            then(v.tensor_tensor(counts[:, 1, :], counts[:, 0, :], ident[:], ALU.add))
            then(v.tensor_scalar(maskb[:], counts[:], 0.0, NOT_AN_EDGE, ALU.is_gt, ALU.mult))
            then(v.tensor_scalar(maskb[:], maskb[:], NOT_AN_EDGE, None, ALU.subtract))
            first_wide(0)
            second(1, 1)
            take_x(1, X[:])
            layernorm(1, X[:], HID[:])
            layernorm(2, HID[:], XN[:])
            dve.wait_ge(S("ffn0_vectors_loaded"), 16)
            then(v.tensor_tensor(XN[:], XN[:], vec(0), ALU.mult))
            v.tensor_tensor(XN[:], XN[:], vec(1), ALU.add).then_inc(S("tr_input"), 1)
            dve.wait_ge(S("tr_input"), 2)
            v.tensor_tensor_reduce(out=junk, in0=XN[:], in1=vec(2), scale=1.0, scalar=0.0, op0=ALU.mult,
                                   op1=ALU.add, accum_out=tk[:, 0:1]).then_inc(S("router0_logit"), 1)
            dve.wait_ge(S("sigmoid_ready"), 1)
            dve.wait_ge(S("score_row"), 1)
            row = MS[:, 0:P]
            v.tensor_scalar(low[:, 0, 0:P], row, tk[:, 1:2], None, ALU.is_lt)
            then(v.scalar_tensor_tensor(low[:, 0, P:2 * P], row, tk[:, 1:2], below[:], ALU.is_equal, ALU.mult))
            then(v.tensor_tensor(low[:, 0, 0:P], low[:, 0, 0:P], low[:, 0, P:2 * P], ALU.add))
            then(v.tensor_reduce(tk[:, 2:3], low[:, 0, 0:P], AX_X, ALU.add))
            v.tensor_scalar(tk[:, 3:4], tk[:, 2:3], float(ROUTED), None, ALU.is_lt)
            v.tensor_scalar(tk[:, 4:5], tk[:, 2:3], float(ROUTED), None, ALU.is_ge)
            then(v.tensor_scalar(tk[:, 5:6], MS[:, P:P + 1], 1e-6, None, ALU.add))
            then(v.reciprocal(tk[:, 6:7], tk[:, 5:6]))
            v.tensor_tensor(tk[:, 7:8], tk[:, 1:2], tk[:, 6:7], ALU.mult).then_inc(S("pool_weight"), 1)
            then(v.scalar_tensor_tensor(BH, vec(5), tk[:, 3:4], HID[:], ALU.mult, ALU.add))
            then(v.scalar_tensor_tensor(BH, vec(6), tk[:, 4:5], BH, ALU.mult, ALU.add))
            dve.wait_ge(S("small_loaded"), 48)
            dve.wait_ge(S("k_zeroed"), 1)
            dve.wait_ge(S("k_product"), 1)
            for t in range(KT):
                for a in range(2):
                    r = slice(a * DH, (a + 1) * DH)
                    ins = v.tensor_scalar(kz[r, t, a, :], PJ[r, t * P:(t + 1) * P], cols[r, 6 + t:7 + t], None,
                                          ALU.add)
            ins.then_inc(S("k_ready"), 1)
            n = HEADS * P
            e3 = EE[:, 0:n].rearrange("p (h s) -> p h s", h=HEADS)
            r3 = TP[:, 0:n].rearrange("p (h s) -> p h s", h=HEADS)
            dve.wait_ge(S("self_logits"), 1)
            then(v.tensor_reduce(hmax[:], r3, AX_X, ALU.max))
            v.tensor_scalar(hneg[:], hmax[:], -(DH ** -0.5), None, ALU.mult).then_inc(S("self_max"), 1)
            dve.wait_ge(S("pooled"), 1)
            then(v.scalar_tensor_tensor(MIX, PJ[:, 0:D], tk[:, 1:2], XN[:], ALU.mult, ALU.add))
            v.tensor_scalar(MIX, MIX, tk[:, 4:5], None, ALU.mult).then_inc(S("tr_input"), 1)
            dve.wait_ge(S("self_exps"), 1)
            then(v.reciprocal(hrec[:], hsum[:]))
            v.tensor_tensor(e3, e3, hrec[:].unsqueeze(2).to_broadcast([P, HEADS, P]), ALU.mult) \
                .then_inc(S("self_weights"), 1)
            dve.wait_ge(S("context"), 1)
            v.tensor_scalar(CTX, AC[:, 0:D], tk[:, 3:4], None, ALU.mult).then_inc(S("tr_input"), 1)
            dve.wait_ge(S("merged"), 1)
            then(v.tensor_tensor(H1[:], PJ[:, 0:D], BH, ALU.add))
            layernorm(3, H1[:], XN[:])
            then(v.tensor_tensor(XN[:], XN[:], vec(3), ALU.mult))
            v.tensor_tensor(XN[:], XN[:], vec(4), ALU.add).then_inc(S("tr_input"), 1)
            then(v.tensor_tensor(XH, X[:], H1[:], ALU.add))
            take_x(2, XH)
            layernorm(4, X[:], XN[:], "tr_input", 6)
            first_narrow(2)
            second(3, 2)
            take_x(3, X[:])
            layernorm(5, X[:], XN[:], "tr_input", 7)
            mixture(1)
            take_x(4, None)
            layernorm(6, X[:], XN[:], "tr_input", 8)
            dve.wait_ge(S("h2_copied"), 3)
            dve.wait_ge(S("vectors_loaded_0"), 16 * (12 // 2 + 1))
            for side in range(2):
                then(v.tensor_tensor(junk, hs2[:], AB[:, 0, side * D:(side + 1) * D], ALU.mult))
                ins = v.tensor_reduce(al[:, side, :], junk.rearrange("p (h c) -> p h c", h=12), AX_X, ALU.add)
                if side == 0:
                    then(ins)
            ins.then_inc(S("vectors_used"), 1)
            dve.wait_ge(S("vectors_used"), 13)
            logits(4, 0)
            for g in range(3):
                if g < 2:
                    logits(4, g + 1)
                weights_of(4, g)
            take_x(5, None, relu=True)
            layernorm(7, X[:], XN[:], "tr_input", 9)
            then(v.memset(comb32[:], 0.0))
            dve.wait_ge(S("l2_gate_product"), 1)
            then(v.tensor_copy(r8[:, 2, :], MS[:, 0:E8]))
            top2(r8[:, 2, :], r8[:, 4, :])
            comb = comb32[:, ROW_B2:ROW_B2 + E8]
            then(v.tensor_tensor(comb, r8[:, 2, :], r8[:, 4, :], ALU.mult))
            dve.wait_ge(S("l2_gelu"), 1)
            g3 = G2.rearrange("p (e f) -> p e f", e=E8)
            v.tensor_tensor(g3, g3, comb.unsqueeze(2).to_broadcast([P, E8, F2]), ALU.mult) \
                .then_inc(S("l2_weighted"), 1)
            take_x(6, X[:])
            layernorm(8, X[:], XN[:], "tr_input", 10)
            first_narrow(5)
            second(6, 4)
            take_x(7, X[:])
            layernorm(9, X[:], XN[:], "tr_input", 11)
            mixture(3)
            take_x(8, None)

        @block.tensor
        def _(pe):
            mm = nc.tensor.matmul

            def turn(k, src):
                pe.wait_ge(S("tr_input"), k + 1)
                for t in range(KT):
                    ins = nc.tensor.transpose(TP[:, t * P:(t + 1) * P], src[:, t * P:(t + 1) * P], ident[:])
                ins.then_inc(S("tr_product"), 1)

            def bias_row(dst, r, c0, c1, start=False, stop=False):
                return mm(dst, ident[0:ROWS, r:r + 1].to_broadcast([ROWS, P]), rows[:, c0:c1], start=start,
                          stop=stop, skip_group_check=True)

            def project(c, j):
                n = w1_slab(c, j)
                if j >= 2:
                    pe.wait_ge(S("h_copied"), SEG_BASE[c] + j - 1)
                landed(pe, n)
                for t in range(KT):
                    ins = mm(bank(j), XT[:, t, :], ring[:, n % RING, t * SEG:(t + 1) * SEG], start=(t == 0),
                             stop=(t == KT - 1))
                ins.then_inc(S("projected"), 1)

            def term_rows(c, g):
                gb, k, at = group(c, g)
                h0 = g * GAT[c]["group"]
                pe.wait_ge(S("vectors_used"), unit_of(c, g) + 1)
                if g:
                    pe.wait_ge(S("logits_ready"), gb)
                for i in range(k):
                    ins = mm(TP[:, SEG + i * P:SEG + (i + 1) * P], al[:, 0, h0 + i:h0 + i + 1].to_broadcast([P, P]),
                             ident[:], start=True, stop=True)
                ins.then_inc(S("term_rows"), 1)

            def turn_attention(c, g):
                gb, k, at = group(c, g)
                pe.wait_ge(S("attn_weights"), gb + 1)
                if g:
                    pe.wait_ge(S("attn_ready"), gb)
                for i in range(k):
                    ins = nc.tensor.transpose(TP[:, 2 * SEG + i * P:2 * SEG + (i + 1) * P],
                                              EE[:, at.start + i * P:at.start + (i + 1) * P], ident[:])
                ins.then_inc(S("attn_turned"), 1)

            def attend(c, i):
                f, C, s = FIRST[c], GAT[c]["C"], SEG_BASE[c] + i
                bias_row(bank(i), f["bias"] + i, 0, SEG, start=True)
                if c == 0:
                    pe.wait_ge(S("attn_ready"), i // 3 + 1)
                else:
                    pe.wait_ge(S("attn_ready"), GROUP_BASE[c] + i + 1)
                at = i * SEG
                while at < (i + 1) * SEG:
                    h = at // C
                    end = min((h + 1) * C, (i + 1) * SEG)
                    g = h // GAT[c]["group"]
                    a = (g % 3) * SEG + (h % GAT[c]["group"]) * P
                    o = at - i * SEG
                    ins = mm(bank(i)[:, o:o + end - at], ALT[:, a:a + P],
                             hs1[:, (i % RING) * SEG + o:(i % RING) * SEG + o + end - at],
                             start=False, stop=(end == (i + 1) * SEG), skip_group_check=True)
                    at = end
                ins.then_inc(S("segment_product"), 1)

            def turn_segment(c, i):
                s = SEG_BASE[c] + i
                pe.wait_ge(S("segment_ready"), s + 1)
                if i >= 2:
                    pe.wait_ge(S("segmentT_ready"), s - 1)
                dst = MS if i % 2 == 0 else TP
                for t in range(4):
                    ins = nc.tensor.transpose(dst[:, t * P:(t + 1) * P], act1[:, i % 2, t * P:(t + 1) * P], ident[:])
                ins.then_inc(S("segment_turned"), 1)

            def product2(c, j):
                s, n = SEG_BASE[c] + j, w2_slab(c, j)
                pe.wait_ge(S("segmentT_ready"), s + 1)
                landed(pe, n)
                for t in range(4):
                    for a, b in halves():
                        ins = mm(AC[:, a:b], act1T[:, j % 2, t * P:(t + 1) * P],
                                 ring[:, n % RING, t * D + a:t * D + b], start=(j == 0 and t == 0),
                                 stop=(j == FIRST[c]["segs"] - 1 and t == 3), skip_group_check=True)
                ins.then_inc(S("segment_used"), 1)

            def edge_counts():
                pe.wait_ge(S("onehot_ready"), 1)
                for t in range(E_TILES):
                    ins = mm(MS[:, 0:P], onehot[:, 1, t, :], onehot[:, 0, t, :], start=(t == 0),
                             stop=(t == E_TILES - 1))
                ins.then_inc(S("counts_product"), 1)

            def first_wide(c):
                per = FIRST[c]["per"]
                groups = FIRST[c]["segs"] // per
                for g in range(groups + 1):
                    if g < groups:
                        if g >= 2:
                            pe.wait_ge(S("segment_ready"), SEG_BASE[c] + per * (g - 1))
                        project(c, per * g)
                    if g:
                        term_rows(c, g - 1)
                    if g < groups:
                        if g == 0:
                            edge_counts()
                        for j in range(1, per):
                            project(c, per * g + j)
                    if g:
                        turn_attention(c, g - 1)
                        pe.wait_ge(S("h_copied"), SEG_BASE[c] + min(per * (g + 1), FIRST[c]["segs"]))
                        for i in range(per + 2):
                            j = per * (g - 1) + i
                            if i < per:
                                if i >= 2:
                                    pe.wait_ge(S("segment_ready"), SEG_BASE[c] + j - 1)
                                attend(c, j)
                            if 0 <= i - 1 < per:
                                turn_segment(c, j - 1)
                            if i >= 2:
                                product2(c, j - 2)

            def first_narrow(c):
                n = FIRST[c]["segs"]
                for t in range(n + 4):
                    if t - 3 >= 1:
                        pe.wait_ge(S("segment_ready"), SEG_BASE[c] + min(t - 3, n))
                    if t < n:
                        project(c, t)
                    if 0 <= t - 1 < n:
                        term_rows(c, t - 1)
                    if 0 <= t - 3 < n:
                        turn_segment(c, t - 3)
                    if 0 <= t - 2 < n:
                        turn_attention(c, t - 2)
                        pe.wait_ge(S("h_copied"), SEG_BASE[c] + min(t + 1, n))
                        attend(c, t - 2)
                    if 0 <= t - 3 < n:
                        product2(c, t - 3)

            def attend_l2(g):
                pe.wait_ge(S("attn_ready"), GROUP_BASE[4] + g + 1)
                for h in range(4 * g, 4 * g + 4):
                    ins = mm(AC[:, h * 64:(h + 1) * 64], ALT[:, h * P:(h + 1) * P], hs2[:, h * 64:(h + 1) * 64],
                             start=False, stop=True, skip_group_check=True)
                return ins

            def second(c, n):
                pe.wait_ge(S("h2_copied"), n)
                for a, b in halves():
                    bias_row(AC[:, a:b], LAYER2_BIAS[c], a, b, start=True)
                term_rows(c, 0)
                turn_attention(c, 0)
                pe.wait_ge(S("attn_ready"), GROUP_BASE[c] + 1)
                for a, b in halves():
                    ins = mm(AC[:, a:b], ALT[:, 0:P], hs2[:, a:b], start=False, stop=True, skip_group_check=True)
                ins.then_inc(S("x_product"), 1)

            def mixture(l):
                m = MOE[l]
                k = {1: 6, 3: 10}[l]
                turn(k, XN)
                pe.wait_ge(S("tr_ready"), k + 1)
                at = {1: 0, 3: KT * E8}[l]
                for t in range(KT):
                    ins = mm(MS[:, 0:E8], XT[:, t, :], small[:, at + t * E8:at + (t + 1) * E8], start=(t == 0),
                             stop=(t == KT - 1))
                if l == 1:
                    ins = mm(MS[:, 8:16], ident[0:ROWS, ROW_MIXED:ROW_MIXED + 1].to_broadcast([ROWS, P]),
                             rows[:, MIXED_EB:MIXED_EB + E8], start=True, stop=True)
                ins.then_inc(S("router_product"), 1)
                for a, b in halves():
                    mm(AC[:, a:b], ident[:], X[:, a:b], start=True, stop=False, skip_group_check=True)
                pe.wait_ge(S("XTl_ready"), {1: 1, 3: 2}[l])

                def up(kind, q, it):
                    pe.wait_ge(S("lo_" + kind), it * 2 + (q + 1))
                    dst = bank("gu".index(kind))
                    for t in range(KT):
                        w = slice(t * SEG, (t + 1) * SEG)
                        mm(dst, XTl[:, t, :], wh[kind][:, w], start=(t == 0), stop=False)
                        mm(dst, XTh[:, t, :], wl[kind][:, w], start=False, stop=False)
                        ins = mm(dst, XTh[:, t, :], wh[kind][:, w], start=False, stop=(t == KT - 1))
                    ins.then_inc(S("pe_" + kind), 1)

                def turn_hidden(q, it):
                    pe.wait_ge(S("hidden_ready"), it * 2 + q)
                    for t in range(4):
                        ins = nc.tensor.transpose(TP[:, t * P:(t + 1) * P], hexp[:, t * P:(t + 1) * P], ident[:])
                    ins.then_inc(S("pe_t"), 1)

                def down(q, it, last=False):
                    d = "g" if last else "d"
                    pe.wait_ge(S("lo_d"), it * 2 + q)
                    pe.wait_ge(S("hTl_ready"), it * 2 + q)
                    for t in range(4):
                        for x, w in ((hTl, wh[d]), (hTh, wl[d]), (hTh, wh[d])):
                            for a, b in halves():
                                ins = mm(AC[:, a:b], x[:, t, :], w[:, t * D + a:t * D + b], start=False,
                                         stop=last and t == 3 and x is hTh and w is wh[d], skip_group_check=True)
                    ins.then_inc(S("pe_d"), 1)

                def chunk(c0, it=0, first=False):
                    q = m["first"] + c0
                    if q:
                        pe.wait_ge(S("silu_ready"), it * 2 + q)
                    up("g", q, it)
                    if not first:
                        turn_hidden(q, it)
                    up("u", q, it)
                    if not first:
                        down(q, it)

                chunk(0, first=True)
                pairs = (m["chunks"] - 2) // 2
                with pe.Fori(0, pairs) as it:
                    chunk(1, it)
                    chunk(2, it)
                for c in range(1 + 2 * pairs, m["chunks"]):
                    chunk(c)
                q = m["first"] + m["chunks"]
                turn_hidden(q, 0)
                down(q, 0, last=True)

            pe.wait_ge(S("const_ready"), 1)
            turn(0, XN)
            pe.wait_ge(S("tr_ready"), 1)
            pe.wait_ge(S("small_loaded"), 48)
            first_wide(0)
            second(1, 1)
            turn(1, XN)
            pe.wait_ge(S("sigmoid_ready"), 1)
            mm(MS[:, 0:P], tk[:, 1:2].to_broadcast([P, P]), ident[:], start=True, stop=True)
            mm(MS[:, P:P + 1], ones[:], tk[:, 1:2], start=True, stop=True).then_inc(S("score_row"), 1)
            pe.wait_ge(S("tr_ready"), 2)
            for w, dst, sem in ((0, TP, "q_product"), (1, PJ, "k_product")):
                for n in range(6 * w // 4, (6 * w + 5) // 4 + 1):
                    landed(pe, FFN0_SLAB + n)
                for t in range(KT):
                    for k in range(KT):
                        ins = mm(dst[:, t * P:(t + 1) * P], w_tile(6 * w + k, t * P, (t + 1) * P), XT[:, k, :],
                                 start=(k == 0), stop=(k == KT - 1))
                ins.then_inc(S(sem), 1)
            pe.wait_ge(S("q_ready"), 1)
            pe.wait_ge(S("k_ready"), 1)
            for t in range(KT):
                ins = mm(TP[:, t * 2 * P:(t + 1) * 2 * P], qT[:, t * P:(t + 1) * P],
                         kz[:, t].rearrange("p a n -> p (a n)"), start=True, stop=True)
            ins.then_inc(S("self_logits"), 1)
            pe.wait_ge(S("pool_weight"), 1)
            for a, b in halves():
                ins = mm(PJ[:, a:b], tk[:, 7:8].to_broadcast([P, P]), XN[:, a:b], start=True, stop=True)
            ins.then_inc(S("pooled"), 1)
            for n in (3, 4):
                landed(pe, FFN0_SLAB + n)
            for a, b in halves():
                bias_row(AC[:, a:b], ROW_BV, a, b, start=True)
                for k in range(KT):
                    ins = mm(AC[:, a:b], XT[:, k, :], w_tile(12 + k, a, b), start=False, stop=(k == KT - 1),
                             skip_group_check=True)
            ins.then_inc(S("v_product"), 1)
            pe.wait_ge(S("self_exps"), 1)
            turn(2, MIX)
            pe.wait_ge(S("tr_ready"), 3)
            landed(pe, FFN0_SLAB + 5)
            for k in range(KT):
                for a, b in halves():
                    mm(PJ[:, a:b], XT[:, k, :], w_tile(18 + k, a, b), start=(k == 0), stop=False,
                       skip_group_check=True)
            pe.wait_ge(S("self_weights"), 1)
            for h in range(HEADS):
                ins = nc.tensor.transpose(TP[:, h * P:(h + 1) * P], EE[:, h * P:(h + 1) * P], ident[:])
            ins.then_inc(S("self_turned"), 1)
            pe.wait_ge(S("self_attn_ready"), 1)
            pe.wait_ge(S("v_ready"), 1)
            for h in range(HEADS):
                ins = mm(AC[:, h * DH:(h + 1) * DH], ALT[:, h * P:(h + 1) * P], V[:, h * DH:(h + 1) * DH],
                         start=True, stop=True)
            ins.then_inc(S("context"), 1)
            turn(3, CTX)
            pe.wait_ge(S("tr_ready"), 4)
            for n in (6, 7):
                landed(pe, FFN0_SLAB + n)
            for k in range(KT):
                for a, b in halves():
                    ins = mm(PJ[:, a:b], XT[:, k, :], w_tile(24 + k, a, b), start=False, stop=(k == KT - 1),
                             skip_group_check=True)
            ins.then_inc(S("merged"), 1)
            for a, b in halves():
                bias_row(AC[:, a:b], ROW_BF2, a, b, start=True)
            turn(4, XN)
            pe.wait_ge(S("tr_ready"), 5)
            for k in range(KT):
                ins = mm(MS[0:F0, 0:P], w_tile(30, k * F0, (k + 1) * F0), XT[:, k, :], start=(k == 0),
                         stop=(k == KT - 1))
            ins.then_inc(S("f_product"), 1)
            pe.wait_ge(S("f_ready"), 1)
            for a, b in halves():
                ins = mm(AC[:, a:b], FT[0:F0, :], w_tile(31, a, b)[0:F0], start=False, stop=True,
                         skip_group_check=True)
            ins.then_inc(S("x_product"), 1)
            turn(5, XN)
            pe.wait_ge(S("tr_ready"), 6)
            first_narrow(2)
            second(3, 2)
            mixture(1)
            turn(7, XN)
            pe.wait_ge(S("tr_ready"), 8)
            at = 2 * KT * E8
            for t in range(KT):
                ins = mm(AC[:, t * P:(t + 1) * P], XT[:, t, :], small[:, at:at + P], start=True, stop=True)
            ins.then_inc(S("l2_h_product"), 1)
            pe.wait_ge(S("h2_copied"), 3)
            for t in range(KT):
                mm(AC[:, t * P:(t + 1) * P], XT[:, t, :], small[:, at + P:at + 2 * P], start=(t in (0, 4)),
                   stop=False, skip_group_check=True)
            term_rows(4, 0)
            for g in range(3):
                if g < 2:
                    term_rows(4, g + 1)
                turn_attention(4, g)
                if g:
                    attend_l2(g - 1)
            attend_l2(2).then_inc(S("x_product"), 1)
            turn(8, XN)
            pe.wait_ge(S("tr_ready"), 9)
            n = L2_SLAB
            landed(pe, n)
            bias_row(MS[:, 0:E8], ROW_MIXED, MIXED_BG, MIXED_BG + E8, start=True)
            for k in range(KT):
                ins = mm(MS[:, 0:E8], XT[:, k, :], ring[:, n % RING, 2304 + k * E8:2304 + (k + 1) * E8], start=False,
                         stop=(k == KT - 1), skip_group_check=True)
            ins.then_inc(S("l2_gate_product"), 1)
            bias_row(PJ[:, 0:384], ROW_MIXED, 0, 384, start=True)
            for k in range(KT):
                ins = mm(PJ[:, 0:384], XT[:, k, :], ring[:, n % RING, k * 384:(k + 1) * 384], start=False,
                         stop=(k == KT - 1), skip_group_check=True)
            ins.then_inc(S("l2_hidden_product"), 1)
            pe.wait_ge(S("l2_weighted"), 1)
            for t in range(3):
                nc.tensor.transpose(TP[:, t * P:(t + 1) * P], G2[:, t * P:(t + 1) * P], ident[:])
            nc.tensor.transpose(TP[0:ROWS, SEG:SEG + P], comb32[:], ident[:]).then_inc(S("l2_turned"), 1)
            n = L2_SLAB + 1
            landed(pe, n)
            pe.wait_ge(S("l2_T_ready"), 2)
            for a, b in halves():
                mm(AC[:, a:b], CBT[0:ROWS, :], rows[:, a:b], start=True, stop=False, skip_group_check=True)
                for t in range(3):
                    ins = mm(AC[:, a:b], G2T[:, t * P:(t + 1) * P], ring[:, n % RING, t * D + a:t * D + b],
                             start=False, stop=(t == 2), skip_group_check=True)
            ins.then_inc(S("x_product"), 1)
            turn(9, XN)
            pe.wait_ge(S("tr_ready"), 10)
            first_narrow(5)
            second(6, 4)
            mixture(3)


def _k_tiles(w):
    k, n = w.shape
    return w.reshape(k // 128, 128, n).transpose(1, 0, 2)


def kernel(**inputs):
    import numpy as np
    import concourse.bacc as bacc
    from concourse.bass_utils import run_bass_kernel_spmd

    i = {k: np.asarray(v) for k, v in inputs.items()}
    f32 = np.float32
    stream = np.zeros((N_SLABS, P, SLAB), f32)

    def by_columns(n, w):
        for j in range(w.shape[1] // SEG):
            stream[n + j] = _k_tiles(w[:, j * SEG:(j + 1) * SEG]).reshape(P, SLAB)

    def by_rows(n, w):
        for j in range(w.shape[0] // SEG):
            stream[n + j] = _k_tiles(w[j * SEG:(j + 1) * SEG]).reshape(P, SLAB)

    def first_layer(c, w1, w2):
        for j in range(FIRST[c]["segs"]):
            by_columns(w1_slab(c, j), w1[:, j * SEG:(j + 1) * SEG])
            by_rows(w2_slab(c, j), w2[j * SEG:(j + 1) * SEG])

    first_layer(0, i["L0_gnn_W1"], i["L0_gnn_W2"])
    first_layer(2, i["L1_gnn_W1"].T, i["L1_gnn_W2"].T)
    first_layer(5, i["L3_gnn_W1"], i["L3_gnn_W2"])
    tiles = np.zeros((P, 32, D), f32)
    for j, name in enumerate(("Wq", "Wk", "Wv", "Wm", "Wo")):
        tiles[:, 6 * j:6 * j + 6] = _k_tiles(i["L0_ffn_" + name])
    tiles[:, 30, 0:KT * F0] = _k_tiles(i["L0_ffn_W1"]).reshape(P, KT * F0)
    tiles[0:F0, 31] = i["L0_ffn_W2"]
    stream[FFN0_SLAB:FFN0_SLAB + 8] = tiles.reshape(P, 8, SLAB).transpose(1, 0, 2)

    def experts(l, e, gate, up, down):
        m = MOE[l]
        for j in range(m["per"]):
            n = m["slab"] + 3 * (e * m["per"] + j)
            f = slice(j * SEG, (j + 1) * SEG)
            by_columns(n, gate[f].T)
            by_columns(n + 1, up[f].T)
            by_rows(n + 2, down[:, f].T)

    for e in range(E8):
        experts(1, e, i["L1_ffn_Wg"][e], i["L1_ffn_Wu"][e], i["L1_ffn_Wd"][e])
        experts(3, e, i["L3_ffn_Wg"][e], i["L3_ffn_Wu"][e], i["L3_ffn_Wd"][e])
    experts(1, E8, i["L1_ffn_sg"], i["L1_ffn_su"], i["L1_ffn_sd"])
    stream[L2_SLAB, :, 0:2304] = _k_tiles(i["L2_ffn_W1"].transpose(1, 0, 2).reshape(D, E8 * F2)).reshape(P, 2304)
    stream[L2_SLAB, :, 2304:2304 + KT * E8] = _k_tiles(i["L2_ffn_Wg"]).reshape(P, KT * E8)
    stream[L2_SLAB + 1, :, 0:2304] = _k_tiles(i["L2_ffn_W2"].reshape(E8 * F2, D)).reshape(P, 2304)

    rows = np.zeros((ROWS, D), f32)
    rows[0:12, 0:SEG] = i["L0_gnn_b1"].reshape(12, SEG)
    rows[12:14, 0:SEG] = i["L1_gnn_b1"].reshape(2, SEG)
    rows[14:18, 0:SEG] = i["L3_gnn_b1"].reshape(4, SEG)
    for r, name in ((18, "L0_gnn_b2"), (19, "L1_gnn_b2"), (20, "L3_gnn_b2"), (ROW_BV, "L0_ffn_bv"),
                    (ROW_BF2, "L0_ffn_bf2")):
        rows[r] = i[name]
    rows[ROW_MIXED, 0:384] = i["L2_ffn_b1"].reshape(384)
    rows[ROW_MIXED, MIXED_BG:MIXED_BG + E8] = i["L2_ffn_bg"]
    rows[ROW_MIXED, MIXED_EB:MIXED_EB + E8] = i["L1_ffn_expert_bias"]
    rows[ROW_B2:ROW_B2 + E8] = i["L2_ffn_b2"]

    cols = np.zeros((P, 16), f32)
    cols[:, 0:6] = i["L0_ffn_bq"].reshape(KT, P).T
    cols[:, 6:12] = i["L0_ffn_bk"].reshape(KT, P).T
    cols[0:F0, 12] = i["L0_ffn_bf1"]

    small = np.zeros((P, 2 * KT * E8 + 2 * P), f32)
    small[:, 0:48] = _k_tiles(i["L1_ffn_w_router"].T).reshape(P, 48)
    small[:, 48:96] = _k_tiles(i["L3_ffn_router_w"].T).reshape(P, 48)
    for j, name in enumerate(("L2_gnn_W", "L2_gnn_W_res")):
        for a in range(2):
            small[64 * a:64 * a + 64, 96 + P * j + 64 * a:96 + P * j + 64 * a + 64] = i[name].T

    names = (("L0_gnn_a_src1", "L0_gnn_a_dst1", 8), ("L0_gnn_a_src2", "L0_gnn_a_dst2", 1),
             ("L1_gnn_att_src1", "L1_gnn_att_dst1", 2), ("L1_gnn_att_src2", "L1_gnn_att_dst2", 1),
             ("L2_gnn_attn_l", "L2_gnn_attn_r", 1), ("L3_gnn_att_src1", "L3_gnn_att_dst1", 4),
             ("L3_gnn_att_src2", "L3_gnn_att_dst2", 1))
    attn = np.concatenate([i[name].reshape(units, -1)[u] for a, b, units in names for u in range(units)
                           for name in (a, b)])[None, :]
    vectors = np.concatenate([i["L0_ffn_" + n].reshape(-1)
                              for n in ("g1", "b1", "Wr", "g2", "b2", "bo", "bm", "br")])[None, :]
    edges = np.concatenate([i["src"].reshape(P, E_TILES), i["dst"].reshape(P, E_TILES)], axis=1)

    nc = bacc.Bacc("TRN2", target_bir_lowering=False, num_devices=1)
    arrays = {}

    def given(name, a):
        arrays["in_" + name] = np.ascontiguousarray(a)
        return nc.dram_tensor("in_" + name, a.shape, mybir.dt.from_np(a.dtype), kind="ExternalInput").ap()

    out = nc.dram_tensor("out", (P, D), F32, kind="ExternalOutput").ap()
    gnn_ffn_kernel(nc, given("x", i["x"]), given("edges", edges), given("weights", stream), given("rows", rows),
                   given("cols", cols), given("small", small), given("attn", attn),
                   given("ffn0_vectors", vectors), out)
    result = run_bass_kernel_spmd(nc, [arrays], core_ids=[0])
    return result.results[0]["out"]
```

```python
from contextlib import ExitStack

import concourse.bass as bass
from concourse import mybir

ALU = mybir.AluOpType
ACT = mybir.ActivationFunctionType
AX_X = mybir.AxisListType.X
F32 = mybir.dt.float32
F32R = mybir.dt.float32r
BF16 = mybir.dt.bfloat16
I32 = mybir.dt.int32

P = 128
D = 768
KT = D // P
E_TILES = 16
SLAB = 3072
SEG = 512
RING = 6
H_RING = 6
LN_EPS = 1e-5
SLOPE = 0.2
NOT_AN_EDGE = 1e30
ROUTED = 19
HEADS = 12
DH = D // HEADS
F0 = 48
E8 = 8
F2 = 48
MIXED_BG, MIXED_EB = E8 * F2, E8 * F2 + E8

GAT = [
    dict(H=8, C=768, group=2, loops=False, unit=0),
    dict(H=1, C=768, group=1, loops=False, unit=8),
    dict(H=8, C=128, group=4, loops=False, unit=9),
    dict(H=1, C=768, group=1, loops=False, unit=11),
    dict(H=12, C=64, group=4, loops=False, unit=12),
    dict(H=4, C=512, group=1, loops=True, unit=13),
    dict(H=1, C=768, group=1, loops=True, unit=17),
]
UNIT = [1536] * 9 + [1024] * 2 + [1536] * 2 + [1024] * 4 + [1536]
FIRST = {
    0: dict(slab=0, segs=12, per=3, bias=0, elu=True),
    2: dict(slab=32, segs=2, per=1, bias=12, elu=False),
    5: dict(slab=119, segs=4, per=1, bias=14, elu=True),
}
LAYER2_BIAS = {1: 18, 3: 19, 6: 20}
ROW_BV, ROW_BF2, ROW_MIXED = 21, 22, 23
ROWS = 32
FFN0_SLAB = 24
L2_SLAB = 117
L2_W = E8 * F2 * KT
N_SLABS = 271
MOE = {
    1: dict(slab=36, chunks=27, per=3, first=0),
    3: dict(slab=127, chunks=48, per=6, first=27),
}
SEG_BASE = {0: 0, 2: 12, 5: 14}
GROUP_BASE = [0, 4, 5, 7, 8, 11, 15]


def slot(n):
    for m in MOE.values():
        c, kind = divmod(n - m["slab"], 3)
        if 0 <= c < m["chunks"]:
            part = 0 if c == 0 else (1, 0, 2)[(c - 1) % 3]
            return RING + kind if part == 2 else (m["slab"] + 3 * part + kind) % RING
    return n % RING


PREVIOUS, LOADS, last = {}, {}, {}
for n in range(N_SLABS):
    PREVIOUS[n] = last.get(slot(n))
    LOADS[n] = LOADS.get(PREVIOUS[n], 0) + 1
    last[slot(n)] = n


def w1_slab(c, j):
    f = FIRST[c]
    if f["per"] == 1:
        return f["slab"] + j
    return f["slab"] + j + max(j // f["per"] - 1, 0) * f["per"]


def w2_slab(c, j):
    f = FIRST[c]
    if f["per"] == 1:
        return f["slab"] + f["segs"] + j
    return f["slab"] + j + min((j // f["per"] + 2) * f["per"], f["segs"])


def is_split(c, j):
    return c == 0 and j % 3 < 2


def split_number(n):
    return n - sum(w2_slab(0, j) < n for j in range(2, FIRST[0]["segs"], 3))


def projected(c, j):
    if c == 0:
        return "split_used", 2 * split_number(w1_slab(c, j)) + 2
    return "plain_projected", {2: 0, 5: 2}[c] + j + 1


def multiplied(c, j):
    if is_split(c, j):
        return "split_used", 2 * split_number(w2_slab(c, j)) + 2
    return "plain_used", (j // 3 if c == 0 else {2: 4, 5: 6}[c] + j) + 1


def copied(c, i):
    if is_split(c, i):
        return "segmentTl_ready", i // 3 * 2 + i % 3 + 1
    return "segmentT_ready", SEG_BASE[c] + i + 1


def when_used(n):
    for m in MOE.values():
        if m["slab"] <= n < m["slab"] + 3 * m["chunks"]:
            k = n - m["slab"]
            return "lo_" + "gud"[k % 3], m["first"] + k // 3 + 1
    for c, f in FIRST.items():
        for j in range(f["segs"]):
            if n == w1_slab(c, j):
                return ("split_lo", 2 * split_number(n) + 2) if c == 0 else projected(c, j)
            if n == w2_slab(c, j):
                return ("split_lo", 2 * split_number(n) + 2) if is_split(c, j) else multiplied(c, j)
    return {24: ("k_product", 1), 25: ("q_product", 1), 26: ("q_product", 1), 27: ("v_product", 1),
            28: ("merged", 1), 29: ("merged", 1), 30: ("merged", 1), 31: ("x_product", 2),
            117: ("l2_hidden_product", 1), 118: ("x_product", 5)}[n]


def gnn_ffn_kernel(nc, x_in, edges_in, weights, rows_in, cols_in, small_in, attn_in, ffn0_vectors, out):
    with ExitStack() as ctx:
        def sb(name, shape, dt=F32):
            return ctx.enter_context(nc.sbuf_tensor(name, shape, dt))

        def psum(name, shape, dt=F32):
            return ctx.enter_context(nc.psum_tensor(name, shape, dt))

        sems = {}

        def S(name):
            if name not in sems:
                sems[name] = ctx.enter_context(nc.semaphore(name))
            return sems[name]

        ring = sb("ring", [P, RING, SLAB])
        extra = sb("extra", [P, 3, SLAB])
        at = [0]

        def third(width):
            at[0] += width
            return extra[:, 2, at[0] - width:at[0]]

        X = extra[:, 1, 0 * D:1 * D]
        XN = extra[:, 1, 1 * D:2 * D]
        HID = extra[:, 1, 2 * D:3 * D]
        H1 = extra[:, 1, 3 * D:4 * D]
        XT = third(D).rearrange("p (k n) -> p k n", k=KT)
        ident = sb("ident", [P, P])
        ones = third(P)
        below = third(P)
        tie8 = sb("tie8", [P, E8, E8])
        counts = sb("counts", [P, 2, P])
        maskb = sb("maskb", [P, 2, P])
        with nc.sbuf_tensor("rows", [2 * ROWS, D], F32) as rows:
            pass
        rows_split = sb("rows_split", [2 * ROWS, D], F32R)
        pick = sb("pick", [2 * ROWS, ROWS], F32R)
        cols = sb("cols", [P, 16])
        small = sb("small", [P, 2 * KT * E8 + 2 * P])
        stats = sb("stats", [P, 2, 6])
        mv = sb("mv", [P, 2])
        veps = sb("veps", [P, 1])
        rstd = sb("rstd", [P, 1])
        power = sb("power", [P, 1])
        al = sb("al", [P, 2, HEADS])
        hmax = sb("hmax", [P, HEADS])
        hneg = sb("hneg", [P, HEADS])
        hsum = sb("hsum", [P, HEADS])
        hrec = sb("hrec", [P, HEADS])
        tk = sb("tk", [P, 8])
        r8 = sb("r8", [P, 8, E8])
        comb = third(E8)
        g64 = sb("g64", [P, 2, E8, E8])
        CB = sb("CB", [P, 48])
        low = [sb("low", [P, SEG])[:], third(SEG)]
        act1 = [sb("act1", [P, SEG])[:], third(SEG)]
        with nc.sbuf_tensor("act1T", [P, 2, SEG], F32) as act1T:
            pass
        act1Th = sb("act1Th", [P, 2, SEG], F32R)
        act1Tl = sb("act1Tl", [P, 2, SEG], F32R)
        rows_hi_copy = act1Th[0:2 * ROWS].rearrange("p a n -> p (a n)")[:, 0:D]
        silu = low[0]
        hexp = act1[0]
        XTh = sb("XTh", [P, KT, P], F32R)
        XTl = sb("XTl", [P, KT, P], F32R)
        hTh = act1Th[:, 0, :]
        AB = extra[:, 0, :].rearrange("p (u n) -> p u n", u=2)
        hs2 = third(D)

        junk = H1[:]

        with nc.sbuf_tensor("scratch", [P, 6 * SLAB], F32) as scratch:
            pass
        wh, wl = {}, {}
        for kind in "dgu":
            wh[kind] = sb(f"w_hi_{kind}", [P, SLAB], F32R)
            wl[kind] = sb(f"w_lo_{kind}", [P, SLAB], F32R)
        end = [0]

        def carve(width):
            start = end[0]
            end[0] = start + (width + 3) // 4 * 4
            return scratch[:, start:start + width]

        hs1 = carve(H_RING * SEG)
        EE = carve(3 * SEG)
        ALT = carve(3 * SEG)
        end[0] = H_RING * SEG
        ids_i = carve(2 * E_TILES).bitcast(I32)
        ids_f = carve(2 * E_TILES)
        iota_i = carve(P).bitcast(I32)
        iota_f = carve(P)
        onehot = carve(E_TILES * P).bitcast(BF16).rearrange("p (a t n) -> p a t n", a=2, t=E_TILES)
        end[0] = 2 * SLAB
        NV = 7
        vec0 = carve(NV * D + 1)
        kz = carve(2 * D).rearrange("p (t a n) -> p t a n", t=KT, a=2)
        qT = carve(D)
        V = carve(D)
        MIX = carve(D)
        CTX = carve(D)
        BH = carve(D)
        FT = carve(P)
        XH = carve(D)
        end[0] = 0
        G2 = carve(E8 * F2)
        G2T = carve(E8 * F2)
        CBT = carve(P)

        HALF = SLAB // 2

        def half_split(k):
            kind, at = "gu"[k % 4 // 2], k % 2 * HALF
            return wh[kind][:, at:at + HALF], wl[kind][:, at:at + HALF]

        def slab_at(n):
            s = slot(n)
            return ring[:, s, :] if s < RING else extra[:, s - RING, :]

        def half_slab(n, half):
            return slab_at(n)[:, half * HALF:(half + 1) * HALF]

        def vec(i):
            return vec0[:, i * D:(i + 1) * D]

        PJ = psum("PJ", [P, 2 * SEG])
        TP = psum("TP", [P, 3 * SEG])
        MS = psum("MS", [P, SEG])
        AC = psum("AC", [P, 2 * SEG])

        land = [S(f"slab_landed_{i}") for i in range(RING + 3)]

        def landed(eng, n):
            eng.wait_ge(land[slot(n)], 16 * LOADS[n])

        def halves():
            return ((0, SEG), (SEG, D))

        def group(c, g):
            k = GAT[c]["group"]
            n = min(k, GAT[c]["H"] - g * k)
            at = (g % 3) * SEG
            return GROUP_BASE[c] + g, n, slice(at, at + n * P)

        def logit_tile(c):
            return low[0] if c in LAYER2_BIAS else EE

        def attn_tile(c):
            return low[1] if c in LAYER2_BIAS else ALT

        def rows_tile(c, g):
            return PJ[:, (g - 1) * SEG:g * SEG] if c == 4 and g else TP[:, SEG:2 * SEG]

        def unit_of(c, g):
            if c == 0:
                return 2 * g + 1
            return GAT[c]["unit"] + (0 if c == 4 else g)

        def ring_seg(j):
            return slice((j % H_RING) * SEG, (j % H_RING + 1) * SEG)

        def bank(j):
            return PJ[:, (j % 2) * SEG:(j % 2 + 1) * SEG]

        def w_tile(t, c0, c1):
            n = FFN0_SLAB + t // 4
            return slab_at(n)[:, (t % 4) * D + c0:(t % 4) * D + c1]

        block = ctx.enter_context(nc.Block())

        @block.sync
        def _(sp):
            sp.dma_start(X[:], x_in).then_inc(S("x_loaded"), 16)

            def slab(n, index):
                sp.dma_start(slab_at(n), weights[index]).then_inc(land[slot(n)], 16)

            def single(n):
                for m, (vectors, opened, lo) in ((MOE[1], (12, 1, 2)), (MOE[3], (18, 2, 3))):
                    if n == m["slab"] + 9:
                        sp.wait_ge(S("vectors_used"), vectors)
                    if n == m["slab"] + 10:
                        sp.wait_ge(S("stream_opened"), opened)
                        sp.wait_ge(S("XTl_ready"), lo)
                    if n == m["slab"] + 11:
                        sp.wait_ge(S("router_product"), opened)
                if PREVIOUS[n] is not None:
                    name, value = when_used(PREVIOUS[n])
                    sp.wait_ge(S(name), value)
                slab(n, n)

            n = 0
            for m in MOE.values():
                loop = m["slab"] + 12
                for n in range(n, loop):
                    single(n)
                rounds = (m["chunks"] - 4) // 3
                with sp.Fori(0, rounds) as it:
                    for j in range(9):
                        sp.wait_ge(S("lo_" + "gud"[j % 3]), it * 3 + (m["first"] + 2 + j // 3))
                        slab(loop + j, it * 9 + (loop + j))
                n = loop + 9 * rounds
            for n in range(n, N_SLABS):
                single(n)
            sp.wait_ge(S("x_ready"), 8)
            sp.dma_start(out, X[:]).then_inc(S("out_stored"), 16)
            sp.wait_ge(S("out_stored"), 16)

        @block.gpsimd
        def _(pool):
            pool.dma_start(ids_i, edges_in).then_inc(S("edges_loaded"), 16)

            def vectors(u):
                if u >= 2:
                    pool.wait_ge(S("vectors_used"), u - 1)
                at = sum(UNIT[:u])
                pool.dma_start(AB[:, u % 2, 0:UNIT[u]], attn_in[:, at:at + UNIT[u]].to_broadcast([P, UNIT[u]])) \
                    .then_inc(S(f"vectors_loaded_{u % 2}"), 16)

            vectors(0)
            vectors(1)
            nc.gpsimd.memset(power[:], -0.5).then_inc(S("const_filled"), 1)
            nc.gpsimd.memset(ident[:], 0.0).then_inc(S("const_filled"), 1)
            nc.gpsimd.memset(ones[:], 1.0).then_inc(S("const_filled"), 1)
            nc.gpsimd.memset(below[:], 1.0).then_inc(S("const_filled"), 1)
            nc.gpsimd.memset(tie8[:], 1.0).then_inc(S("const_filled"), 1)
            pool.wait_ge(S("const_filled"), 5)
            nc.gpsimd.affine_select(out=ident[:], in_=ident[:], compare_op=ALU.not_equal, fill=1.0, base=0,
                                    pattern=[[-1, P]], channel_multiplier=1).then_inc(S("const_ready"), 1)
            nc.gpsimd.iota(iota_i, pattern=[[1, P]], base=0, channel_multiplier=0).then_inc(S("iota_made"), 1)
            nc.gpsimd.affine_select(out=below[:], in_=below[:], compare_op=ALU.is_gt, fill=0.0, base=0,
                                    pattern=[[-1, P]], channel_multiplier=1).then_inc(S("const_ready"), 1)
            nc.gpsimd.affine_select(out=tie8[:], in_=tie8[:], compare_op=ALU.is_gt, fill=0.0, base=0,
                                    pattern=[[1, E8], [-1, E8]], channel_multiplier=0).then_inc(S("const_ready"), 1)

            def ln_power(i):
                pool.wait_ge(S("ln_variance"), i + 1)
                nc.gpsimd.tensor_tensor(rstd[:], veps[:], power[:], ALU.pow).then_inc(S("ln_rstd"), 1)

            ln_power(0)
            pool.dma_start(rows[:], rows_in).then_inc(S("small_loaded"), 16)
            pool.dma_start(cols[:], cols_in).then_inc(S("small_loaded"), 16)
            pool.dma_start(small[:], small_in).then_inc(S("small_loaded"), 16)
            for u in range(2, 9):
                vectors(u)
            pool.wait_ge(S("split_used"), 38)
            pool.dma_start(vec0, ffn0_vectors.to_broadcast([P, NV * D + 1])).then_inc(S("ffn0_vectors_loaded"), 16)
            pool.wait_ge(S("split_used"), 40)
            nc.gpsimd.memset(kz, 0.0).then_inc(S("k_zeroed"), 1)
            for u in range(9, 11):
                vectors(u)
            for i in range(1, 5):
                ln_power(i)
            vectors(11)
            ln_power(5)
            pool.wait_ge(S("lo_g"), 25)
            vectors(12)
            vectors(13)
            ln_power(6)
            vectors(14)
            ln_power(7)
            ln_power(8)
            for u in range(15, 18):
                vectors(u)
            ln_power(9)

        @block.scalar
        def _(act):
            A = nc.scalar.activation

            def transposed(k):
                act.wait_ge(S("tr_product"), k + 1)
                A(XT[:].rearrange("p k n -> p (k n)"), TP[:, 0:D], ACT.Copy).then_inc(S("tr_ready"), 1)

            def transposed_hi(k):
                act.wait_ge(S("tr_product"), k + 1)
                A(XTh[:].rearrange("p k n -> p (k n)"), TP[:, 0:D], ACT.Copy).then_inc(S("tr_ready"), 1)

            def split_hi(n):
                landed(act, n)
                for half in range(2):
                    k = 2 * split_number(n) + half
                    if k >= 4:
                        act.wait_ge(S("split_used"), k - 3)
                    A(half_split(k)[0], half_slab(n, half), ACT.Copy).then_inc(S("split_hi"), 1)

            def rows_hi():
                act.wait_ge(S("const_ready"), 1)
                for r in (slice(0, ROWS), slice(ROWS, 2 * ROWS)):
                    A(pick[r], ident[r, r], ACT.Copy)
                act.wait_ge(S("small_loaded"), 48)
                A(rows_hi_copy[ROWS:2 * ROWS], rows[ROWS:2 * ROWS], ACT.Copy)
                A(rows_split[0:ROWS], rows[0:ROWS], ACT.Copy).then_inc(S("rows_hi"), 1)

            def copy_h(c, j):
                name, value = projected(c, j)
                act.wait_ge(S(name), value)
                A(hs1[:, ring_seg(j)], bank(j), ACT.Copy).then_inc(S("h_copied"), 1)

            def copy_h2():
                A(hs2[:], AC[:, 0:D], ACT.Copy).then_inc(S("h2_copied"), 1)

            def exps(c, g):
                gb, k, at = group(c, g)
                act.wait_ge(S("logits_ready"), gb + 1)
                for i in range(k):
                    e = logit_tile(c)[:, at.start + i * P:at.start + (i + 1) * P]
                    h = g * GAT[c]["group"] + i
                    ins = A(e, e, ACT.Exp, bias=hneg[:, h:h + 1])
                ins.then_inc(S("exps_ready"), 1)

            def turned(c, g):
                gb, k, at = group(c, g)
                act.wait_ge(S("attn_turned"), gb + 1)
                A(attn_tile(c)[:, at], TP[:, 2 * SEG:2 * SEG + k * P], ACT.Copy).then_inc(S("attn_ready"), 1)

            def low_exp(c, i):
                if FIRST[c]["elu"]:
                    e = {0: 0, 5: 12}[c] + i
                    act.wait_ge(S("segment_product"), SEG_BASE[c] + i + 1)
                    if i >= 2:
                        act.wait_ge(S("segment_ready"), SEG_BASE[c] + i - 1)
                    A(low[i % 2], bank(i), ACT.Relu, scale=-1.0).then_inc(S("low_ready"), 1)
                    act.wait_ge(S("low_ready"), e + 1)
                    A(low[i % 2], low[i % 2], ACT.Exp, scale=-1.0).then_inc(S("low_exp"), 1)

            def segment_turned(c, i):
                s = SEG_BASE[c] + i
                act.wait_ge(S("segment_turned"), s + 1)
                if i >= 2:
                    name, value = multiplied(c, i - 2)
                    act.wait_ge(S(name), value)
                dst = act1Th if is_split(c, i) else act1T
                A(dst[:, i % 2, :], MS[:] if i % 2 == 0 else TP[:, 0:SEG], ACT.Copy) \
                    .then_inc(S("segmentT_ready"), 1)

            def first_wide(c):
                per = FIRST[c]["per"]
                groups = FIRST[c]["segs"] // per
                for g in range(groups + 1):
                    first = 3 * (g - 1)
                    if g < groups:
                        if g != 1:
                            split_hi(w1_slab(c, 3 * g))
                        split_hi(w1_slab(c, 3 * g + 1))
                        copy_h(c, 3 * g)
                        split_hi(w1_slab(c, 3 * g + 2))
                    if g == 1:
                        rows_hi()
                    if g == groups:
                        split_hi(w2_slab(c, first))
                    elif g:
                        exps(c, g - 1)
                    if g < groups:
                        copy_h(c, 3 * g + 1)
                    if g == 0:
                        split_hi(w1_slab(c, 3))
                    if 0 < g < groups:
                        split_hi(w2_slab(c, first))
                    if g < groups:
                        copy_h(c, 3 * g + 2)
                    if g:
                        turned(c, g - 1)
                        low_exp(c, first)
                        low_exp(c, first + 1)
                        segment_turned(c, first)
                        low_exp(c, first + 2)
                        segment_turned(c, first + 1)
                        split_hi(w2_slab(c, first + 1))
                        segment_turned(c, first + 2)
                    if g == groups - 1:
                        exps(c, g)

            def first_narrow(c):
                n = FIRST[c]["segs"]
                for t in range(n + 3):
                    if t < n:
                        copy_h(c, t)
                    if 0 <= t - 3:
                        segment_turned(c, t - 3)
                    if 0 <= t - 2 < n:
                        turned(c, t - 2)
                    if 0 <= t - 1 < n:
                        exps(c, t - 1)
                    if 0 <= t - 2 < n:
                        low_exp(c, t - 2)

            def hi(l, kind, c0, it, dst=None):
                m = MOE[l]
                n = m["slab"] + 3 * c0 + "gud".index(kind)
                act.wait_ge(land[slot(n)], it * 16 + 16 * LOADS[n])
                if dst:
                    act.wait_ge(S("pe_" + dst), it * 3 + (m["first"] + c0 + 1))
                elif m["first"] + c0:
                    act.wait_ge(S("pe_" + kind), it * 3 + (m["first"] + c0))
                    if c0 == 0:
                        act.wait_ge(S("pe_d"), m["first"])
                A(wh[dst or kind][:], slab_at(n), ACT.Copy).then_inc(S("hi_" + kind), 1)

            def second(c):
                act.wait_ge(S("vectors_used"), GAT[c]["unit"] + 1)
                copy_h2()
                if c == 6:
                    hi(3, "g", 0, 0)
                exps(c, 0)
                turned(c, 0)
                if c == 6:
                    hi(3, "u", 0, 0)
                if c > 1:
                    hi({3: 1, 6: 3}[c], "d", 0, 0)

            def mixture(l):
                m = MOE[l]
                k = {1: 6, 3: 10}[l]

                def chunk(c0, it=0, first=False, last=False):
                    q = m["first"] + c0
                    act.wait_ge(S("pe_g"), it * 3 + (q + 1))
                    if q:
                        act.wait_ge(S("hidden_ready"), it * 3 + q)
                    if first:
                        hi(l, "g", 1, it)
                    A(silu, PJ[:, 0:SEG], ACT.Silu).then_inc(S("silu_ready"), 1)
                    if not first:
                        act.wait_ge(S("pe_t"), it * 3 + q)
                        A(hTh, TP[:, 0:SEG], ACT.Copy).then_inc(S("hTh_ready"), 1)
                    if last:
                        hi(l, "d", c0, it, dst="g")
                    else:
                        if not first:
                            hi(l, "g", c0 + 1, it)
                        hi(l, "u", c0 + 1, it)
                        if not first:
                            hi(l, "d", c0, it)

                transposed(k)
                act.wait_ge(S("tr_ready"), k + 1)
                A(XTh[:], XT[:], ACT.Copy).then_inc(S("XTh_ready"), 1)
                act.wait_ge(S("router_shifted"), {1: 1, 3: 2}[l])
                A(r8[:, 1, :], r8[:, 0, :], ACT.Exp).then_inc(S("router_exp"), 1)
                chunk(0, first=True)
                rounds = (m["chunks"] - 2) // 3
                with act.Fori(0, rounds) as it:
                    chunk(1, it)
                    chunk(2, it)
                    chunk(3, it)
                for c in range(1 + 3 * rounds, m["chunks"]):
                    chunk(c, last=(c == m["chunks"] - 1))
                act.wait_ge(S("pe_t"), m["first"] + m["chunks"])
                A(act1Th[:, 1], TP[:, 0:SEG], ACT.Copy).then_inc(S("hTh_ready"), 1)

            transposed_hi(0)
            first_wide(0)
            second(1)
            transposed(1)
            act.wait_ge(S("router0_logit"), 1)
            A(tk[:, 1:2], tk[:, 0:1], ACT.Sigmoid, bias=vec0[:, NV * D:NV * D + 1]).then_inc(S("sigmoid_ready"), 1)
            act.wait_ge(S("small_loaded"), 48)
            act.wait_ge(S("q_product"), 1)
            for t in range(KT):
                ins = A(qT[:, t * P:(t + 1) * P], TP[:, t * P:(t + 1) * P], ACT.Identity, bias=cols[:, t:t + 1])
            ins.then_inc(S("q_ready"), 1)
            act.wait_ge(S("self_max"), 1)
            for h in range(HEADS):
                ins = A(EE[:, h * P:(h + 1) * P], TP[:, h * P:(h + 1) * P], ACT.Exp, bias=hneg[:, h:h + 1],
                        scale=DH ** -0.5, accum_out=hsum[:, h:h + 1])
            ins.then_inc(S("self_exps"), 1)
            act.wait_ge(S("v_product"), 1)
            A(V, AC[:, 0:D], ACT.Copy).then_inc(S("v_ready"), 1)
            transposed(2)
            act.wait_ge(S("self_turned"), 1)
            A(ALT[:, 0:HEADS * P], TP[:, 0:HEADS * P], ACT.Copy).then_inc(S("self_attn_ready"), 1)
            transposed(3)
            transposed(4)
            act.wait_ge(S("f_product"), 1)
            A(FT[0:F0, :], MS[0:F0, 0:P], ACT.Gelu, bias=cols[0:F0, 12:13]).then_inc(S("f_ready"), 1)
            transposed(5)
            hi(1, "g", 0, 0)
            hi(1, "u", 0, 0)
            first_narrow(2)
            second(3)
            mixture(1)
            transposed(7)
            exps(4, 0)
            act.wait_ge(S("vectors_used"), 13)
            copy_h2()
            for g in range(3):
                if g < 2:
                    exps(4, g + 1)
                turned(4, g)
            transposed(8)
            act.wait_ge(S("l2_hidden_product"), 1)
            A(G2, PJ[:, 0:E8 * F2], ACT.Gelu).then_inc(S("l2_gelu"), 1)
            act.wait_ge(S("l2_turned"), 1)
            A(G2T, TP[:, 0:E8 * F2], ACT.Copy).then_inc(S("l2_T_ready"), 1)
            A(CBT[0:E8, :], TP[0:E8, SEG:SEG + P], ACT.Copy).then_inc(S("l2_T_ready"), 1)
            transposed(9)
            first_narrow(5)
            second(6)
            mixture(3)

        @block.vector
        def _(dve):
            v = nc.vector
            step = [0]

            def then(ins):
                step[0] += 1
                ins.then_inc(S("vector_step"), 1)
                dve.wait_ge(S("vector_step"), step[0])

            def layernorm(i, src, dst, sem=None, count=0):
                v.bn_stats(stats[:, 0, :], src[:, 0:384])
                then(v.bn_stats(stats[:, 1, :], src[:, 384:768]))
                then(v.bn_aggr(mv[:], stats[:]))
                v.tensor_scalar(veps[:], mv[:, 1:2], LN_EPS, None, ALU.add).then_inc(S("ln_variance"), 1)
                dve.wait_ge(S("ln_rstd"), i + 1)
                last = v.tensor_scalar(dst, src, mv[:, 0:1], rstd[:], ALU.subtract, ALU.mult)
                if sem is None:
                    then(last)
                else:
                    last.then_inc(S(sem), 1)
                    dve.wait_ge(S(sem), count)

            def terms(u, heads, C, src):
                dve.wait_ge(S(f"vectors_loaded_{u % 2}"), 16 * (u // 2 + 1))
                k = len(heads)
                for side in range(2):
                    for i, h in enumerate(heads):
                        ins = v.tensor_tensor_reduce(out=junk[:, i * C:(i + 1) * C], in0=src[:, i * C:(i + 1) * C],
                                                     in1=AB[:, u % 2, (side * k + i) * C:(side * k + i + 1) * C],
                                                     scale=1.0, scalar=0.0, op0=ALU.mult, op1=ALU.add,
                                                     accum_out=al[:, side, h:h + 1])
                    if side == 0:
                        then(ins)
                ins.then_inc(S("vectors_used"), 1)
                dve.wait_ge(S("vectors_used"), u + 1)

            def logits(c, g):
                gb, k, at = group(c, g)
                h0 = g * GAT[c]["group"]
                mask = maskb[:, int(GAT[c]["loops"]), :]
                e3 = logit_tile(c)[:, at].rearrange("p (h s) -> p h s", h=k)
                r3 = rows_tile(c, g)[:, 0:k * P].rearrange("p (h s) -> p h s", h=k)
                dve.wait_ge(S("term_rows"), gb + 1)
                m = hmax[:, h0:h0 + k]
                for i in range(k):
                    ins = v.tensor_tensor_reduce(out=e3[:, i, :], in0=r3[:, i, :], in1=mask, scale=1.0,
                                                 scalar=-3.0e38, op0=ALU.add, op1=ALU.max,
                                                 accum_out=hmax[:, h0 + i:h0 + i + 1])
                then(ins)
                v.scalar_tensor_tensor(e3, e3, SLOPE, e3, ALU.mult, ALU.max)
                then(v.scalar_tensor_tensor(m, m, SLOPE, m, ALU.mult, ALU.max))
                v.tensor_scalar(hneg[:, h0:h0 + k], m, -1.0, None, ALU.mult).then_inc(S("logits_ready"), 1)

            def weights_of(c, g):
                gb, k, at = group(c, g)
                h0 = g * GAT[c]["group"]
                e3 = logit_tile(c)[:, at].rearrange("p (h s) -> p h s", h=k)
                dve.wait_ge(S("exps_ready"), gb + 1)
                for i in range(k):
                    ins = v.tensor_tensor_reduce(out=e3[:, i, :], in0=e3[:, i, :],
                                                 in1=counts[:, int(GAT[c]["loops"]), :], scale=1.0, scalar=0.0,
                                                 op0=ALU.mult, op1=ALU.add, accum_out=hsum[:, h0 + i:h0 + i + 1])
                then(ins)
                then(v.tensor_scalar(hsum[:, h0:h0 + k], hsum[:, h0:h0 + k], 1e-16, None,
                                     ALU.max if c == 4 else ALU.add))
                then(v.reciprocal(hrec[:, h0:h0 + k], hsum[:, h0:h0 + k]))
                v.tensor_tensor(e3, e3, hrec[:, h0:h0 + k].unsqueeze(2).to_broadcast([P, k, P]), ALU.mult) \
                    .then_inc(S("attn_weights"), 1)

            def activate(c, i):
                s = SEG_BASE[c] + i
                z = bank(i)
                dve.wait_ge(S("segment_product"), s + 1)
                if i >= 2:
                    dve.wait_ge(S("segment_turned"), s - 1)
                if FIRST[c]["elu"]:
                    dve.wait_ge(S("low_exp"), {0: 0, 5: 12}[c] + i + 1)
                    v.scalar_tensor_tensor(act1[i % 2], low[i % 2], -1.0, z, ALU.add, ALU.max) \
                        .then_inc(S("segment_ready"), 1)
                else:
                    v.tensor_scalar(act1[i % 2], z, 0.0, None, ALU.max).then_inc(S("segment_ready"), 1)

            def edges_one_hot():
                dve.wait_ge(S("iota_made"), 1)
                v.tensor_copy(iota_f, iota_i)
                dve.wait_ge(S("edges_loaded"), 16)
                then(v.tensor_copy(ids_f, ids_i))
                ids3 = ids_f.rearrange("p (a t) -> p a t", a=2)
                for a in range(2):
                    ins = v.tensor_tensor(onehot[:, a], iota_f.unsqueeze(1).to_broadcast([P, E_TILES, P]),
                                          ids3[:, a].unsqueeze(2).to_broadcast([P, E_TILES, P]), ALU.is_equal)
                ins.then_inc(S("onehot_ready"), 1)

            def edge_masks():
                dve.wait_ge(S("counts_product"), 1)
                dve.wait_ge(S("const_ready"), 3)
                then(v.tensor_copy(counts[:, 0, :], MS[:, 0:P]))
                then(v.tensor_tensor(counts[:, 1, :], counts[:, 0, :], ident[:], ALU.add))
                then(v.tensor_scalar(maskb[:], counts[:], 0.0, NOT_AN_EDGE, ALU.is_gt, ALU.mult))
                then(v.tensor_scalar(maskb[:], maskb[:], NOT_AN_EDGE, None, ALU.subtract))

            def transposed_lo(k):
                dve.wait_ge(S("tr_ready"), k + 1)
                v.tensor_tensor(XTl[:].rearrange("p k n -> p (k n)"), TP[:, 0:D],
                                XTh[:].bitcast(F32).rearrange("p k n -> p (k n)"), ALU.subtract) \
                    .then_inc(S("XTl_ready"), 1)

            def split_lo(n):
                for half in range(2):
                    k = 2 * split_number(n) + half
                    hi, lo = half_split(k)
                    dve.wait_ge(S("split_hi"), k + 1)
                    v.tensor_tensor(lo, half_slab(n, half), hi.bitcast(F32), ALU.subtract) \
                        .then_inc(S("split_lo"), 1)

            def segment_lo(c, i):
                dve.wait_ge(S("segmentT_ready"), SEG_BASE[c] + i + 1)
                v.tensor_tensor(act1Tl[:, i % 2, :], MS[:] if i % 2 == 0 else TP[:, 0:SEG],
                                act1Th[:, i % 2, :].bitcast(F32), ALU.subtract).then_inc(S("segmentTl_ready"), 1)

            def first_wide(c):
                per, C = FIRST[c]["per"], GAT[c]["C"]
                groups = FIRST[c]["segs"] // per

                def wide_terms(h):
                    dve.wait_ge(S("h_copied"), SEG_BASE[c] + ((h + 1) * C + SEG - 1) // SEG)
                    at = h * C % (H_RING * SEG)
                    terms(h, [h], C, hs1[:, at:at + C])

                for g in range(groups + 1):
                    first = 3 * (g - 1)
                    if g < groups:
                        if g != 1:
                            split_lo(w1_slab(c, 3 * g))
                        split_lo(w1_slab(c, 3 * g + 1))
                    if g == 0:
                        edges_one_hot()
                    elif g < groups:
                        logits(c, g - 1)
                    if g < groups:
                        split_lo(w1_slab(c, 3 * g + 2))
                    if 0 < g < groups:
                        weights_of(c, g - 1)
                    if g == 0:
                        wide_terms(0)
                        split_lo(w1_slab(c, 3))
                    else:
                        if g == 1:
                            dve.wait_ge(S("rows_hi"), 1)
                            low_rows = slice(ROWS, 2 * ROWS)
                            v.tensor_tensor(rows_split[low_rows], rows[low_rows], rows_hi_copy[low_rows].bitcast(F32),
                                            ALU.subtract).then_inc(S("rows_lo"), 1)
                        split_lo(w2_slab(c, first))
                        activate(c, first)
                        activate(c, first + 1)
                        segment_lo(c, first)
                        if g < groups:
                            wide_terms(2 * g)
                        activate(c, first + 2)
                        segment_lo(c, first + 1)
                        split_lo(w2_slab(c, first + 1))
                    if g < groups:
                        wide_terms(2 * g + 1)
                    if g == 0:
                        edge_masks()
                    if g == groups - 1:
                        logits(c, g)
                        weights_of(c, g)

            def first_narrow(c):
                n, k, C = FIRST[c]["segs"], GAT[c]["group"], GAT[c]["C"]
                for t in range(n + 2):
                    if 0 <= t - 1 < n:
                        logits(c, t - 1)
                    if t < n:
                        dve.wait_ge(S("h_copied"), SEG_BASE[c] + t + 1)
                        terms(GAT[c]["unit"] + t, range(t * k, t * k + k), C, hs1[:, ring_seg(t)])
                    if c == 2 and t == 0:
                        lo(1, "u", 0, 0)
                    if 0 <= t - 2 and not FIRST[c]["elu"]:
                        activate(c, t - 2)
                    if 0 <= t - 1 < n:
                        weights_of(c, t - 1)
                    if 0 <= t - 2 and FIRST[c]["elu"]:
                        activate(c, t - 2)

            def lo(l, kind, c0, it, dst=None):
                m = MOE[l]
                n = m["slab"] + 3 * c0 + "gud".index(kind)
                dve.wait_ge(S("hi_" + kind), it * 3 + (m["first"] + c0 + 1))
                v.tensor_tensor(wl[dst or kind][:], slab_at(n), wh[dst or kind][:].bitcast(F32),
                                ALU.subtract).then_inc(S("lo_" + kind), 1)

            def second(c):
                name, value = multiplied(c - 1, FIRST[c - 1]["segs"] - 1)
                dve.wait_ge(S(name), value)
                terms(GAT[c]["unit"], [0], D, AC)
                logits(c, 0)
                weights_of(c, 0)
                if c == 6:
                    lo(3, "g", 0, 0)

            def take_x(n, add, relu=False):
                if n in (4, 8):
                    dve.wait_ge(S("pe_d"), {4: 27, 8: 75}[n])
                else:
                    dve.wait_ge(S("x_product"), n - (n > 4))
                if relu:
                    ins = v.scalar_tensor_tensor(X[:], AC[:, 0:D], 0.0, X[:], ALU.max, ALU.add)
                elif add is not None:
                    ins = v.tensor_tensor(X[:], AC[:, 0:D], add, ALU.add)
                else:
                    ins = v.tensor_copy(X[:], AC[:, 0:D])
                ins.then_inc(S("x_ready"), 1)
                dve.wait_ge(S("x_ready"), n)

            def top2(values, chosen):
                vi = values.unsqueeze(2).to_broadcast([P, E8, E8])
                vj = values.unsqueeze(1).to_broadcast([P, E8, E8])
                v.tensor_tensor(g64[:, 0], vj, vi, ALU.is_gt)
                then(v.tensor_tensor(g64[:, 1], vj, vi, ALU.is_equal))
                then(v.tensor_tensor(g64[:, 1], g64[:, 1], tie8[:], ALU.mult))
                then(v.tensor_tensor(g64[:, 0], g64[:, 0], g64[:, 1], ALU.add))
                then(v.tensor_reduce(r8[:, 7, :], g64[:, 0], AX_X, ALU.add))
                then(v.tensor_scalar(chosen, r8[:, 7, :], 2.0, None, ALU.is_lt))

            def mixture(l):
                m = MOE[l]
                k = {1: 6, 3: 10}[l]

                def turned(q, it, half=0):
                    dve.wait_ge(S("hTh_ready"), it * 3 + q)
                    v.tensor_tensor(act1Tl[:, half], TP[:, 0:SEG], act1Th[:, half].bitcast(F32), ALU.subtract) \
                        .then_inc(S("hTl_ready"), 1)

                def chunk(c0, it=0, first=False, last=False):
                    q = m["first"] + c0
                    if not first:
                        turned(q, it)
                    if not last:
                        lo(l, "g", c0 + 1, it)
                    dve.wait_ge(S("silu_ready"), it * 3 + (q + 1))
                    dve.wait_ge(S("pe_u"), it * 3 + (q + 1))
                    v.scalar_tensor_tensor(hexp, silu, CB[:, bass.ds(it * 3 + c0, 1)], PJ[:, SEG:2 * SEG],
                                           ALU.mult, ALU.mult).then_inc(S("hidden_ready"), 1)
                    if last:
                        lo(l, "d", c0, it, dst="g")
                    else:
                        lo(l, "u", c0 + 1, it)
                        if not first:
                            lo(l, "d", c0, it)

                if l == 3:
                    lo(l, "u", 0, 0)
                dve.wait_ge(S("tr_ready"), k + 1)
                dve.wait_ge(S("XTh_ready"), {1: 1, 3: 2}[l])
                v.tensor_tensor(XTl[:], XT[:], XTh[:].bitcast(F32), ALU.subtract).then_inc(S("XTl_ready"), 1)
                lo(l, "d", 0, 0)
                dve.wait_ge(S("router_product"), {1: 1, 3: 2}[l])
                then(v.tensor_copy(r8[:, 2, :], MS[:, 0:E8]))
                then(v.tensor_reduce(hmax[:, 0:1], r8[:, 2, :], AX_X, ALU.max))
                v.tensor_scalar(r8[:, 0, :], r8[:, 2, :], hmax[:, 0:1], None, ALU.subtract) \
                    .then_inc(S("router_shifted"), 1)
                dve.wait_ge(S("router_exp"), {1: 1, 3: 2}[l])
                if l == 1:
                    then(v.tensor_reduce(hsum[:, 0:1], r8[:, 1, :], AX_X, ALU.add))
                    then(v.reciprocal(hrec[:, 0:1], hsum[:, 0:1]))
                    then(v.tensor_scalar(r8[:, 1, :], r8[:, 1, :], hrec[:, 0:1], None, ALU.mult))
                    then(v.tensor_tensor(r8[:, 3, :], r8[:, 1, :], MS[:, 8:16], ALU.add))
                    top2(r8[:, 3, :], r8[:, 4, :])
                    then(v.tensor_tensor(r8[:, 1, :], r8[:, 1, :], r8[:, 4, :], ALU.mult))
                    then(v.tensor_reduce(hsum[:, 0:1], r8[:, 1, :], AX_X, ALU.add))
                    then(v.tensor_scalar(hsum[:, 0:1], hsum[:, 0:1], 1e-9, None, ALU.add))
                else:
                    top2(r8[:, 2, :], r8[:, 4, :])
                    then(v.tensor_tensor(r8[:, 1, :], r8[:, 1, :], r8[:, 4, :], ALU.mult))
                    then(v.tensor_reduce(hsum[:, 0:1], r8[:, 1, :], AX_X, ALU.add))
                then(v.reciprocal(hrec[:, 0:1], hsum[:, 0:1]))
                then(v.tensor_scalar(r8[:, 5, :], r8[:, 1, :], hrec[:, 0:1], None, ALU.mult))
                per = m["per"]
                then(v.tensor_copy(CB[:, 0:E8 * per].rearrange("p (e j) -> p e j", j=per),
                                   r8[:, 5, :].unsqueeze(2).to_broadcast([P, E8, per])))
                if l == 1:
                    then(v.memset(CB[:, E8 * per:E8 * per + per], 1.0))
                chunk(0, first=True)
                rounds = (m["chunks"] - 2) // 3
                with dve.Fori(0, rounds) as it:
                    chunk(1, it)
                    chunk(2, it)
                    chunk(3, it)
                for c in range(1 + 3 * rounds, m["chunks"]):
                    chunk(c, last=(c == m["chunks"] - 1))
                turned(m["first"] + m["chunks"], 0, 1)

            dve.wait_ge(S("x_loaded"), 16)
            layernorm(0, X[:], XN[:], "tr_input", 1)
            transposed_lo(0)
            first_wide(0)
            second(1)
            take_x(1, X[:])
            layernorm(1, X[:], HID[:])
            layernorm(2, HID[:], XN[:])
            dve.wait_ge(S("ffn0_vectors_loaded"), 16)
            then(v.tensor_tensor(XN[:], XN[:], vec(0), ALU.mult))
            v.tensor_tensor(XN[:], XN[:], vec(1), ALU.add).then_inc(S("tr_input"), 1)
            dve.wait_ge(S("tr_input"), 2)
            v.tensor_tensor_reduce(out=junk, in0=XN[:], in1=vec(2), scale=1.0, scalar=0.0, op0=ALU.mult,
                                   op1=ALU.add, accum_out=tk[:, 0:1]).then_inc(S("router0_logit"), 1)
            dve.wait_ge(S("sigmoid_ready"), 1)
            dve.wait_ge(S("score_row"), 1)
            row = MS[:, 0:P]
            v.tensor_scalar(low[0][:, 0:P], row, tk[:, 1:2], None, ALU.is_lt)
            then(v.scalar_tensor_tensor(low[0][:, P:2 * P], row, tk[:, 1:2], below[:], ALU.is_equal, ALU.mult))
            then(v.tensor_tensor(low[0][:, 0:P], low[0][:, 0:P], low[0][:, P:2 * P], ALU.add))
            then(v.tensor_reduce(tk[:, 2:3], low[0][:, 0:P], AX_X, ALU.add))
            v.tensor_scalar(tk[:, 3:4], tk[:, 2:3], float(ROUTED), None, ALU.is_lt)
            v.tensor_scalar(tk[:, 4:5], tk[:, 2:3], float(ROUTED), None, ALU.is_ge)
            then(v.tensor_scalar(tk[:, 5:6], MS[:, P:P + 1], 1e-6, None, ALU.add))
            then(v.reciprocal(tk[:, 6:7], tk[:, 5:6]))
            v.tensor_tensor(tk[:, 7:8], tk[:, 1:2], tk[:, 6:7], ALU.mult).then_inc(S("pool_weight"), 1)
            then(v.scalar_tensor_tensor(BH, vec(5), tk[:, 3:4], HID[:], ALU.mult, ALU.add))
            then(v.scalar_tensor_tensor(BH, vec(6), tk[:, 4:5], BH, ALU.mult, ALU.add))
            dve.wait_ge(S("small_loaded"), 48)
            dve.wait_ge(S("k_zeroed"), 1)
            dve.wait_ge(S("k_product"), 1)
            for t in range(KT):
                for a in range(2):
                    r = slice(a * DH, (a + 1) * DH)
                    ins = v.tensor_scalar(kz[r, t, a, :], PJ[r, t * P:(t + 1) * P], cols[r, 6 + t:7 + t], None,
                                          ALU.add)
            ins.then_inc(S("k_ready"), 1)
            n = HEADS * P
            e3 = EE[:, 0:n].rearrange("p (h s) -> p h s", h=HEADS)
            r3 = TP[:, 0:n].rearrange("p (h s) -> p h s", h=HEADS)
            dve.wait_ge(S("pooled"), 1)
            then(v.scalar_tensor_tensor(MIX, PJ[:, 0:D], tk[:, 1:2], XN[:], ALU.mult, ALU.add))
            v.tensor_scalar(MIX, MIX, tk[:, 4:5], None, ALU.mult).then_inc(S("tr_input"), 1)
            dve.wait_ge(S("self_logits"), 1)
            then(v.tensor_reduce(hmax[:], r3, AX_X, ALU.max))
            v.tensor_scalar(hneg[:], hmax[:], -(DH ** -0.5), None, ALU.mult).then_inc(S("self_max"), 1)
            dve.wait_ge(S("self_exps"), 1)
            then(v.reciprocal(hrec[:], hsum[:]))
            v.tensor_tensor(e3, e3, hrec[:].unsqueeze(2).to_broadcast([P, HEADS, P]), ALU.mult) \
                .then_inc(S("self_weights"), 1)
            dve.wait_ge(S("context"), 1)
            v.tensor_scalar(CTX, AC[:, 0:D], tk[:, 3:4], None, ALU.mult).then_inc(S("tr_input"), 1)
            dve.wait_ge(S("merged"), 1)
            then(v.tensor_tensor(H1[:], PJ[:, 0:D], BH, ALU.add))
            layernorm(3, H1[:], XN[:])
            then(v.tensor_tensor(XN[:], XN[:], vec(3), ALU.mult))
            v.tensor_tensor(XN[:], XN[:], vec(4), ALU.add).then_inc(S("tr_input"), 1)
            then(v.tensor_tensor(XH, X[:], H1[:], ALU.add))
            take_x(2, XH)
            layernorm(4, X[:], XN[:], "tr_input", 6)
            lo(1, "g", 0, 0)
            first_narrow(2)
            second(3)
            take_x(3, X[:])
            layernorm(5, X[:], XN[:], "tr_input", 7)
            mixture(1)
            take_x(4, None)
            layernorm(6, X[:], XN[:], "tr_input", 8)
            dve.wait_ge(S("l2_h_product"), 1)
            dve.wait_ge(S("vectors_loaded_0"), 16 * (12 // 2 + 1))

            def l2_terms(g):
                for side in range(2):
                    part = junk[:, g * 4 * C2:(g + 1) * 4 * C2]
                    at = side * D + g * 4 * C2
                    then(v.tensor_tensor(part, AC[:, g * 4 * C2:(g + 1) * 4 * C2], AB[:, 0, at:at + 4 * C2],
                                         ALU.mult))
                    ins = v.tensor_reduce(al[:, side, 4 * g:4 * g + 4], part.rearrange("p (h c) -> p h c", h=4), AX_X,
                                          ALU.add)
                    if side == 0:
                        then(ins)
                name, value = ("l2_terms", g + 1) if g < 2 else ("vectors_used", 13)
                ins.then_inc(S(name), 1)
                dve.wait_ge(S(name), value)

            C2 = GAT[4]["C"]
            l2_terms(0)
            l2_terms(1)
            logits(4, 0)
            l2_terms(2)
            logits(4, 1)
            weights_of(4, 0)
            logits(4, 2)
            weights_of(4, 1)
            weights_of(4, 2)
            take_x(5, None, relu=True)
            layernorm(7, X[:], XN[:], "tr_input", 9)
            dve.wait_ge(S("l2_gate_product"), 1)
            then(v.tensor_copy(r8[:, 2, :], MS[:, 0:E8]))
            top2(r8[:, 2, :], r8[:, 4, :])
            then(v.tensor_tensor(comb, r8[:, 2, :], r8[:, 4, :], ALU.mult))
            dve.wait_ge(S("l2_gelu"), 1)
            g3 = G2.rearrange("p (e f) -> p e f", e=E8)
            v.tensor_tensor(g3, g3, comb.unsqueeze(2).to_broadcast([P, E8, F2]), ALU.mult) \
                .then_inc(S("l2_weighted"), 1)
            take_x(6, X[:])
            layernorm(8, X[:], XN[:], "tr_input", 10)
            first_narrow(5)
            second(6)
            take_x(7, X[:])
            layernorm(9, X[:], XN[:], "tr_input", 11)
            mixture(3)
            take_x(8, None)

        @block.tensor
        def _(pe):
            mm = nc.tensor.matmul

            def keep_warm(count, dst=MS[:, 3 * P:4 * P]):
                for _ in range(count):
                    mm(dst, ident[:], ident[:], start=True, stop=True)

            def turn(k, src, warm=0):
                keep_warm(warm)
                pe.wait_ge(S("tr_input"), k + 1)
                for t in range(KT):
                    ins = nc.tensor.transpose(TP[:, t * P:(t + 1) * P], src[:, t * P:(t + 1) * P], ident[:])
                ins.then_inc(S("tr_product"), 1)

            def bias_row(dst, r, c0, c1, start=False, stop=False):
                return mm(dst, pick[:, r:r + 1].to_broadcast([2 * ROWS, P]), rows_split[0:2 * ROWS, c0:c1],
                          start=start, stop=stop, skip_group_check=True)

            def project(c, j):
                n = w1_slab(c, j)
                if j >= 2:
                    pe.wait_ge(S("h_copied"), SEG_BASE[c] + j - 1)
                if c:
                    landed(pe, n)
                    for t in range(KT):
                        ins = mm(bank(j), XT[:, t, :], slab_at(n)[:, t * SEG:(t + 1) * SEG], start=(t == 0),
                                 stop=(t == KT - 1))
                    ins.then_inc(S("plain_projected"), 1)
                    return
                for t in range(KT):
                    k = 2 * split_number(n) + t // 3
                    hi, lo = half_split(k)
                    w = slice(t % 3 * SEG, (t % 3 + 1) * SEG)
                    if t % 3 == 0:
                        pe.wait_ge(S("split_lo"), k + 1)
                    mm(bank(j), XTl[:, t, :], hi[:, w], start=(t == 0), stop=False)
                    mm(bank(j), XTh[:, t, :], lo[:, w], start=False, stop=False)
                    ins = mm(bank(j), XTh[:, t, :], hi[:, w], start=False, stop=(t == KT - 1))
                    if t % 3 == 2:
                        ins.then_inc(S("split_used"), 1)

            def term_rows(c, g):
                gb, k, at = group(c, g)
                h0 = g * GAT[c]["group"]
                if c == 4 and g < 2:
                    pe.wait_ge(S("l2_terms"), g + 1)
                else:
                    pe.wait_ge(S("vectors_used"), unit_of(c, g) + 1)
                if g and c != 4:
                    pe.wait_ge(S("logits_ready"), gb)
                for i in range(k):
                    h, dst = h0 + i, rows_tile(c, g)[:, i * P:(i + 1) * P]
                    mm(dst, al[:, 0, h:h + 1].to_broadcast([P, P]), ident[:], start=True, stop=False)
                    ins = mm(dst, ident[:], al[:, 1, h:h + 1].to_broadcast([P, P]), start=False, stop=True)
                ins.then_inc(S("term_rows"), 1)

            def turn_attention(c, g):
                gb, k, at = group(c, g)
                pe.wait_ge(S("attn_weights"), gb + 1)
                if g:
                    pe.wait_ge(S("attn_ready"), gb)
                for i in range(k):
                    ins = nc.tensor.transpose(TP[:, 2 * SEG + i * P:2 * SEG + (i + 1) * P],
                                              logit_tile(c)[:, at.start + i * P:at.start + (i + 1) * P], ident[:])
                ins.then_inc(S("attn_turned"), 1)

            def attend(c, i):
                f, C, s = FIRST[c], GAT[c]["C"], SEG_BASE[c] + i
                bias_row(bank(i), f["bias"] + i, 0, SEG, start=True)
                if c == 0:
                    pe.wait_ge(S("attn_ready"), i // 3 + 1)
                else:
                    pe.wait_ge(S("attn_ready"), GROUP_BASE[c] + i + 1)
                at = i * SEG
                while at < (i + 1) * SEG:
                    h = at // C
                    end = min((h + 1) * C, (i + 1) * SEG)
                    g = h // GAT[c]["group"]
                    a = (g % 3) * SEG + (h % GAT[c]["group"]) * P
                    o = at - i * SEG
                    ins = mm(bank(i)[:, o:o + end - at], ALT[:, a:a + P],
                             hs1[:, (i % H_RING) * SEG + o:(i % H_RING) * SEG + o + end - at],
                             start=False, stop=(end == (i + 1) * SEG), skip_group_check=True)
                    at = end
                ins.then_inc(S("segment_product"), 1)

            def turn_segment(c, i):
                s = SEG_BASE[c] + i
                pe.wait_ge(S("segment_ready"), s + 1)
                if i >= 2:
                    name, value = copied(c, i - 2)
                    pe.wait_ge(S(name), value)
                dst = MS if i % 2 == 0 else TP
                for t in range(4):
                    ins = nc.tensor.transpose(dst[:, t * P:(t + 1) * P], act1[i % 2][:, t * P:(t + 1) * P], ident[:])
                ins.then_inc(S("segment_turned"), 1)

            def product2(c, j):
                n, last = w2_slab(c, j), FIRST[c]["segs"] - 1
                name, value = copied(c, j)
                pe.wait_ge(S(name), value)
                xh, xl = act1Th[:, j % 2, :], act1Tl[:, j % 2, :]
                if not is_split(c, j):
                    landed(pe, n)
                    for t in range(4):
                        for a, b in halves():
                            ins = mm(AC[:, a:b], act1T[:, j % 2, t * P:(t + 1) * P],
                                     slab_at(n)[:, t * D + a:t * D + b], start=(j == 0 and t == 0),
                                     stop=(j == last and t == 3), skip_group_check=True)
                    ins.then_inc(S("plain_used"), 1)
                    return
                for t in range(4):
                    k = 2 * split_number(n) + t // 2
                    hi, lo = half_split(k)
                    if t % 2 == 0:
                        pe.wait_ge(S("split_lo"), k + 1)
                    for x, w in ((xl, hi), (xh, lo), (xh, hi)):
                        for a, b in halves():
                            ins = mm(AC[:, a:b], x[:, t * P:(t + 1) * P], w[:, t % 2 * D + a:t % 2 * D + b],
                                     start=(j == 0 and t == 0 and x is xl), stop=False, skip_group_check=True)
                    if t % 2:
                        ins.then_inc(S("split_used"), 1)

            def edge_counts():
                pe.wait_ge(S("onehot_ready"), 1)
                for t in range(E_TILES):
                    ins = mm(MS[:, 0:P], onehot[:, 1, t, :], onehot[:, 0, t, :], start=(t == 0),
                             stop=(t == E_TILES - 1))
                ins.then_inc(S("counts_product"), 1)

            def first_wide(c):
                per = FIRST[c]["per"]
                groups = FIRST[c]["segs"] // per
                for g in range(groups + 1):
                    if g < groups:
                        if g >= 2:
                            pe.wait_ge(S("segment_ready"), SEG_BASE[c] + per * (g - 1))
                        project(c, per * g)
                    if 0 < g < groups:
                        term_rows(c, g - 1)
                    if g < groups:
                        for j in range(1, per):
                            project(c, per * g + j)
                            if g == 0 and j == 1:
                                edge_counts()
                    if g:
                        turn_attention(c, g - 1)
                        pe.wait_ge(S("rows_lo"), 1)
                        pe.wait_ge(S("h_copied"), SEG_BASE[c] + min(per * (g + 1), FIRST[c]["segs"]))
                        for i in range(per + 2):
                            j = per * (g - 1) + i
                            if i < per:
                                if i >= 2:
                                    pe.wait_ge(S("segment_ready"), SEG_BASE[c] + j - 1)
                                attend(c, j)
                            if 0 <= i - 1 < per:
                                turn_segment(c, j - 1)
                            if i >= 2:
                                if g == groups - 1 and i == per + 1:
                                    term_rows(c, g)
                                product2(c, j - 2)

            def first_narrow(c):
                n = FIRST[c]["segs"]
                for t in range(n + 4):
                    if t - 3 >= 1:
                        pe.wait_ge(S("segment_ready"), SEG_BASE[c] + min(t - 3, n))
                    if t < n:
                        project(c, t)
                    if 0 <= t - 1 < n:
                        term_rows(c, t - 1)
                        if n == 2:
                            keep_warm(12 if t == 1 else 4)
                    if 0 <= t - 3 < n:
                        turn_segment(c, t - 3)
                        if n == 2:
                            product2(c, t - 3)
                    if 0 <= t - 2 < n:
                        turn_attention(c, t - 2)
                        pe.wait_ge(S("h_copied"), SEG_BASE[c] + min(t + 1, n))
                        attend(c, t - 2)
                    if 0 <= t - 3 < n and n > 2:
                        product2(c, t - 3)

            def attend_l2(g):
                pe.wait_ge(S("attn_ready"), GROUP_BASE[4] + g + 1)
                for h in range(4 * g, 4 * g + 4):
                    ins = mm(AC[:, h * 64:(h + 1) * 64], ALT[:, h * P:(h + 1) * P], hs2[:, h * 64:(h + 1) * 64],
                             start=False, stop=True, skip_group_check=True)
                return ins

            def second(c, n):
                keep_warm(8)
                term_rows(c, 0)
                pe.wait_ge(S("h2_copied"), n)
                for a, b in halves():
                    bias_row(AC[:, a:b], LAYER2_BIAS[c], a, b, start=True)
                keep_warm(10)
                turn_attention(c, 0)
                pe.wait_ge(S("attn_ready"), GROUP_BASE[c] + 1)
                for a, b in halves():
                    ins = mm(AC[:, a:b], attn_tile(c)[:, 0:P], hs2[:, a:b], start=False, stop=True,
                             skip_group_check=True)
                ins.then_inc(S("x_product"), 1)

            def mixture(l):
                m = MOE[l]
                k = {1: 6, 3: 10}[l]
                keep_warm(5)
                pe.wait_ge(S("x_ready"), {1: 3, 3: 7}[l])
                for a, b in halves():
                    ins = mm(AC[:, a:b], ident[:], X[:, a:b], start=True, stop=False, skip_group_check=True)
                ins.then_inc(S("stream_opened"), 1)
                turn(k, XN, warm=7)
                keep_warm(4)
                pe.wait_ge(S("tr_ready"), k + 1)
                at = {1: 0, 3: KT * E8}[l]
                for t in range(KT):
                    ins = mm(MS[:, 0:E8], XT[:, t, :], small[:, at + t * E8:at + (t + 1) * E8], start=(t == 0),
                             stop=(t == KT - 1))
                if l == 1:
                    ins = bias_row(MS[:, 8:16], ROW_MIXED, MIXED_EB, MIXED_EB + E8, start=True, stop=True)
                ins.then_inc(S("router_product"), 1)
                keep_warm(3, bank(1)[:, 0:P])
                pe.wait_ge(S("XTl_ready"), {1: 2, 3: 3}[l])

                def up(kind, q, it):
                    pe.wait_ge(S("lo_" + kind), it * 3 + (q + 1))
                    dst = bank("gu".index(kind))
                    for t in range(KT):
                        w = slice(t * SEG, (t + 1) * SEG)
                        mm(dst, XTl[:, t, :], wh[kind][:, w], start=(t == 0), stop=False)
                        mm(dst, XTh[:, t, :], wl[kind][:, w], start=False, stop=False)
                        ins = mm(dst, XTh[:, t, :], wh[kind][:, w], start=False, stop=(t == KT - 1))
                    ins.then_inc(S("pe_" + kind), 1)

                def turn_hidden(q, it):
                    pe.wait_ge(S("hidden_ready"), it * 3 + q)
                    for t in range(4):
                        ins = nc.tensor.transpose(TP[:, t * P:(t + 1) * P], hexp[:, t * P:(t + 1) * P], ident[:])
                    ins.then_inc(S("pe_t"), 1)

                def down(q, it, tiles=range(4), last=False):
                    d, half = ("g", 1) if last else ("d", 0)
                    xh, xl = act1Th[:, half], act1Tl[:, half]
                    pe.wait_ge(S("lo_d"), it * 3 + q)
                    pe.wait_ge(S("hTl_ready"), it * 3 + q)
                    for t in tiles:
                        for x, w in ((xl, wh[d]), (xh, wl[d]), (xh, wh[d])):
                            for a, b in halves():
                                ins = mm(AC[:, a:b], x[:, t * P:(t + 1) * P], w[:, t * D + a:t * D + b], start=False,
                                         stop=last and t == 3 and x is xh and w is wh[d], skip_group_check=True)
                    if 3 in tiles:
                        ins.then_inc(S("pe_d"), 1)

                def chunk(c0, it=0, first=False, last=False):
                    q = m["first"] + c0
                    if q:
                        pe.wait_ge(S("silu_ready"), it * 3 + q)
                    up("g", q, it)
                    if not first:
                        turn_hidden(q, it)
                    up("u", q, it)
                    if last:
                        down(q, it, tiles=range(2))
                        turn_hidden(q + 1, it)
                        down(q, it, tiles=range(2, 4))
                        down(q + 1, it, last=True)
                    elif not first:
                        down(q, it)

                chunk(0, first=True)
                rounds = (m["chunks"] - 2) // 3
                with pe.Fori(0, rounds) as it:
                    chunk(1, it)
                    chunk(2, it)
                    chunk(3, it)
                for c in range(1 + 3 * rounds, m["chunks"]):
                    chunk(c, last=(c == m["chunks"] - 1))

            pe.wait_ge(S("const_ready"), 1)
            turn(0, XN)
            pe.wait_ge(S("XTl_ready"), 1)
            first_wide(0)
            second(1, 1)
            turn(1, XN, warm=32)
            keep_warm(3)
            pe.wait_ge(S("tr_ready"), 2)
            for w, dst, sem in ((0, PJ, "k_product"), (1, TP, "q_product")):
                for n in range(6 * w // 4, (6 * w + 5) // 4 + 1):
                    landed(pe, FFN0_SLAB + n)
                for t in range(KT):
                    for k in range(KT):
                        ins = mm(dst[:, t * P:(t + 1) * P], w_tile(6 * w + k, t * P, (t + 1) * P), XT[:, k, :],
                                 start=(k == 0), stop=(k == KT - 1))
                ins.then_inc(S(sem), 1)
                if w == 0:
                    pe.wait_ge(S("sigmoid_ready"), 1)
                    mm(MS[:, 0:P], tk[:, 1:2].to_broadcast([P, P]), ident[:], start=True, stop=True)
                    mm(MS[:, P:P + 1], ones[:], tk[:, 1:2], start=True, stop=True).then_inc(S("score_row"), 1)
            pe.wait_ge(S("k_ready"), 1)
            pe.wait_ge(S("pool_weight"), 1)
            for a, b in halves():
                ins = mm(PJ[:, a:b], tk[:, 7:8].to_broadcast([P, P]), XN[:, a:b], start=True, stop=True)
            ins.then_inc(S("pooled"), 1)
            pe.wait_ge(S("q_ready"), 1)
            for t in range(KT):
                ins = mm(TP[:, t * 2 * P:(t + 1) * 2 * P], qT[:, t * P:(t + 1) * P],
                         kz[:, t].rearrange("p a n -> p (a n)"), start=True, stop=True)
            ins.then_inc(S("self_logits"), 1)
            for n in (3, 4):
                landed(pe, FFN0_SLAB + n)
            for a, b in halves():
                bias_row(AC[:, a:b], ROW_BV, a, b, start=True)
                for k in range(KT):
                    ins = mm(AC[:, a:b], XT[:, k, :], w_tile(12 + k, a, b), start=False, stop=(k == KT - 1),
                             skip_group_check=True)
            ins.then_inc(S("v_product"), 1)
            pe.wait_ge(S("self_exps"), 1)
            turn(2, MIX)
            pe.wait_ge(S("tr_ready"), 3)
            landed(pe, FFN0_SLAB + 5)
            for k in range(KT):
                for a, b in halves():
                    mm(PJ[:, a:b], XT[:, k, :], w_tile(18 + k, a, b), start=(k == 0), stop=False,
                       skip_group_check=True)
            pe.wait_ge(S("self_weights"), 1)
            for h in range(HEADS):
                ins = nc.tensor.transpose(TP[:, h * P:(h + 1) * P], EE[:, h * P:(h + 1) * P], ident[:])
            ins.then_inc(S("self_turned"), 1)
            keep_warm(7)
            pe.wait_ge(S("self_attn_ready"), 1)
            pe.wait_ge(S("v_ready"), 1)
            for h in range(HEADS):
                ins = mm(AC[:, h * DH:(h + 1) * DH], ALT[:, h * P:(h + 1) * P], V[:, h * DH:(h + 1) * DH],
                         start=True, stop=True)
            ins.then_inc(S("context"), 1)
            turn(3, CTX, warm=4)
            pe.wait_ge(S("tr_ready"), 4)
            for n in (6, 7):
                landed(pe, FFN0_SLAB + n)
            for k in range(KT):
                for a, b in halves():
                    ins = mm(PJ[:, a:b], XT[:, k, :], w_tile(24 + k, a, b), start=False, stop=(k == KT - 1),
                             skip_group_check=True)
            ins.then_inc(S("merged"), 1)
            for a, b in halves():
                bias_row(AC[:, a:b], ROW_BF2, a, b, start=True)
            turn(4, XN, warm=18)
            pe.wait_ge(S("tr_ready"), 5)
            for k in range(KT):
                ins = mm(MS[0:F0, 0:P], w_tile(30, k * F0, (k + 1) * F0), XT[:, k, :], start=(k == 0),
                         stop=(k == KT - 1))
            ins.then_inc(S("f_product"), 1)
            pe.wait_ge(S("f_ready"), 1)
            for a, b in halves():
                ins = mm(AC[:, a:b], FT[0:F0, :], w_tile(31, a, b)[0:F0], start=False, stop=True,
                         skip_group_check=True)
            ins.then_inc(S("x_product"), 1)
            turn(5, XN, warm=15)
            pe.wait_ge(S("tr_ready"), 6)
            first_narrow(2)
            second(3, 2)
            mixture(1)
            turn(7, XN, warm=15)
            pe.wait_ge(S("tr_ready"), 8)
            at = 2 * KT * E8
            for t in range(KT):
                ins = mm(AC[:, t * P:(t + 1) * P], XT[:, t, :], small[:, at:at + P], start=True, stop=True)
            ins.then_inc(S("l2_h_product"), 1)
            keep_warm(6)
            term_rows(4, 0)
            term_rows(4, 1)
            keep_warm(6)
            term_rows(4, 2)
            pe.wait_ge(S("h2_copied"), 3)
            for t in range(KT):
                mm(AC[:, t * P:(t + 1) * P], XT[:, t, :], small[:, at + P:at + 2 * P], start=(t in (0, 4)),
                   stop=False, skip_group_check=True)
            keep_warm(5)
            for g in range(3):
                turn_attention(4, g)
                if g < 2:
                    keep_warm(3)
                    attend_l2(g)
            attend_l2(2).then_inc(S("x_product"), 1)
            turn(8, XN, warm=15)
            pe.wait_ge(S("tr_ready"), 9)
            n = L2_SLAB
            landed(pe, n)
            bias_row(MS[:, 0:E8], ROW_MIXED, MIXED_BG, MIXED_BG + E8, start=True)
            for k in range(KT):
                ins = mm(MS[:, 0:E8], XT[:, k, :], slab_at(n)[:, L2_W + k * E8:L2_W + (k + 1) * E8], start=False,
                         stop=(k == KT - 1), skip_group_check=True)
            ins.then_inc(S("l2_gate_product"), 1)
            bias_row(PJ[:, 0:E8 * F2], ROW_MIXED, 0, E8 * F2, start=True)
            for k in range(KT):
                ins = mm(PJ[:, 0:E8 * F2], XT[:, k, :], slab_at(n)[:, k * E8 * F2:(k + 1) * E8 * F2], start=False,
                         stop=(k == KT - 1), skip_group_check=True)
            ins.then_inc(S("l2_hidden_product"), 1)
            keep_warm(5, AC[:, 0:P])
            pe.wait_ge(S("l2_weighted"), 1)
            for t in range(3):
                nc.tensor.transpose(TP[:, t * P:(t + 1) * P], G2[:, t * P:(t + 1) * P], ident[:])
            nc.tensor.transpose(TP[0:E8, SEG:SEG + P], comb, ident[:]).then_inc(S("l2_turned"), 1)
            keep_warm(3, AC[:, 0:P])
            n = L2_SLAB + 1
            landed(pe, n)
            pe.wait_ge(S("l2_T_ready"), 2)
            for a, b in halves():
                mm(AC[:, a:b], CBT[0:E8, :], slab_at(n)[0:E8, L2_W + a:L2_W + b], start=True, stop=False,
                   skip_group_check=True)
                for t in range(3):
                    ins = mm(AC[:, a:b], G2T[:, t * P:(t + 1) * P], slab_at(n)[:, t * D + a:t * D + b],
                             start=False, stop=(t == 2), skip_group_check=True)
            ins.then_inc(S("x_product"), 1)
            turn(9, XN, warm=15)
            pe.wait_ge(S("tr_ready"), 10)
            first_narrow(5)
            second(6, 4)
            mixture(3)


def _k_tiles(w):
    k, n = w.shape
    return w.reshape(k // 128, 128, n).transpose(1, 0, 2)


def kernel(**inputs):
    import numpy as np
    import concourse.bacc as bacc
    from concourse.bass_utils import run_bass_kernel_spmd

    i = {k: np.asarray(v) for k, v in inputs.items()}
    f32 = np.float32
    stream = np.zeros((N_SLABS, P, SLAB), f32)

    def by_columns(n, w):
        for j in range(w.shape[1] // SEG):
            stream[n + j] = _k_tiles(w[:, j * SEG:(j + 1) * SEG]).reshape(P, SLAB)

    def by_rows(n, w):
        for j in range(w.shape[0] // SEG):
            stream[n + j] = _k_tiles(w[j * SEG:(j + 1) * SEG]).reshape(P, SLAB)

    def first_layer(c, w1, w2):
        for j in range(FIRST[c]["segs"]):
            by_columns(w1_slab(c, j), w1[:, j * SEG:(j + 1) * SEG])
            by_rows(w2_slab(c, j), w2[j * SEG:(j + 1) * SEG])

    first_layer(0, i["L0_gnn_W1"], i["L0_gnn_W2"])
    first_layer(2, i["L1_gnn_W1"].T, i["L1_gnn_W2"].T)
    first_layer(5, i["L3_gnn_W1"], i["L3_gnn_W2"])
    tiles = np.zeros((P, 32, D), f32)
    for j, name in enumerate(("Wk", "Wq", "Wv", "Wm", "Wo")):
        tiles[:, 6 * j:6 * j + 6] = _k_tiles(i["L0_ffn_" + name])
    tiles[:, 30, 0:KT * F0] = _k_tiles(i["L0_ffn_W1"]).reshape(P, KT * F0)
    tiles[0:F0, 31] = i["L0_ffn_W2"]
    stream[FFN0_SLAB:FFN0_SLAB + 8] = tiles.reshape(P, 8, SLAB).transpose(1, 0, 2)

    def experts(l, e, gate, up, down):
        m = MOE[l]
        for j in range(m["per"]):
            n = m["slab"] + 3 * (e * m["per"] + j)
            f = slice(j * SEG, (j + 1) * SEG)
            by_columns(n, gate[f].T)
            by_columns(n + 1, up[f].T)
            by_rows(n + 2, down[:, f].T)

    for e in range(E8):
        experts(1, e, i["L1_ffn_Wg"][e], i["L1_ffn_Wu"][e], i["L1_ffn_Wd"][e])
        experts(3, e, i["L3_ffn_Wg"][e], i["L3_ffn_Wu"][e], i["L3_ffn_Wd"][e])
    experts(1, E8, i["L1_ffn_sg"], i["L1_ffn_su"], i["L1_ffn_sd"])
    stream[L2_SLAB, :, 0:L2_W] = _k_tiles(i["L2_ffn_W1"].transpose(1, 0, 2).reshape(D, E8 * F2)).reshape(P, L2_W)
    stream[L2_SLAB, :, L2_W:L2_W + KT * E8] = _k_tiles(i["L2_ffn_Wg"]).reshape(P, KT * E8)
    stream[L2_SLAB + 1, :, 0:L2_W] = _k_tiles(i["L2_ffn_W2"].reshape(E8 * F2, D)).reshape(P, L2_W)

    rows = np.zeros((2 * ROWS, D), f32)
    rows[0:12, 0:SEG] = i["L0_gnn_b1"].reshape(12, SEG)
    rows[12:14, 0:SEG] = i["L1_gnn_b1"].reshape(2, SEG)
    rows[14:18, 0:SEG] = i["L3_gnn_b1"].reshape(4, SEG)
    for r, name in ((18, "L0_gnn_b2"), (19, "L1_gnn_b2"), (20, "L3_gnn_b2"), (ROW_BV, "L0_ffn_bv"),
                    (ROW_BF2, "L0_ffn_bf2")):
        rows[r] = i[name]
    rows[ROW_MIXED, 0:E8 * F2] = i["L2_ffn_b1"].reshape(E8 * F2)
    rows[ROW_MIXED, MIXED_BG:MIXED_BG + E8] = i["L2_ffn_bg"]
    rows[ROW_MIXED, MIXED_EB:MIXED_EB + E8] = i["L1_ffn_expert_bias"]
    rows[ROWS:2 * ROWS] = rows[0:ROWS]
    stream[L2_SLAB + 1, 0:E8, L2_W:L2_W + D] = i["L2_ffn_b2"]

    cols = np.zeros((P, 16), f32)
    cols[:, 0:6] = i["L0_ffn_bq"].reshape(KT, P).T
    cols[:, 6:12] = i["L0_ffn_bk"].reshape(KT, P).T
    cols[0:F0, 12] = i["L0_ffn_bf1"]

    small = np.zeros((P, 2 * KT * E8 + 2 * P), f32)
    small[:, 0:48] = _k_tiles(i["L1_ffn_w_router"].T).reshape(P, 48)
    small[:, 48:96] = _k_tiles(i["L3_ffn_router_w"].T).reshape(P, 48)
    for j, name in enumerate(("L2_gnn_W", "L2_gnn_W_res")):
        for a in range(2):
            small[64 * a:64 * a + 64, 96 + P * j + 64 * a:96 + P * j + 64 * a + 64] = i[name].T

    names = (("L0_gnn_a_src1", "L0_gnn_a_dst1", 8), ("L0_gnn_a_src2", "L0_gnn_a_dst2", 1),
             ("L1_gnn_att_src1", "L1_gnn_att_dst1", 2), ("L1_gnn_att_src2", "L1_gnn_att_dst2", 1),
             ("L2_gnn_attn_l", "L2_gnn_attn_r", 1), ("L3_gnn_att_src1", "L3_gnn_att_dst1", 4),
             ("L3_gnn_att_src2", "L3_gnn_att_dst2", 1))
    attn = np.concatenate([i[name].reshape(units, -1)[u] for a, b, units in names for u in range(units)
                           for name in (a, b)])[None, :]
    vectors = np.concatenate([i["L0_ffn_" + n].reshape(-1)
                              for n in ("g1", "b1", "Wr", "g2", "b2", "bo", "bm", "br")])[None, :]
    edges = np.concatenate([i["src"].reshape(P, E_TILES), i["dst"].reshape(P, E_TILES)], axis=1)

    nc = bacc.Bacc("TRN2", target_bir_lowering=False, num_devices=1)
    arrays = {}

    def given(name, a):
        arrays["in_" + name] = np.ascontiguousarray(a)
        return nc.dram_tensor("in_" + name, a.shape, mybir.dt.from_np(a.dtype), kind="ExternalInput").ap()

    out = nc.dram_tensor("out", (P, D), F32, kind="ExternalOutput").ap()
    gnn_ffn_kernel(nc, given("x", i["x"]), given("edges", edges), given("weights", stream), given("rows", rows),
                   given("cols", cols), given("small", small), given("attn", attn),
                   given("ffn0_vectors", vectors), out)
    result = run_bass_kernel_spmd(nc, [arrays], core_ids=[0])
    return result.results[0]["out"]
```
